# Optimizing a Trainium2 kernel written in Bass

```python
import numpy as np
import jax
import jax.numpy as jnp

def _softmax(x, axis=-1):
    return jax.nn.softmax(x, axis=axis)

def _gelu(x):
    return jax.nn.gelu(x, approximate=True)

def _silu(x):
    return jax.nn.silu(x)

def _sigmoid(x):
    return jax.nn.sigmoid(x)

def _layernorm(x, axis=-1, eps=1e-05):
    m = jnp.mean(x, axis=axis, keepdims=True)
    v = jnp.var(x, axis=axis, keepdims=True)
    return (x - m) / jnp.sqrt(v + eps)

def _scatter_add(tgt, idx, src, axis=0):
    return tgt.at[idx].add(src)

def _segment_sum(src, seg, n):
    return jax.ops.segment_sum(src, seg, n)
kernel_name = 'mk_seq_postln_d1_jaxref_r4_90f761'

def setup_inputs(seed: int=0):
    np.random.seed(seed)
    _w = jnp.asarray

    def _L0_attn_setup():
        import jax, jax.numpy as jnp
        import numpy as np
        NUM_HEADS = 16
        ATT_WINDOW = 128
        GLOBAL_SIZE = 64
        key = jax.random.key(seed)
        ks = jax.random.split(key, 10)
        B, S, HID = (1, 512, 256)
        w = lambda k: jax.random.normal(k, (HID, HID), jnp.float32) * 0.02
        b = lambda k: jax.random.normal(k, (HID,), jnp.float32) * 0.02
        return {'x': jax.random.normal(ks[0], (B, S, HID), jnp.float32), 'wq': w(ks[1]), 'bq': b(ks[2]), 'wk': w(ks[3]), 'bk': b(ks[4]), 'wv': w(ks[5]), 'bv': b(ks[6]), 'wo': w(ks[7]), 'bo': b(ks[8])}
    _L0_attn_in = _L0_attn_setup()

    def _L0_ffn_setup():
        import jax, jax.numpy as jnp
        import numpy as np
        B, T, D, E, H = (8, 512, 256, 8, 64)
        LN_EPS = 1e-05
        key = jax.random.key(seed)
        ks = jax.random.split(key, 4)
        return {'x': jax.random.normal(ks[0], (B, T, D), dtype=jnp.float32), 'Wg': jax.random.normal(ks[1], (E, D), dtype=jnp.float32) * 0.02, 'ln_scale': jnp.ones((E, D), dtype=jnp.float32), 'ln_bias': jnp.zeros((E, D), dtype=jnp.float32), 'W1': jax.random.normal(ks[2], (E, D, H), dtype=jnp.float32) * 0.02, 'b1': jnp.zeros((E, H), dtype=jnp.float32), 'W2': jax.random.normal(ks[3], (E, H, D), dtype=jnp.float32) * 0.02, 'b2': jnp.zeros((E, D), dtype=jnp.float32)}
    _L0_ffn_in = _L0_ffn_setup()
    _d = {'L0_attn_x': _L0_attn_in['x'], 'L0_attn_wq': _L0_attn_in['wq'], 'L0_attn_bq': _L0_attn_in['bq'], 'L0_attn_wk': _L0_attn_in['wk'], 'L0_attn_bk': _L0_attn_in['bk'], 'L0_attn_wv': _L0_attn_in['wv'], 'L0_attn_bv': _L0_attn_in['bv'], 'L0_attn_wo': _L0_attn_in['wo'], 'L0_attn_bo': _L0_attn_in['bo'], 'L0_ffn_Wg': _L0_ffn_in['Wg'], 'L0_ffn_ln_scale': _L0_ffn_in['ln_scale'], 'L0_ffn_ln_bias': _L0_ffn_in['ln_bias'], 'L0_ffn_W1': _L0_ffn_in['W1'], 'L0_ffn_b1': _L0_ffn_in['b1'], 'L0_ffn_W2': _L0_ffn_in['W2'], 'L0_ffn_b2': _L0_ffn_in['b2']}
    _x0 = _d['L0_attn_x']
    _d['L0_attn_x'] = jax.random.normal(jax.random.fold_in(jax.random.key(seed), 1), (2, 2048, 256), dtype=_x0.dtype)
    del _x0
    return _d

def reference(L0_attn_x, L0_attn_wq, L0_attn_bq, L0_attn_wk, L0_attn_bk, L0_attn_wv, L0_attn_bv, L0_attn_wo, L0_attn_bo, L0_ffn_Wg, L0_ffn_ln_scale, L0_ffn_ln_bias, L0_ffn_W1, L0_ffn_b1, L0_ffn_W2, L0_ffn_b2):

    def _L0_attn_ref(x, wq, bq, wk, bk, wv, bv, wo, bo):
        import jax, jax.numpy as jnp
        import numpy as np
        NUM_HEADS = 16
        ATT_WINDOW = 128
        GLOBAL_SIZE = 64
        B, S, HID = x.shape
        H = NUM_HEADS
        D = HID // H
        W = ATT_WINDOW
        G = GLOBAL_SIZE
        scale = D ** (-0.5)
        q = (x @ wq.T + bq).reshape(B, S, H, D)
        k = (x @ wk.T + bk).reshape(B, S, H, D)
        v = (x @ wv.T + bv).reshape(B, S, H, D)
        nW = S // W
        qw = q.reshape(B, nW, W, H, D)
        kw = k.reshape(B, nW, W, H, D)
        loc = jnp.einsum('bnihd,bnjhd->bnihj', qw, kw) * scale
        scores = jnp.zeros((B, nW, W, H, nW, W), x.dtype)
        n_idx = jnp.arange(nW)
        scores = scores.at[:, n_idx, :, :, n_idx, :].set(loc.transpose(1, 0, 2, 3, 4))
        scores = scores.reshape(B, S, H, S)
        gi = jnp.arange(0, S, S // G)
        gq = q[:, gi]
        gk = k[:, gi]
        gsc = jnp.einsum('bihd,bjhd->bihj', gq, gk) * scale
        scores = scores.at[:, gi[:, None], :, gi[None, :]].add(gsc.transpose(1, 3, 0, 2))
        attn = jax.nn.softmax(scores, axis=-1)
        out = jnp.einsum('bihj,bjhd->bihd', attn, v).reshape(B, S, HID)
        return out @ wo.T + bo

    def _L0_ffn_ref(x, Wg, ln_scale, ln_bias, W1, b1, W2, b2):
        import jax, jax.numpy as jnp
        import numpy as np
        B, T, D, E, H = (8, 512, 256, 8, 64)
        LN_EPS = 1e-05
        Bs, Ts, Ds = x.shape
        xt = x.reshape(Bs * Ts, Ds)
        logits = xt @ Wg.T
        top1 = jnp.argmax(logits, axis=-1)
        mu = jnp.mean(xt, axis=-1, keepdims=True)
        var = jnp.mean(jnp.square(xt - mu), axis=-1, keepdims=True)
        xhat = (xt - mu) * jax.lax.rsqrt(var + LN_EPS)
        n_experts = Wg.shape[0]

        def body(y, p):
            s_e, b_e, w1, bb1, w2, bb2, eid = p
            h = jax.nn.gelu((xhat * s_e + b_e) @ w1 + bb1, approximate=False)
            out = h @ w2 + bb2
            mask = (top1 == eid)[:, None].astype(out.dtype)
            return (y + mask * out, None)
        y0 = jnp.zeros_like(xt)
        y, _ = jax.lax.scan(body, y0, (ln_scale, ln_bias, W1, b1, W2, b2, jnp.arange(n_experts)))
        return y.reshape(Bs, Ts, Ds)
    x = L0_attn_x
    x = _layernorm(x + _L0_attn_ref(x, L0_attn_wq, L0_attn_bq, L0_attn_wk, L0_attn_bk, L0_attn_wv, L0_attn_bv, L0_attn_wo, L0_attn_bo), axis=-1)
    x = _layernorm(x + _L0_ffn_ref(x, L0_ffn_Wg, L0_ffn_ln_scale, L0_ffn_ln_bias, L0_ffn_W1, L0_ffn_b1, L0_ffn_W2, L0_ffn_b2), axis=-1)
    return x

_drawn_inputs = setup_inputs


def setup_inputs(seed=0):
    import zlib

    import numpy as np

    out = dict(_drawn_inputs(seed))
    spreads = {'L0_ffn_ln_scale': (1.0, 0.6),
     'L0_ffn_ln_bias': (0.0, 2.0),
     'L0_ffn_b1': (0.0, 0.8),
     'L0_ffn_b2': (0.0, 0.1)}
    factors = {'L0_attn_wq': 8.0,
     'L0_attn_bq': 8.0,
     'L0_attn_wk': 8.0,
     'L0_attn_bk': 40.745,
     'L0_attn_wv': 8.0,
     'L0_attn_bv': 4.929,
     'L0_attn_wo': 5.678,
     'L0_attn_bo': 5.328}
    for name, (base, spread) in spreads.items():
        noise = np.random.default_rng([zlib.crc32(name.encode()), seed]).standard_normal(out[name].shape)
        drawn = base * np.exp(spread * noise) if base else spread * noise
        out[name] = jnp.asarray(drawn.astype(out[name].dtype))
    for name, factor in factors.items():
        out[name] = (out[name] * factor).astype(out[name].dtype)
    return out
```

```python
import concourse.bass as bass
from concourse import mybir
from contextlib import ExitStack


def windowed_attention_then_top1_experts(
    nc: bass.Bass,
    x_dram: bass.AP,
    wq_dram: bass.AP,
    bq_dram: bass.AP,
    wk_dram: bass.AP,
    bk_dram: bass.AP,
    wv_dram: bass.AP,
    bv_dram: bass.AP,
    wo_dram: bass.AP,
    bo_dram: bass.AP,
    wg_dram: bass.AP,
    ln_scale_dram: bass.AP,
    ln_bias_dram: bass.AP,
    w1_dram: bass.AP,
    b1_dram: bass.AP,
    w2_dram: bass.AP,
    b2_dram: bass.AP,
    out_dram: bass.AP,
):
    fp32 = mybir.dt.float32
    bf16 = mybir.dt.bfloat16
    i32 = mybir.dt.int32
    ALU = mybir.AluOpType
    ACT = mybir.ActivationFunctionType
    AX = mybir.AxisListType

    P = 128
    B, S, HID = x_dram.shape
    HEADS = 16
    DH = HID // HEADS
    WINDOW = 128
    GLOBALS = 64
    STRIDE = S // GLOBALS
    GPW = WINDOW // STRIDE
    NW = B * S // WINDOW
    WPB = S // WINDOW
    KC = HID // P
    UNITS = 4
    HPU = HEADS // UNITS
    VA = DH + 1
    NV = HEADS * VA
    EXW = NV + HEADS
    SCALE = float(DH) ** -0.5
    CUT = -1.0e30
    EXPERTS, _, EH = w1_dram.shape
    FC = EXPERTS * EH // P
    EPC = P // EH
    EPS = 1e-5
    TG = 4
    NG = NW // TG
    NVEC = 3 * EXPERTS + 3
    GT = TG * P
    RSQRT_SEED = float(0x5F3759DF)
    NEWTON = 3
    NEWTON_STEPS = 2 + 4 * NEWTON

    ctx = ExitStack()
    with ctx:
        def sb(name, shape, dt=fp32):
            return ctx.enter_context(nc.sbuf_tensor(name, shape, dt))

        def sem(name):
            return ctx.enter_context(nc.semaphore(name))

        rows = sb("rows", [P, NW * HID])
        xg = sb("xg", [P, HID])
        w_raw = sb("w_raw", [P, 4, KC, HID])
        wT = sb("wT", [P, 4, KC, HID])
        bv_wide = sb("bv_wide", [P, KC, P])
        bo_wide = sb("bo_wide", [P, HID])
        out_bias = sb("out_bias", [P, HID])
        ident = sb("ident", [P, P])
        ident_b = sb("ident_b", [P, P], bf16)
        pid = sb("pid", [P, 1], i32)
        cid = sb("cid", [P, P], i32)
        pbits = sb("pbits", [P, 4], i32)
        pvals = sb("pvals", [P, 4])
        cbits = sb("cbits", [P, 2, P], i32)
        cvals = sb("cvals", [P, 2, P])
        is_glob = sb("is_glob", [P, 1])
        q_scale = sb("q_scale", [P, 2, P])
        zero_w = sb("zero_w", [P, P])
        neg_zero_w = sb("neg_zero_w", [P, P])
        cut_cols = sb("cut_cols", [P, HPU, GPW])
        zeros16 = sb("zeros16", [P, HEADS])
        g_factor = sb("g_factor", [P, P])
        g_cut = sb("g_cut", [P, P])
        xgT = sb("xgT", [P, KC, P])
        qg = sb("qg", [P, KC, 2, P])
        kg = sb("kg", [P, KC, P])
        vg = sb("vg", [P, NV])
        dg = sb("dg", [P, UNITS, HPU * P])
        pg = sb("pg", [P, UNITS, HPU * P])
        mg_raw = sb("mg_raw", [P, HEADS])
        g_row = sb("g_row", [P, EXW])
        table = sb("table", [P, NW * EXW])
        xsum = sb("xsum", [P, B, WPB // 2 * HID])
        xsumT = sb("xsumT", [P, B, KC, P])
        v_all = sb("v_all", [P, B * NV])

        xs = sb("xs", [P, 2, HID])
        xT = sb("xT", [P, 2, KC, P])
        qm = sb("qm", [P, 2, KC, 2, P])
        kT = sb("kT", [P, 2, KC, P])
        va = sb("va", [P, 2, NV])
        row_max = sb("row_max_t", [P, 2, HEADS])
        guard = sb("guard_t", [P, 2, HEADS])
        shifted = sb("shifted_t", [P, UNITS, HPU * P])
        probs = sb("probs_t", [P, UNITS, HPU * P])
        e_arg = sb("e_arg_t", [P, 2, 2 * HEADS])
        e_val = sb("e_val_t", [P, 2, 2 * HEADS])
        rest = sb("rest_t", [P, 2, NV])
        gl = sb("gl_t", [P, NV])
        num = sb("num_t", [P, 2, NV])
        rden = sb("rden_t", [P, 2, HEADS])
        attn = sb("attn_t", [P, 2, HID])
        aT = sb("aT_t", [P, 2, KC, P])
        biased = sb("biased_t", [P, 2, HID])
        residual = sb("residual_t", [P, 2, HID])
        bn6 = sb("bn6", [P, TG, 6])
        mean_var = sb("mean_var", [P, 2, 2])
        stats = sb("stats_t", [P, NW * 2])

        rs1 = sb("rs1", [P, NW])
        var1 = sb("var1", [P, NW])
        rs2 = sb("rs2", [P, NW])
        nt = sb("newton_t", [P, NW])
        ny = sb("newton_y", [P, NW])
        nx = sb("newton_x", [P, NW])

        vec_rows = sb("vec_rows", [NVEC, HID])
        vecT = sb("vecT", [P, KC, NVEC])
        bq_col, bk_col, bv_col = (vecT[:, :, 3 * EXPERTS + i] for i in range(3))
        b1_rows = sb("b1_rows", [FC, P])
        w1 = sb("w1", [P, KC, EXPERTS, EH])
        w1s = sb("w1s", [P, KC, EXPERTS * EH])
        w2 = sb("w2", [P, FC, HID])
        b1 = sb("b1", [P, FC])
        b1s = sb("b1s", [P, FC])
        b2_f = sb("b2_f", [3 * EXPERTS, HID])
        b2_h = sb("b2_h", [3 * EXPERTS, 3, HID], bf16)
        b2_sel = sb("b2_sel", [P, 3])
        b2_t = sb("b2_t", [3 * EXPERTS, 3, HID])
        b2_stack = sb("b2_stack", [3 * EXPERTS, HID], bf16)
        pick = sb("pick", [3 * EXPERTS, FC, P], bf16)
        rank = sb("rank", [P, EXPERTS])
        rank_i = sb("rank_i", [P, EXPERTS], i32)
        xh = sb("xh", [P, TG, HID])
        xhT = xsum[:, 0, :].rearrange("p (b c n) -> p b c n", b=2, c=KC)
        zmax = sb("zmax", [P, 2, TG])
        hit = sb("hit", [P, TG, EXPERTS])
        onehot = sb("onehot", [P, TG, 3, EXPERTS], bf16)
        ohT = sb("ohT", [3 * EXPERTS, 2, GT], bf16)
        hT = xsum[:, 1, :].rearrange("p (f n) -> p f n", f=FC)
        hm = table[:, 0:4096].rearrange("p (b f n) -> p b f n", b=2, f=FC)
        ysum = table[:, 4096:6144].rearrange("p (b t n) -> p b t n", b=2, t=TG)
        ystat = sb("ystat", [P, 2, TG, 2])
        yrs = sb("yrs", [P, 3, TG])
        yout = table[:, 6144:8192].rearrange("p (b t n) -> p b t n", b=2, t=TG)

        scratch = nc.dram_tensor("global_sums", (P, EXW), fp32, kind="Internal").ap()

        ps = ctx.enter_context(nc.psum_tensor("ps", [P, 8, 512], fp32))
        ps_score = [ps[:, 0, :], ps[:, 1, :]]
        ps_dT = [ps[:, 2, :], ps[:, 3, :]]
        ps_xq = ps[:, 4, :]
        ps_kv = ps[:, 5, :]
        ps_rao = ps[:, 6, :]
        ps_pv = ps[:, 7, 0:NV]

        def quad(u):
            return slice(32 * u, 32 * u + 32)

        def by_head(ap):
            return ap.rearrange("p (c u a) -> p u c a", c=KC, u=UNITS)

        def heads_of(u):
            return [(c, a, 8 * c + 2 * u + a) for c in range(KC) for a in range(2)]

        def keys(ap):
            return ap.rearrange("p (c a j) -> p c a j", c=KC, a=2)

        def wide(ap):
            return ap.rearrange("p (h e) -> p h e", e=VA)

        def row(ap, w, width):
            return ap[:, bass.ds(w * width, width)]

        def need(eng, s, count):
            if not isinstance(count, int) or count > 0:
                eng.wait_ge(s, count)

        ld_xg, ld_w, ld_bo, ld_gate, ld_w1, ld_w2, ld_b = (
            sem(n) for n in ("ld_xg", "ld_w", "ld_bo", "ld_gate", "ld_w1", "ld_w2", "ld_b"))
        ld_x = [sem(f"ld_x{i}") for i in range(8)]
        pool_const = sem("pool_const")
        dve_const = sem("dve_const")
        table_zero = sem("table_zero")
        wT_in_psum = sem("wT_in_psum")
        wT_ready = sem("wT_ready")
        vecT_in_psum = sem("vecT_in_psum")
        vecT_ready = sem("vecT_ready")
        xgT_in_psum = sem("xgT_in_psum")
        xgT_ready = sem("xgT_ready")
        qg_in_psum = sem("qg_in_psum")
        qg_ready = sem("qg_ready")
        kvg_in_psum = sem("kvg_in_psum")
        kvg_ready = sem("kvg_ready")
        bias_in_psum = sem("bias_in_psum")
        bias_ready = sem("bias_ready")
        b1_in_psum = sem("b1_in_psum")
        gs_in_psum = sem("gs_in_psum")
        gs_scaled = sem("gs_scaled")
        gs_cut = sem("gs_cut")
        gs_max = sem("gs_max")
        gs_shifted = sem("gs_shifted")
        gT_in_psum = sem("gT_in_psum")
        g_probs = sem("g_probs")
        g_pv = sem("g_pv")
        g_rows_ready = sem("g_rows_ready")
        g_stored = sem("g_stored")
        table_ready = sem("table_ready")
        xsum_ready = sem("xsum_ready")
        pool_step = sem("pool_step")
        xsumT_in_psum = sem("xsumT_in_psum")
        xsumT_ready = sem("xsumT_ready")
        vall_in_psum = sem("vall_in_psum")
        vall_ready = sem("vall_ready")
        ffn_w_ready = sem("ffn_w_ready")
        xs_ready = sem("xs_ready")
        xT_in_psum = sem("xT_in_psum")
        xT_ready = sem("xT_ready")
        q_in_psum = sem("q_in_psum")
        q_ready = sem("q_ready")
        kv_in_psum = sem("kv_in_psum")
        k_ready = sem("k_ready")
        v_ready = sem("v_ready")
        scores_in_psum = sem("scores_in_psum")
        max_ready = sem("max_ready")
        guard_ready = sem("guard_ready")
        shifted_ready = sem("shifted_ready")
        cut_ready = sem("cut_ready")
        dT_in_psum = sem("dT_in_psum")
        probs_ready = sem("probs_ready")
        pv_in_psum = sem("pv_in_psum")
        r_in_psum = sem("r_in_psum")
        rest_ready = sem("rest_ready")
        e_arg_ready = sem("e_arg_ready")
        e_ready = sem("e_ready")
        rest_step = sem("rest_step")
        num_ready = sem("num_ready")
        rden_ready = sem("rden_ready")
        attn_ready = sem("attn_ready")
        aT_in_psum = sem("aT_in_psum")
        aT_ready = sem("aT_ready")
        o_in_psum = sem("o_in_psum")
        biased_ready = sem("biased_ready")
        residual_ready = sem("residual_ready")
        bn_ready = sem("bn_ready")
        stats_ready = sem("stats_ready")
        kept = sem("kept")
        ln_step = sem("ln_step")
        xh_ready = sem("xh_ready")
        x1_ready = sem("x1_ready")
        xhT_in_psum = sem("xhT_in_psum")
        xhT_ready = sem("xhT_ready")
        z_in_psum = sem("z_in_psum")
        route_step = sem("route_step")
        onehot_ready = sem("onehot_ready")
        ohT_in_psum = sem("ohT_in_psum")
        ohT_ready = sem("ohT_ready")
        h_in_psum = sem("h_in_psum")
        mask_in_psum = sem("mask_in_psum")
        h_ready = sem("h_ready")
        hm_ready = sem("hm_ready")
        y_in_psum = sem("y_in_psum")
        ysum_ready = sem("ysum_ready")
        ybn_ready = sem("ybn_ready")
        ystat_ready = sem("ystat_ready")
        y_newton = sem("y_newton")
        yout_ready = sem("yout_ready")
        stored = [sem("stored0"), sem("stored1")]

        WQ, WK, WV, WO = range(4)
        block = ctx.enter_context(nc.Block())

        LOOP_A = (3, NW - 1)

        def attention_steps(eng, step):
            for t in range(-1, LOOP_A[0]):
                step(t, t % 2)
            with eng.Fori(LOOP_A[0], LOOP_A[1] - 1, 2) as t:
                for k in range(2):
                    step(t + k, (LOOP_A[0] + k) % 2, steady=True)
            for t in range(LOOP_A[1], NW + 2):
                step(t, t % 2)

        def live(w, steady):
            return steady or 0 <= w < NW

        LOOP_B = (2, NG - 2)

        def expert_steps(eng, step):
            for n in range(-1, LOOP_B[0]):
                step(n, n % 2)
            with eng.Fori(LOOP_B[0], LOOP_B[1] - 1, 2) as n:
                for k in range(2):
                    step(n + k, (LOOP_B[0] + k) % 2, steady=True)
            for n in range(LOOP_B[1], NG + 1):
                step(n, n % 2)

        def live_group(n, steady):
            return steady or 0 <= n < NG

        @block.sync
        def _(sp):
            sp.dma_start(xg[:], x_dram.rearrange("b (g s) d -> (b g) s d", s=STRIDE)[:, 0, :]).then_inc(ld_xg, 16)
            for i, w in enumerate((wq_dram, wk_dram, wv_dram, wo_dram)):
                sp.dma_start(w_raw[:, i, :, :], w.rearrange("(c p) n -> p c n", p=P)).then_inc(ld_w, 16)
            x_t = x_dram.rearrange("b (w p) d -> p (b w) d", p=P)
            rows_v = rows[:].rearrange("p (w d) -> p w d", d=HID)
            for i in range(8):
                k = NW // 8
                sp.dma_start(rows_v[:, i * k:(i + 1) * k, :], x_t[:, i * k:(i + 1) * k, :]).then_inc(ld_x[i], 16)
            for c in range(KC):
                sp.dma_start(w1[:, c, :, :], w1_dram[:, c * P:(c + 1) * P, :].rearrange("e p h -> p e h")).then_inc(ld_w1, 16)
            sp.dma_start(w2[:], w2_dram.rearrange("(c e) h d -> (e h) c d", e=EPC)).then_inc(ld_w2, 16)
            sp.wait_ge(g_rows_ready, 2)
            sp.dma_start(scratch, g_row[:]).then_inc(g_stored, 16)
            sp.wait_ge(g_stored, 16)
            sp.wait_ge(table_zero, 1)
            sp.dma_start(table[0:P:STRIDE, :].rearrange("a (w c) -> a w c", c=EXW),
                         scratch.rearrange("(w a) c -> a w c", a=GPW)).then_inc(table_ready, 16)

            def step(n, p, steady=False):
                if live_group(n - 1, steady):
                    sp.wait_ge(yout_ready, n)
                    out_t = out_dram.rearrange("b (w p) d -> p (b w) d", p=P)
                    sp.dma_start(out_t[:, bass.ds((n - 1) * TG, TG), :], yout[:, 1 - p, :, :]).then_inc(stored[1 - p], 16)
            expert_steps(sp, step)
            for p in range(2):
                sp.wait_ge(stored[p], 16 * (NG // 2))

        @block.gpsimd
        def _(pool):
            pool.memset(ident[:], 0.0).then_inc(pool_const, 1)
            pool.memset(ident_b[:], 0.0).then_inc(pool_const, 1)
            pool.memset(pick[:], 0.0).then_inc(pool_const, 1)
            pool.wait_ge(pool_const, 3)
            for m in (ident, ident_b):
                pool.affine_select(out=m[:], in_=m[:], compare_op=ALU.not_equal, fill=1.0, base=0,
                                   pattern=[[-1, P]], channel_multiplier=1).then_inc(pool_const, 1)
            pool.iota(pid[:], pattern=[[0, 1]], base=0, channel_multiplier=1).then_inc(pool_const, 1)
            pool.iota(cid[:], pattern=[[1, P]], base=0, channel_multiplier=0).then_inc(pool_const, 1)
            pool.affine_select(out=pick[:].rearrange("r c (k h) -> r c k h", k=EPC), in_=pick[:].rearrange("r c (k h) -> r c k h", k=EPC),
                               compare_op=ALU.not_equal, fill=1.0, base=0,
                               pattern=[[-EPC, FC], [-1, EPC], [0, EH]], channel_multiplier=1).then_inc(pool_const, 1)
            pool.iota(rank_i[:], pattern=[[-1, EXPERTS]], base=EXPERTS, channel_multiplier=0).then_inc(pool_const, 1)
            pool.memset(va[:], 1.0).then_inc(pool_const, 1)
            pool.memset(vg[:], 1.0).then_inc(pool_const, 1)
            pool.memset(zeros16[:], 0.0).then_inc(pool_const, 1)
            pool.memset(table[:], 0.0).then_inc(table_zero, 1)
            for b in range(B):
                for i in range(4):
                    pool.wait_ge(ld_x[4 * b + i], 16)
                n = WPB // 2 * HID
                base = b * WPB * HID
                pool.tensor_tensor(xsum[:, b, 0:n], rows[:, base:base + n], rows[:, base + n:base + 2 * n],
                                   ALU.add).then_inc(pool_step, 1)
                k = 1
                while n > HID:
                    n //= 2
                    pool.wait_ge(pool_step, 4 * b + k)
                    done = pool.tensor_tensor(xsum[:, b, 0:n], xsum[:, b, 0:n], xsum[:, b, n:2 * n], ALU.add)
                    done.then_inc(pool_step, 1)
                    k += 1
            pool.wait_ge(table_ready, 16)

            def step(t, p, steady=False):
                nxt, cur, prev, pp = (live(t + k, steady) for k in (1, 0, -1, -2))

                def cut(u):
                    pool.wait_ge(shifted_ready, 4 * t + u + 1)
                    part = shifted[:, u, :].rearrange("p (h j) -> p h j", j=P)[:, :, 0:P:STRIDE]
                    pool.tensor_tensor(part, part, cut_cols[:], ALU.add).then_inc(cut_ready, 1)

                if nxt:
                    need(pool, xT_in_psum, t)
                    pool.tensor_copy(xs[:, 1 - p, :], row(rows, t + 1, HID)).then_inc(xs_ready, 1)
                if cur:
                    cut(0)
                if prev:
                    pool.wait_ge(rest_ready, t)
                    pool.wait_ge(e_ready, t)
                    e = e_val[:, 1 - p, :]
                    r = wide(rest[:, 1 - p, :])
                    pool.tensor_tensor(r, r, e[:, 0:HEADS].unsqueeze(2).broadcast_to([P, HEADS, VA]),
                                       ALU.mult).then_inc(rest_step, 1)
                    pool.tensor_tensor(wide(gl[:]), wide(table[:, bass.ds((t - 1) * EXW, NV)]),
                                       e[:, HEADS:2 * HEADS].unsqueeze(2).broadcast_to([P, HEADS, VA]),
                                       ALU.mult).then_inc(rest_step, 1)
                    pool.wait_ge(rest_step, 3 * t - 1)
                    pool.tensor_tensor(rest[:, 1 - p, :], rest[:, 1 - p, :], gl[:], ALU.add).then_inc(rest_step, 1)
                if cur:
                    cut(1)
                if cur:
                    cut(2)
                if pp:
                    need(pool, residual_ready, t - 3)
                    pool.tensor_tensor(biased[:, p, :], row(rows, t - 2, HID), out_bias[:], ALU.add).then_inc(biased_ready, 1)
                if cur:
                    cut(3)
                    need(pool, e_ready, t - 1)
                    pool.wait_ge(guard_ready, 4 * t + 4)
                    pool.tensor_tensor(e_arg[:, p, 0:HEADS], zeros16[:], guard[:, p, :], ALU.subtract)
                    pool.tensor_tensor(e_arg[:, p, HEADS:2 * HEADS], table[:, bass.ds(t * EXW + NV, HEADS)],
                                       guard[:, p, :], ALU.subtract).then_inc(e_arg_ready, 1)
                if live(t - 3, steady):
                    pool.wait_ge(stats_ready, t - 2)
                if prev:
                    need(pool, aT_in_psum, t - 2)
                    pool.wait_ge(rden_ready, t)
                    pool.tensor_tensor(attn[:, 1 - p, :].rearrange("p (h e) -> p h e", e=DH),
                                       wide(num[:, 1 - p, :])[:, :, 0:DH],
                                       rden[:, 1 - p, :].unsqueeze(2).broadcast_to([P, HEADS, DH]),
                                       ALU.mult).then_inc(attn_ready, 1)
                if live(t - 3, steady):
                    keep(t - 3, 1 - p)

            def keep(w, pw):
                pool.tensor_copy(row(rows, w, HID), residual[:, pw, :])
                pool.tensor_copy(row(stats, w, 2), mean_var[:, pw, :]).then_inc(kept, 1)

            attention_steps(pool, step)
            pool.wait_ge(stats_ready, NW)
            keep(NW - 1, (NW - 1) % 2)

        @block.scalar
        def _(act):
            act.dma_start(bo_wide[:], bo_dram.rearrange("(a n) -> a n", a=1).broadcast_to([P, HID])).then_inc(ld_bo, 16)
            for i, src in enumerate((wg_dram, ln_scale_dram, ln_bias_dram)):
                act.dma_start(vec_rows[EXPERTS * i:EXPERTS * (i + 1), :], src).then_inc(ld_gate, 16)
            for i, src in enumerate((bq_dram, bk_dram, bv_dram)):
                act.dma_start(vec_rows[3 * EXPERTS + i:3 * EXPERTS + i + 1, :],
                              src.rearrange("(a n) -> a n", a=1)).then_inc(ld_gate, 16)
            act.dma_start(b1_rows[:], b1_dram.rearrange("(c e) h -> c (e h)", e=EPC)).then_inc(ld_gate, 16)
            for i in range(3):
                act.dma_start(b2_f[EXPERTS * i:EXPERTS * (i + 1), :], b2_dram).then_inc(ld_b, 16)

            def copy(dst, src):
                return act.activation(dst, src, ACT.Copy)

            act.wait_ge(xgT_in_psum, 1)
            copy(xgT[:].rearrange("p c n -> p (c n)"), ps[:, 5, 0:HID]).then_inc(xgT_ready, 1)
            act.wait_ge(vecT_in_psum, 1)
            copy(b1[:], ps[:, 4, KC * NVEC:KC * NVEC + FC])
            copy(vecT[:].rearrange("p c n -> p (c n)"), ps[:, 4, 0:KC * NVEC]).then_inc(vecT_ready, 1)
            for i in (WV, WO):
                act.wait_ge(wT_in_psum, i + 1)
                copy(wT[:, i, :, :].rearrange("p c n -> p (c n)"), ps[:, i, :]).then_inc(wT_ready, 1)
            act.wait_ge(kvg_in_psum, 1)
            act.wait_ge(pool_const, 12)
            for c in range(KC):
                last = act.activation(kg[:, c, :], ps[:, 7, c * P:(c + 1) * P], ACT.Identity, bias=bk_col[:, c:c + 1])
            last.then_inc(kvg_ready, 1)
            copy(wide(vg[:])[:, :, 0:DH], ps[:, 7, HID:2 * HID].rearrange("p (h e) -> p h e", e=DH)).then_inc(kvg_ready, 1)
            for u in range(UNITS):
                act.wait_ge(gT_in_psum, u + 1)
                act.activation(pg[:, u, :], ps[:, u, :], ACT.Exp).then_inc(g_probs, 1)
            act.wait_ge(g_pv, 1)
            copy(g_row[:, 0:NV], ps[:, 5, 0:NV]).then_inc(g_rows_ready, 1)
            for b in range(B):
                act.wait_ge(xsumT_in_psum, b + 1)
                copy(xsumT[:, b, :, :].rearrange("p c n -> p (c n)"), ps[:, 2 + b, 0:HID]).then_inc(xsumT_ready, 1)

            def step(t, p, steady=False):
                nxt, cur, prev, pp = (live(t + k, steady) for k in (1, 0, -1, -2))

                def exp(w, u):
                    g = 4 * w + u
                    need(act, pv_in_psum, g - 3)
                    act.wait_ge(dT_in_psum, g + 1)
                    act.activation(probs[:, u, :], ps_dT[u % 2], ACT.Exp).then_inc(probs_ready, 1)

                if prev:
                    exp(t - 1, 2)
                    need(act, rest_step, 3 * (t - 2))
                    act.wait_ge(e_arg_ready, t)
                    act.activation(e_val[:, 1 - p, :], e_arg[:, 1 - p, :], ACT.Exp).then_inc(e_ready, 1)
                if pp:
                    need(act, o_in_psum, t - 3)
                    act.wait_ge(aT_in_psum, t - 1)
                    copy(aT[:, p, :, :].rearrange("p c n -> p (c n)"), ps_rao[:, 0:HID]).then_inc(aT_ready, 1)
                if nxt:
                    need(act, kv_in_psum, t)
                    act.wait_ge(xT_in_psum, t + 2)
                    copy(xT[:, 1 - p, :, :].rearrange("p c n -> p (c n)"), ps_xq[:, 0:HID]).then_inc(xT_ready, 1)
                if prev:
                    exp(t - 1, 3)
                if nxt:
                    need(act, scores_in_psum, 4 * t)
                    act.wait_ge(kv_in_psum, t + 2)
                    for c in range(KC):
                        last = act.activation(kT[:, 1 - p, c, :], ps_kv[:, c * P:(c + 1) * P], ACT.Identity,
                                              bias=bk_col[:, c:c + 1])
                    last.then_inc(k_ready, 1)
                if cur:
                    exp(t, 0)
                if nxt:
                    need(act, pv_in_psum, 4 * t)
                    copy(wide(va[:, 1 - p, :])[:, :, 0:DH],
                         ps_kv[:, HID:2 * HID].rearrange("p (h e) -> p h e", e=DH)).then_inc(v_ready, 1)
                if cur:
                    exp(t, 1)

            attention_steps(act, step)

            def step(n, p, steady=False):
                nxt, cur, prev = (live_group(n + k, steady) for k in (1, 0, -1))

                def evacuate(pair):
                    act.wait_ge(xhT_in_psum, 2 * (n + 1) + pair + 1)
                    need(act, h_in_psum, 4 * n)
                    act.activation(xhT[:, 1 - p, :, pair * 2 * P:(pair + 1) * 2 * P].rearrange("p c (t n) -> p t c n", t=2),
                                   ps[:, 6, :].rearrange("p (t c n) -> p t c n", t=2, c=KC), ACT.Copy).then_inc(xhT_ready, 1)

                for c in range(FC):
                    if nxt and c >= 2:
                        evacuate(c - 2)
                    if cur:
                        need(act, hm_ready, 4 * n + c - 3)
                        act.wait_ge(h_in_psum, 4 * n + c + 1)
                        act.activation(hT[:, c, :], ps[:, c % 2, :], ACT.Gelu, bias=b1s[:, c:c + 1]).then_inc(h_ready, 1)
                if nxt:
                    act.wait_ge(ohT_in_psum, n + 2)
                    act.activation(ohT[:, 1 - p, :], ps[0:3 * EXPERTS, 7, 64:64 + GT // 2].bitcast(bf16), ACT.Copy).then_inc(ohT_ready, 1)

            act.wait_ge(ffn_w_ready, 1)
            expert_steps(act, step)

        @block.vector
        def _(dve):
            count = [0]

            def link(ins):
                count[0] += 1
                ins.then_inc(dve_const, 1)
                dve.wait_ge(dve_const, count[0])

            dve.wait_ge(pool_const, 12)
            dve.tensor_scalar(pbits[:, 0:1], pid[:], DH, None, ALU.bitwise_and)
            dve.tensor_scalar(pbits[:, 1:2], pid[:], 2, None, ALU.logical_shift_right)
            dve.tensor_scalar(pbits[:, 2:3], pid[:], 6, None, ALU.logical_shift_right)
            link(dve.tensor_scalar(pbits[:, 3:4], pid[:], STRIDE - 1, None, ALU.bitwise_and))
            dve.tensor_scalar(cbits[:, 0, :], cid[:], 2, None, ALU.logical_shift_right)
            link(dve.tensor_scalar(cbits[:, 1, :], cid[:], 6, None, ALU.logical_shift_right))
            dve.tensor_copy(pvals[:], pbits[:])
            link(dve.tensor_copy(cvals[:], cbits[:]))
            dve.tensor_scalar(q_scale[:, 0, :], pvals[:, 0:1].broadcast_to([P, P]), 0.0, SCALE, ALU.is_equal, ALU.mult)
            link(dve.tensor_scalar(q_scale[:, 1, :], pvals[:, 0:1].broadcast_to([P, P]), float(DH), SCALE, ALU.is_equal, ALU.mult))
            for i in (WQ, WK):
                dve.wait_ge(wT_in_psum, i + 1)
                dve.tensor_copy(wT[:, i, :, :].rearrange("p c n -> p (c n)"), ps[:, i, :]).then_inc(wT_ready, 1)
            dve.tensor_scalar(g_factor[:], cvals[:, 0, :], pvals[:, 1:2], 1.0, ALU.is_equal, ALU.add)
            link(dve.tensor_scalar(g_cut[:], cvals[:, 1, :], pvals[:, 2:3], 1.0, ALU.is_equal, ALU.subtract))
            link(dve.tensor_scalar(g_cut[:], g_cut[:], -CUT, None, ALU.mult))
            dve.wait_ge(vecT_ready, 1)
            dve.wait_ge(qg_in_psum, 1)
            for c in range(KC):
                last = dve.scalar_tensor_tensor(qg[:, c, :, :], ps[:, 6, c * P:(c + 1) * P].unsqueeze(1).broadcast_to([P, 2, P]),
                                                bq_col[:, c:c + 1], q_scale[:], ALU.add, ALU.mult)
            last.then_inc(qg_ready, 1)
            link(dve.tensor_scalar(is_glob[:], pvals[:, 3:4], 0.0, None, ALU.is_equal))
            link(dve.memset(zero_w[:], 1.0))
            link(dve.scalar_tensor_tensor(zero_w[:, 0:P:STRIDE], zero_w[:, 0:P:STRIDE], is_glob[:],
                                          zero_w[:, 0:P:STRIDE], ALU.subtract, ALU.mult))
            link(dve.tensor_scalar(neg_zero_w[:], zero_w[:], -1.0, None, ALU.mult))
            link(dve.tensor_scalar(cut_cols[:].rearrange("p h g -> p (h g)"), is_glob[:].broadcast_to([P, HPU * GPW]), CUT, None, ALU.mult))
            dve.tensor_copy(bv_wide[:], bv_col.unsqueeze(2).broadcast_to([P, KC, P]))
            for b in range(B):
                last = dve.tensor_scalar(wide(v_all[:, b * NV:(b + 1) * NV])[:, :, DH], is_glob[:].broadcast_to([P, HEADS]),
                                         float(-GLOBALS), float(S), ALU.mult, ALU.add)
            link(last)
            link(dve.tensor_copy(rank[:], rank_i[:]))
            consts_done = count[0]

            for u in range(UNITS):
                dve.wait_ge(gs_in_psum, u + 1)
                dve.tensor_tensor(keys(dg[:, u, :]), keys(ps[:, u, :]),
                                  g_factor[:].unsqueeze(1).unsqueeze(1).broadcast_to([P, KC, 2, P]), ALU.mult).then_inc(gs_scaled, 1)
                dve.wait_ge(gs_scaled, u + 1)
                dve.tensor_tensor(keys(dg[:, u, :]), keys(dg[:, u, :]),
                                  g_cut[:].unsqueeze(1).unsqueeze(1).broadcast_to([P, KC, 2, P]), ALU.add).then_inc(gs_cut, 1)
                dve.wait_ge(gs_cut, u + 1)
                dve.tensor_reduce(by_head(mg_raw[:])[:, u], keys(dg[:, u, :]), op=ALU.max, axis=AX.X).then_inc(gs_max, 1)
                dve.wait_ge(gs_max, 2 * u + 1)
                dve.tensor_scalar(by_head(g_row[:, NV:EXW])[:, u], by_head(mg_raw[:])[:, u], 0.0, None, ALU.max).then_inc(gs_max, 1)
                dve.wait_ge(gs_max, 2 * u + 2)
                dve.tensor_tensor(keys(dg[:, u, :]), keys(dg[:, u, :]),
                                  by_head(g_row[:, NV:EXW])[:, u].unsqueeze(3).broadcast_to([P, KC, 2, P]),
                                  ALU.subtract).then_inc(gs_shifted, 1)
            dve.wait_ge(gs_shifted, UNITS)
            dve.wait_ge(bias_in_psum, 1)
            dve.wait_ge(ld_bo, 16)
            dve.tensor_tensor(out_bias[:], ps[:, 4, 0:HID], bo_wide[:], ALU.add).then_inc(g_rows_ready, 1)
            dve.wait_ge(ld_w1, 16 * KC)
            dve.wait_ge(vecT_ready, 1)
            for c in range(KC):
                last = dve.tensor_tensor(w1s[:, c, :].rearrange("p (e h) -> p e h", h=EH), w1[:, c, :, :],
                                         vecT[:, c, EXPERTS:2 * EXPERTS].unsqueeze(2).broadcast_to([P, EXPERTS, EH]), ALU.mult)
            dve.wait_ge(b1_in_psum, 1)
            dve.wait_ge(ld_b, 48)
            for k in range(EPC):
                part = slice(k * EH, (k + 1) * EH)
                last = dve.tensor_tensor(b1s[part, :], ps[part, 6, k:EPC * FC:EPC], b1[part, :], ALU.add)
            dve.tensor_scalar(b2_sel[:, 0:1], pvals[:, 1:2], 1.5, None, ALU.is_le)
            dve.tensor_scalar(b2_sel[:, 2:3], pvals[:, 1:2], 3.5, None, ALU.is_ge)
            link(dve.tensor_copy(b2_h[:, 0, :], b2_f[:]))
            link(dve.tensor_tensor(b2_t[:, 0, :], b2_f[:], b2_h[:, 0, :], ALU.subtract))
            link(dve.tensor_copy(b2_h[:, 1, :], b2_t[:, 0, :]))
            link(dve.tensor_tensor(b2_t[:, 1, :], b2_t[:, 0, :], b2_h[:, 1, :], ALU.subtract))
            link(dve.tensor_tensor(b2_sel[:, 1:2], b2_sel[:, 0:1], b2_sel[:, 2:3], ALU.add))
            link(dve.tensor_scalar(b2_sel[:, 1:2], b2_sel[:, 1:2], -1.0, 1.0, ALU.mult, ALU.add))
            rs = slice(0, 3 * EXPERTS)
            link(dve.tensor_scalar(b2_t[:, 2, :], b2_t[:, 1, :], b2_sel[rs, 2:3], None, ALU.mult))
            link(dve.scalar_tensor_tensor(b2_t[:, 0, :], b2_h[:, 1, :], b2_sel[rs, 1:2], b2_t[:, 2, :], ALU.mult, ALU.add))
            dve.scalar_tensor_tensor(b2_stack[:], b2_h[:, 0, :], b2_sel[rs, 0:1], b2_t[:, 0, :], ALU.mult, ALU.add).then_inc(ffn_w_ready, 1)
            for b in range(B):
                dve.wait_ge(vall_in_psum, b + 1)
                dve.tensor_copy(wide(v_all[:, b * NV:(b + 1) * NV])[:, :, 0:DH],
                                ps[:, 2 + b, HID:2 * HID].rearrange("p (h e) -> p h e", e=DH)).then_inc(vall_ready, 1)
            dve.wait_ge(vall_ready, B)
            dve.wait_ge(table_ready, 16)

            def step(t, p, steady=False):
                nxt, cur, prev, pp = (live(t + k, steady) for k in (1, 0, -1, -2))

                def shift(u):
                    g = 4 * t + u
                    dve.wait_ge(scores_in_psum, g + 1)
                    dve.tensor_reduce(by_head(row_max[:, p, :])[:, u], keys(ps_score[u % 2]), op=ALU.max,
                                      axis=AX.X).then_inc(max_ready, 1)
                    if u == 0:
                        need(dve, e_arg_ready, t - 1)
                    dve.wait_ge(max_ready, g + 1)
                    dve.tensor_tensor(by_head(guard[:, p, :])[:, u], by_head(row_max[:, p, :])[:, u],
                                      by_head(table[:, bass.ds(t * EXW + NV, HEADS)])[:, u], ALU.max).then_inc(guard_ready, 1)
                    need(dve, dT_in_psum, g - 3)
                    dve.wait_ge(guard_ready, g + 1)
                    dve.tensor_tensor(keys(shifted[:, u, :]), keys(ps_score[u % 2]),
                                      by_head(guard[:, p, :])[:, u].unsqueeze(3).broadcast_to([P, KC, 2, P]),
                                      ALU.subtract).then_inc(shifted_ready, 1)

                if cur:
                    need(dve, num_ready, t - 1)
                    dve.wait_ge(r_in_psum, t + 1)
                    dve.tensor_tensor(rest[:, p, :], ps_rao[:, 0:NV], v_all[:, bass.ds(t // WPB * NV, NV)],
                                      ALU.add).then_inc(rest_ready, 1)
                    shift(0)
                    shift(1)
                if nxt:
                    dve.wait_ge(q_in_psum, t + 2)
                    for c in range(KC):
                        last = dve.scalar_tensor_tensor(qm[:, 1 - p, c, :, :],
                                                        ps_xq[:, HID + c * P:HID + (c + 1) * P].unsqueeze(1).broadcast_to([P, 2, P]),
                                                        bq_col[:, c:c + 1], q_scale[:], ALU.add, ALU.mult)
                    last.then_inc(q_ready, 1)
                if cur:
                    shift(2)
                if prev:
                    need(dve, attn_ready, t - 2)
                    dve.wait_ge(pv_in_psum, 4 * t)
                    dve.wait_ge(rest_step, 3 * t)
                    dve.tensor_tensor(num[:, 1 - p, :], ps_pv, rest[:, 1 - p, :], ALU.add).then_inc(num_ready, 1)
                if pp:
                    dve.wait_ge(o_in_psum, t - 1)
                    dve.wait_ge(biased_ready, t - 1)
                    need(dve, kept, t - 3)
                    dve.tensor_tensor(residual[:, p, :], ps_rao[:, 0:HID], biased[:, p, :], ALU.add).then_inc(residual_ready, 1)
                if prev:
                    dve.wait_ge(num_ready, t)
                    dve.reciprocal(rden[:, 1 - p, :], wide(num[:, 1 - p, :])[:, :, DH]).then_inc(rden_ready, 1)
                if pp:
                    dve.wait_ge(residual_ready, t - 1)
                    dve.bn_stats(bn6[:, 0, :], residual[:, p, :]).then_inc(bn_ready, 1)
                if cur:
                    if pp:
                        dve.wait_ge(bn_ready, t - 1)
                    shift(3)
                elif pp:
                    dve.wait_ge(bn_ready, t - 1)
                if pp:
                    dve.bn_aggr(mean_var[:, p, :], bn6[:, 0, :]).then_inc(stats_ready, 1)

            attention_steps(dve, step)

            def rsqrt(x, y, t, signal, start):
                k = [0]

                def link(ins):
                    k[0] += 1
                    ins.then_inc(signal, 1)
                    dve.wait_ge(signal, start + k[0])

                link(dve.tensor_scalar(t.bitcast(i32), x.bitcast(i32), 1, None, ALU.logical_shift_right))
                link(dve.tensor_scalar(y.bitcast(i32), t.bitcast(i32), -1.0, RSQRT_SEED, ALU.mult, ALU.add))
                for _ in range(NEWTON):
                    link(dve.tensor_tensor(t, y, y, ALU.mult))
                    link(dve.tensor_tensor(t, t, x, ALU.mult))
                    link(dve.tensor_scalar(t, t, -0.5, 1.5, ALU.mult, ALU.add))
                    link(dve.tensor_tensor(y, y, t, ALU.mult))
                return start + k[0]

            dve.wait_ge(kept, NW)
            var = stats[:].rearrange("p (w s) -> p w s", s=2)[:, :, 1]
            done = [0]

            def ln_link(ins):
                done[0] += 1
                ins.then_inc(ln_step, 1)
                dve.wait_ge(ln_step, done[0])

            ln_link(dve.tensor_scalar(nx[:], var, EPS, None, ALU.add))
            done[0] = rsqrt(nx[:], rs1[:], nt[:], ln_step, done[0])
            ln_link(dve.tensor_tensor(var1[:], rs1[:], rs1[:], ALU.mult))
            ln_link(dve.tensor_tensor(var1[:], var1[:], var, ALU.mult))
            ln_link(dve.tensor_scalar(var1[:], var1[:], EPS, None, ALU.add))
            done[0] = rsqrt(var1[:], rs2[:], nt[:], ln_step, done[0])
            ln_link(dve.tensor_tensor(rs2[:], rs1[:], rs2[:], ALU.mult))

            def step(n, p, steady=False):
                nxt, cur, prev = (live_group(n + k, steady) for k in (1, 0, -1))

                def normalise(j):
                    w = TG * (n + 1) + j
                    need(dve, xhT_in_psum, 2 * (n + 1) - 2 + j // 2 + 1)
                    dve.tensor_scalar(xh[:, j, :], row(rows, w, HID), stats[:, bass.ds(2 * w, 1)], rs2[:, bass.ds(w, 1)],
                                      ALU.subtract, ALU.mult).then_inc(xh_ready, 1)
                    dve.tensor_scalar(row(rows, w, HID), row(rows, w, HID), stats[:, bass.ds(2 * w, 1)], rs1[:, bass.ds(w, 1)],
                                      ALU.subtract, ALU.mult).then_inc(x1_ready, 1)

                def finish(j):
                    w = TG * (n - 1) + j
                    dve.wait_ge(y_in_psum, w + 1)
                    dve.wait_ge(x1_ready, w + 1)
                    dve.tensor_tensor(ysum[:, 1 - p, j, :], ps[:, 4 + j % 2, 0:HID], row(rows, w, HID), ALU.add).then_inc(ysum_ready, 1)
                    dve.wait_ge(ysum_ready, w + 1)
                    dve.bn_stats(bn6[:, j, :], ysum[:, 1 - p, j, :]).then_inc(ybn_ready, 1)

                for c in range(FC):
                    if nxt and c < 2:
                        normalise(2 * c)
                        normalise(2 * c + 1)
                    if cur:
                        dve.wait_ge(h_ready, 4 * n + c + 1)
                        dve.wait_ge(mask_in_psum, 4 * n + c + 1)
                        need(dve, y_in_psum, 4 * (n - 1))
                        dve.tensor_tensor(hm[:, p, c, :], ps[:, 2 + c % 2, :], hT[:, c, :], ALU.mult).then_inc(hm_ready, 1)
                    if nxt and c == FC - 1:
                        z = ps[:, 7, 0:TG * EXPERTS].rearrange("p (t e) -> p t e", e=EXPERTS)
                        r = 4 * (n + 1)
                        dve.wait_ge(z_in_psum, n + 2)
                        dve.tensor_reduce(zmax[:, 0, :], z, op=ALU.max, axis=AX.X).then_inc(route_step, 1)
                        dve.wait_ge(route_step, r + 1)
                        dve.tensor_tensor(hit[:], z, zmax[:, 0, :].unsqueeze(2).broadcast_to([P, TG, EXPERTS]), ALU.is_equal).then_inc(route_step, 1)
                        dve.wait_ge(route_step, r + 2)
                        dve.tensor_tensor(hit[:], hit[:], rank[:].unsqueeze(1).broadcast_to([P, TG, EXPERTS]), ALU.mult).then_inc(route_step, 1)
                        dve.wait_ge(route_step, r + 3)
                        dve.tensor_reduce(zmax[:, 1, :], hit[:], op=ALU.max, axis=AX.X).then_inc(route_step, 1)
                        dve.wait_ge(route_step, r + 4)
                        dve.tensor_tensor(onehot[:], hit[:].unsqueeze(2).broadcast_to([P, TG, 3, EXPERTS]),
                                          zmax[:, 1, :].unsqueeze(2).unsqueeze(2).broadcast_to([P, TG, 3, EXPERTS]),
                                          ALU.is_equal).then_inc(onehot_ready, 1)
                    if prev:
                        finish(c)
                if prev:
                    dve.wait_ge(ybn_ready, 4 * n)
                    dve.memset(yrs[:, 0, :], EPS)
                    for j in range(TG):
                        last = dve.bn_aggr(ystat[:, 1 - p, j, :], bn6[:, j, :])
                    last.then_inc(ystat_ready, 1)
                    k = (n - 1) * (NEWTON_STEPS + 1)
                    dve.wait_ge(ystat_ready, n)
                    dve.tensor_tensor(yrs[:, 0, :], ystat[:, 1 - p, :, 1], yrs[:, 0, :], ALU.add).then_inc(y_newton, 1)
                    dve.wait_ge(y_newton, k + 1)
                    rsqrt(yrs[:, 0, :], yrs[:, 1, :], yrs[:, 2, :], y_newton, k + 1)
                    need(dve, stored[1 - p], 16 * ((n - 1) // 2))
                    for j in range(TG):
                        last = dve.tensor_scalar(yout[:, 1 - p, j, :], ysum[:, 1 - p, j, :], ystat[:, 1 - p, j, 0:1],
                                                 yrs[:, 1, j:j + 1], ALU.subtract, ALU.mult)
                    last.then_inc(yout_ready, 1)

            expert_steps(dve, step)

        @block.tensor
        def _(pe):
            mm = nc.tensor.matmul

            def product(out, lhsT, rhs):
                for c in range(KC):
                    last = mm(out, lhsT(c), rhs(c), start=(c == 0), stop=(c == KC - 1))
                return last

            pe.wait_ge(pool_const, 5)
            pe.wait_ge(ld_xg, 16)
            for c in range(KC):
                last = nc.tensor.transpose(ps[:, 5, c * P:(c + 1) * P], xg[:, c * P:(c + 1) * P], ident[:])
            last.then_inc(xgT_in_psum, 1)
            pe.wait_ge(ld_gate, 112)
            for c in range(KC):
                last = nc.tensor.transpose(ps[:, 4, c * NVEC:(c + 1) * NVEC],
                                           vec_rows[:, c * P:(c + 1) * P], ident[0:NVEC, 0:NVEC])
            last = nc.tensor.transpose(ps[:, 4, KC * NVEC:KC * NVEC + FC], b1_rows[:], ident[0:FC, 0:FC])
            last.then_inc(vecT_in_psum, 1)
            pe.wait_ge(ld_w, 64)
            for i in range(4):
                for oc in range(KC):
                    for ic in range(KC):
                        last = nc.tensor.transpose(ps[:, i, ic * HID + oc * P:ic * HID + (oc + 1) * P],
                                                   w_raw[:, i, oc, ic * P:(ic + 1) * P], ident[:])
                last.then_inc(wT_in_psum, 1)
            pe.wait_ge(xgT_ready, 1)
            pe.wait_ge(wT_ready, 4)
            for o in range(KC):
                last = product(ps[:, 6, o * P:(o + 1) * P], lambda c: wT[:, WQ, c, o * P:(o + 1) * P], lambda c: xgT[:, c, :])
            last.then_inc(qg_in_psum, 1)
            for o in range(KC):
                product(ps[:, 7, o * P:(o + 1) * P], lambda c: wT[:, WK, c, o * P:(o + 1) * P], lambda c: xgT[:, c, :])
            product(ps[:, 7, HID:2 * HID], lambda c: xgT[:, c, :], lambda c: wT[:, WV, c, :]).then_inc(kvg_in_psum, 1)
            pe.wait_ge(qg_ready, 1)
            pe.wait_ge(kvg_ready, 1)
            for u in range(UNITS):
                for i, (c, a, _) in enumerate(heads_of(u)):
                    last = mm(ps[:, u, i * P:(i + 1) * P], qg[quad(u), c, a, :], kg[quad(u), c, :], start=True, stop=True)
                last.then_inc(gs_in_psum, 1)
            pe.wait_ge(vecT_ready, 1)
            pe.wait_ge(dve_const, 12)
            product(ps[:, 4, 0:HID], lambda c: bv_wide[:, c, :], lambda c: wT[:, WO, c, :]).then_inc(bias_in_psum, 1)
            pe.wait_ge(ld_w1, 16 * KC)
            for f in range(FC):
                last = product(ps[:, 6, f * EPC:(f + 1) * EPC],
                               lambda c: w1[:, c, f * EPC:(f + 1) * EPC, :].rearrange("p e h -> p (e h)"),
                               lambda c: vecT[:, c, 2 * EXPERTS + f * EPC:2 * EXPERTS + (f + 1) * EPC])
            last.then_inc(b1_in_psum, 1)
            for u in range(UNITS):
                pe.wait_ge(gs_shifted, u + 1)
                for i in range(HPU):
                    last = nc.tensor.transpose(ps[:, u, i * P:(i + 1) * P], dg[:, u, i * P:(i + 1) * P], ident[:])
                last.then_inc(gT_in_psum, 1)
            pe.wait_ge(kvg_ready, 2)
            for u in range(UNITS):
                pe.wait_ge(g_probs, u + 1)
                for i, (_, _, h) in enumerate(heads_of(u)):
                    last = mm(ps[:, 5, h * VA:(h + 1) * VA], pg[:, u, i * P:(i + 1) * P], vg[:, h * VA:(h + 1) * VA],
                              start=True, stop=True)
            last.then_inc(g_pv, 1)
            for b in range(B):
                pe.wait_ge(pool_step, 4 * (b + 1))
                for c in range(KC):
                    last = mm(ps[:, 2 + b, c * P:(c + 1) * P], xsum[:, b, c * P:(c + 1) * P], zero_w[:], start=True, stop=True)
                last.then_inc(xsumT_in_psum, 1)
            for b in range(B):
                pe.wait_ge(xsumT_ready, b + 1)
                product(ps[:, 2 + b, HID:2 * HID], lambda c: xsumT[:, b, c, :], lambda c: wT[:, WV, c, :]).then_inc(vall_in_psum, 1)
            pe.wait_ge(vall_ready, B)
            pe.wait_ge(g_rows_ready, 2)

            def step(t, p, steady=False):
                nxt, cur, prev, pp = (live(t + k, steady) for k in (1, 0, -1, -2))

                def scores(u):
                    g = 4 * t + u
                    if u == 0:
                        pe.wait_ge(q_ready, t + 1)
                        pe.wait_ge(k_ready, t + 1)
                    need(pe, shifted_ready, g - 1)
                    for i, (c, a, _) in enumerate(heads_of(u)):
                        last = mm(ps_score[u % 2][:, i * P:(i + 1) * P], qm[quad(u), p, c, a, :], kT[quad(u), p, c, :],
                                  start=True, stop=True)
                    last.then_inc(scores_in_psum, 1)

                def turn(w, u):
                    g = 4 * w + u
                    need(pe, probs_ready, g - 1)
                    pe.wait_ge(cut_ready, g + 1)
                    for i in range(HPU):
                        last = nc.tensor.transpose(ps_dT[u % 2][:, i * P:(i + 1) * P], shifted[:, u, i * P:(i + 1) * P], ident[:])
                    last.then_inc(dT_in_psum, 1)

                def weigh(w, u, pw):
                    pe.wait_ge(probs_ready, 4 * w + u + 1)
                    if u == 0:
                        need(pe, num_ready, w)
                    for i, (_, _, h) in enumerate(heads_of(u)):
                        last = mm(ps_pv[:, h * VA:(h + 1) * VA], probs[:, u, i * P:(i + 1) * P],
                                  va[:, pw, h * VA:(h + 1) * VA], start=True, stop=True)
                    last.then_inc(pv_in_psum, 1)

                if cur:
                    scores(0)
                if prev:
                    turn(t - 1, 2)
                    weigh(t - 1, 1, 1 - p)
                if pp:
                    if cur:
                        pe.wait_ge(rest_ready, t + 1)
                    pe.wait_ge(attn_ready, t - 1)
                    for c in range(KC):
                        last = nc.tensor.transpose(ps_rao[:, c * P:(c + 1) * P], attn[:, p, c * P:(c + 1) * P], ident[:])
                    last.then_inc(aT_in_psum, 1)
                if nxt:
                    need(pe, q_ready, t + 1)
                    pe.wait_ge(xs_ready, t + 2)
                    for c in range(KC):
                        last = nc.tensor.transpose(ps_xq[:, c * P:(c + 1) * P], xs[:, 1 - p, c * P:(c + 1) * P], ident[:])
                    last.then_inc(xT_in_psum, 1)
                if cur:
                    scores(1)
                if prev:
                    turn(t - 1, 3)
                    weigh(t - 1, 2, 1 - p)
                if nxt:
                    pe.wait_ge(xT_ready, t + 2)
                    for o in range(KC):
                        last = product(ps_xq[:, HID + o * P:HID + (o + 1) * P], lambda c: wT[:, WQ, c, o * P:(o + 1) * P],
                                       lambda c: xT[:, 1 - p, c, :])
                    last.then_inc(q_in_psum, 1)
                    need(pe, v_ready, t + 1)
                    for o in range(KC):
                        product(ps_kv[:, o * P:(o + 1) * P], lambda c: wT[:, WK, c, o * P:(o + 1) * P],
                                lambda c: xT[:, 1 - p, c, :])
                    product(ps_kv[:, HID:2 * HID], lambda c: xT[:, 1 - p, c, :], lambda c: wT[:, WV, c, :]).then_inc(kv_in_psum, 1)
                if cur:
                    scores(2)
                    turn(t, 0)
                if prev:
                    weigh(t - 1, 3, 1 - p)
                if pp:
                    pe.wait_ge(aT_ready, t - 1)
                    product(ps_rao[:, 0:HID], lambda c: aT[:, p, c, :], lambda c: wT[:, WO, c, :]).then_inc(o_in_psum, 1)
                if cur:
                    scores(3)
                    turn(t, 1)
                    weigh(t, 0, p)
                if nxt:
                    need(pe, residual_ready, t - 1)
                    pe.wait_ge(v_ready, t + 2)
                    mm(ps_rao[:, 0:NV], neg_zero_w[:], va[:, 1 - p, :], start=True, stop=True).then_inc(r_in_psum, 1)

            attention_steps(pe, step)
            pe.wait_ge(ffn_w_ready, 1)
            pe.wait_ge(residual_ready, NW)
            pe.wait_ge(ld_w2, 16)

            def step(n, p, steady=False):
                nxt, cur, prev = (live_group(n + k, steady) for k in (1, 0, -1))
                for c in range(FC):
                    if cur:
                        if c == 0:
                            pe.wait_ge(xhT_ready, 2 * n + 2)
                            pe.wait_ge(ohT_ready, n + 1)
                        need(pe, hm_ready, 4 * n + c - 1)
                        mm(ps[:, 2 + c % 2, :], pick[:, c, :], ohT[:, p, :], start=True, stop=True).then_inc(mask_in_psum, 1)
                        need(pe, h_ready, 4 * n + c - 1)
                        product(ps[:, c % 2, :], lambda k: w1s[:, k, c * P:(c + 1) * P], lambda k: xhT[:, p, k, :]).then_inc(h_in_psum, 1)
                    if nxt and c < 2:
                        g = 2 * (n + 1) + c
                        need(pe, xhT_ready, g)
                        pe.wait_ge(xh_ready, 2 * g + 2)
                        for j in range(2):
                            for k in range(KC):
                                last = nc.tensor.transpose(ps[:, 6, (j * KC + k) * P:(j * KC + k + 1) * P],
                                                           xh[:, 2 * c + j, k * P:(k + 1) * P], ident[:])
                        last.then_inc(xhT_in_psum, 1)
                    if nxt and c == 2:
                        pe.wait_ge(xhT_ready, 2 * n + 4)
                        need(pe, ohT_ready, n + 1)
                        for j in range(TG):
                            last = product(ps[:, 7, j * EXPERTS:(j + 1) * EXPERTS],
                                           lambda k: xhT[:, 1 - p, k, j * P:(j + 1) * P], lambda k: vecT[:, k, 0:EXPERTS])
                        last.then_inc(z_in_psum, 1)
                    if prev:
                        w = TG * (n - 1) + c
                        if c == 0:
                            pe.wait_ge(hm_ready, 4 * n)
                        need(pe, ysum_ready, w - 1)
                        y = ps[:, 4 + c % 2, 0:HID]
                        for f in range(FC):
                            mm(y, hm[:, 1 - p, f, c * P:(c + 1) * P], w2[:, f, :], start=(f == 0), stop=False)
                        mm(y, ohT[:, 1 - p, c * P:(c + 1) * P], b2_stack[:], start=False, stop=True).then_inc(y_in_psum, 1)
                if nxt:
                    pe.wait_ge(onehot_ready, n + 2)
                    for j in range(TG):
                        last = nc.tensor.transpose(ps[0:3 * EXPERTS, 7, 64 + j * P // 2:64 + (j + 1) * P // 2].bitcast(bf16),
                                                   onehot[:, j, :, :].rearrange("p r e -> p (r e)"), ident_b[:])
                    last.then_inc(ohT_in_psum, 1)

            expert_steps(pe, step)


_INS = ['L0_attn_x', 'L0_attn_wq', 'L0_attn_bq', 'L0_attn_wk', 'L0_attn_bk', 'L0_attn_wv', 'L0_attn_bv',
        'L0_attn_wo', 'L0_attn_bo', 'L0_ffn_Wg', 'L0_ffn_ln_scale', 'L0_ffn_ln_bias', 'L0_ffn_W1', 'L0_ffn_b1',
        'L0_ffn_W2', 'L0_ffn_b2']
_OUTS = [((2, 2048, 256), 'float32')]


def kernel(**inputs):
    import numpy as _np
    import concourse.bacc as _bacc
    from concourse import mybir as _mybir
    from concourse.bass_utils import run_bass_kernel_spmd as _run

    nc = _bacc.Bacc("TRN2", target_bir_lowering=False, num_devices=1)
    arrays, args = {}, []
    for name in _INS:
        a = _np.ascontiguousarray(inputs[name])
        arrays[f"in_{name}_dram"] = a
        args.append(nc.dram_tensor(f"in_{name}_dram", a.shape, _mybir.dt.from_np(a.dtype), kind="ExternalInput").ap())
    for i, (shape, dtype) in enumerate(_OUTS):
        dt = _mybir.dt.from_np(_np.dtype(dtype))
        args.append(nc.dram_tensor(f"out_{i}_dram", shape, dt, kind="ExternalOutput").ap())
    windowed_attention_then_top1_experts(nc, *args)
    r = _run(nc, [arrays], core_ids=[0])
    got = tuple(r.results[0][f"out_{i}_dram"] for i in range(len(_OUTS)))
    return got[0]
```

```python
import concourse.bass as bass
from concourse import mybir
from contextlib import ExitStack


def windowed_attention_then_top1_experts(
    nc: bass.Bass,
    x_dram: bass.AP,
    wq_dram: bass.AP,
    bq_dram: bass.AP,
    wk_dram: bass.AP,
    bk_dram: bass.AP,
    wv_dram: bass.AP,
    bv_dram: bass.AP,
    wo_dram: bass.AP,
    bo_dram: bass.AP,
    wg_dram: bass.AP,
    ln_scale_dram: bass.AP,
    ln_bias_dram: bass.AP,
    w1_dram: bass.AP,
    b1_dram: bass.AP,
    w2_dram: bass.AP,
    b2_dram: bass.AP,
    out_dram: bass.AP,
):
    fp32 = mybir.dt.float32
    bf16 = mybir.dt.bfloat16
    i32 = mybir.dt.int32
    ALU = mybir.AluOpType
    ACT = mybir.ActivationFunctionType
    AX = mybir.AxisListType

    P = 128
    B, S, HID = x_dram.shape
    HEADS = 16
    DH = HID // HEADS
    WINDOW = 128
    GLOBALS = 64
    STRIDE = S // GLOBALS
    GPW = WINDOW // STRIDE
    NW = B * S // WINDOW
    WPB = S // WINDOW
    KC = HID // P
    UNITS = 4
    HPU = HEADS // UNITS
    VP = 32
    VA = DH + 1
    NV = HEADS * VA
    EXW = NV + HEADS
    SCALE = float(DH) ** -0.5
    CUT = -1.0e30
    EXPERTS, _, EH = w1_dram.shape
    FC = EXPERTS * EH // P
    EPC = P // EH
    EPS = 1e-5
    TG = 4
    NG = NW // TG
    NVEC = 3 * EXPERTS + 3
    GT = TG * P
    RSQRT_SEED = float(0x5F3759DF)
    NEWTON = 3
    NEWTON_STEPS = 2 + 4 * NEWTON

    ctx = ExitStack()
    with ctx:
        def sb(name, shape, dt=fp32):
            return ctx.enter_context(nc.sbuf_tensor(name, shape, dt))

        def sem(name):
            return ctx.enter_context(nc.semaphore(name))

        rows = sb("rows", [P, NW * HID])
        xg = sb("xg", [P, HID])
        w_raw = sb("w_raw", [P, 4, KC, HID])
        wT = sb("wT", [P, 4, KC, HID])
        bv_wide = sb("bv_wide", [P, KC, P])
        bo_wide = sb("bo_wide", [P, HID])
        out_bias = sb("out_bias", [P, HID])
        ident = sb("ident", [P, P])
        ident_b = sb("ident_b", [P, P], bf16)
        pid = sb("pid", [P, 1], i32)
        cid = sb("cid", [P, P], i32)
        pbits = sb("pbits", [P, 4], i32)
        pvals = sb("pvals", [P, 4])
        cbits = sb("cbits", [P, 2, P], i32)
        cvals = sb("cvals", [P, 2, P])
        is_glob = sb("is_glob", [P, 1])
        q_scale = sb("q_scale", [P, 2, P])
        zero_w = sb("zero_w", [P, P])
        neg_zero_w = sb("neg_zero_w", [P, P])
        cut_cols = sb("cut_cols", [P, HPU, GPW])
        zeros16 = sb("zeros16", [P, HEADS])
        g_factor = sb("g_factor", [P, P])
        g_cut = sb("g_cut", [P, P])
        xgT = sb("xgT", [P, KC, P])
        qg = sb("qg", [P, KC, 2, P])
        kg = sb("kg", [P, KC, P])
        vg = sb("vg", [P, NV])
        dg = sb("dg", [P, UNITS, HPU * P])
        pg = sb("pg", [P, UNITS, HPU * P])
        mg_raw = sb("mg_raw", [P, HEADS])
        g_row = sb("g_row", [P, EXW])
        table = sb("table", [P, NW * EXW])
        xsum = sb("xsum", [P, B, WPB // 2 * HID])
        xsumT = sb("xsumT", [P, B, KC, P])
        v_all = sb("v_all", [P, B * NV])

        xs = sb("xs", [P, 2, HID])
        xT = sb("xT", [P, 2, KC, P])
        qm = sb("qm", [P, 2, KC, 2, P])
        kT = sb("kT", [P, 2, KC, P])
        va = sb("va", [P, 2, HEADS * VP])
        pvT = sb("pvT_t", [P, 512])
        row_max = sb("row_max_t", [P, 2, HEADS])
        guard = sb("guard_t", [P, 2, HEADS])
        shifted = sb("shifted_t", [P, UNITS, HPU * P])
        probs = sb("probs_t", [P, UNITS, HPU * P])
        e_arg = sb("e_arg_t", [P, 2, 2 * HEADS])
        e_val = sb("e_val_t", [P, 2, 2 * HEADS])
        rest = sb("rest_t", [P, 2, NV])
        gl = sb("gl_t", [P, NV])
        num = sb("num_t", [P, 2, NV])
        rden = sb("rden_t", [P, 2, HEADS])
        attn = sb("attn_t", [P, 2, HID])
        aT = sb("aT_t", [P, 2, KC, P])
        biased = sb("biased_t", [P, 2, HID])
        residual = sb("residual_t", [P, 2, HID])
        bn6 = sb("bn6", [P, TG, 6])
        mean_var = sb("mean_var", [P, 2, 2])
        stats = sb("stats_t", [P, NW * 2])

        rs1 = sb("rs1", [P, NW])
        var1 = sb("var1", [P, NW])
        rs2 = sb("rs2", [P, NW])
        nt = sb("newton_t", [P, NW])
        ny = sb("newton_y", [P, NW])
        nx = sb("newton_x", [P, NW])

        vec_rows = sb("vec_rows", [NVEC, HID])
        vecT = sb("vecT", [P, KC, NVEC])
        bq_col, bk_col, bv_col = (vecT[:, :, 3 * EXPERTS + i] for i in range(3))
        b1_rows = sb("b1_rows", [FC, P])
        w1 = sb("w1", [P, KC, EXPERTS, EH])
        w1s = sb("w1s", [P, KC, EXPERTS * EH])
        w2 = sb("w2", [P, FC, HID])
        b1 = sb("b1", [P, FC])
        b1s = sb("b1s", [P, FC])
        b2_f = sb("b2_f", [3 * EXPERTS, HID])
        b2_h = sb("b2_h", [3 * EXPERTS, 3, HID], bf16)
        b2_sel = sb("b2_sel", [P, 3])
        b2_t = sb("b2_t", [3 * EXPERTS, 3, HID])
        b2_stack = sb("b2_stack", [3 * EXPERTS, HID], bf16)
        pick = sb("pick", [3 * EXPERTS, FC, P], bf16)
        rank = sb("rank", [P, EXPERTS])
        rank_i = sb("rank_i", [P, EXPERTS], i32)
        xh = pg[:, 0:2, :].rearrange("p u (t n) -> p (u t) n", t=TG // 2)
        xhT = xsum[:, 0, :].rearrange("p (b c n) -> p b c n", b=2, c=KC)
        zmax = sb("zmax", [P, 2, TG])
        hit = sb("hit", [P, TG, EXPERTS])
        onehot = sb("onehot", [P, TG, 3, EXPERTS], bf16)
        ohT = sb("ohT", [3 * EXPERTS, 2, GT], bf16)
        hT = xsum[:, 1, :].rearrange("p (f n) -> p f n", f=FC)
        hm = table[:, 0:4096].rearrange("p (b f n) -> p b f n", b=2, f=FC)
        ysum = table[:, 4096:6144].rearrange("p (b t n) -> p b t n", b=2, t=TG)
        ystat = sb("ystat", [P, 2, TG, 2])
        yrs = sb("yrs", [P, 2, TG])
        yout = table[:, 6144:8192].rearrange("p (b t n) -> p b t n", b=2, t=TG)
        yvar = sb("yvar", [P, TG])
        ytmp = sb("ytmp", [P, TG])

        scratch = nc.dram_tensor("global_sums", (P, EXW), fp32, kind="Internal").ap()

        ps = ctx.enter_context(nc.psum_tensor("ps", [P, 8, 512], fp32))
        ps_score = [ps[:, 0, :], ps[:, 1, :]]
        ps_dT = [ps[:, 2, :], ps[:, 3, :]]
        ps_xq = ps[:, 4, :]
        ps_kv = ps[:, 5, :]
        ps_rao = ps[:, 6, :]
        ps_pv = ps[:, 7, :]

        def quad(u):
            return slice(32 * u, 32 * u + 32)

        def by_head(ap):
            return ap.rearrange("p (c u a) -> p u c a", c=KC, u=UNITS)

        def heads_of(u):
            return [(c, a, 8 * c + 2 * u + a) for c in range(KC) for a in range(2)]

        def keys(ap):
            return ap.rearrange("p (c a j) -> p c a j", c=KC, a=2)

        def wide(ap):
            return ap.rearrange("p (h e) -> p h e", e=VA)

        def padded(ap):
            return ap.rearrange("p (h e) -> p h e", e=VP)

        def row(ap, w, width):
            return ap[:, bass.ds(w * width, width)]

        def need(eng, s, count):
            if not isinstance(count, int) or count > 0:
                eng.wait_ge(s, count)

        ld_xg, ld_w, ld_bo, ld_gate, ld_w1, ld_w2, ld_b = (
            sem(n) for n in ("ld_xg", "ld_w", "ld_bo", "ld_gate", "ld_w1", "ld_w2", "ld_b"))
        ld_x = [sem(f"ld_x{i}") for i in range(8)]
        pool_const = sem("pool_const")
        dve_const = sem("dve_const")
        table_zero = sem("table_zero")
        wT_in_psum = sem("wT_in_psum")
        wT_ready = sem("wT_ready")
        vecT_in_psum = sem("vecT_in_psum")
        vecT_ready = sem("vecT_ready")
        xgT_in_psum = sem("xgT_in_psum")
        xgT_ready = sem("xgT_ready")
        qg_in_psum = sem("qg_in_psum")
        qg_ready = sem("qg_ready")
        kvg_in_psum = sem("kvg_in_psum")
        kvg_ready = sem("kvg_ready")
        bias_in_psum = sem("bias_in_psum")
        bias_ready = sem("bias_ready")
        b1_in_psum = sem("b1_in_psum")
        gs_in_psum = sem("gs_in_psum")
        gs_scaled = sem("gs_scaled")
        gs_cut = sem("gs_cut")
        gs_max = sem("gs_max")
        gs_shifted = sem("gs_shifted")
        gT_in_psum = sem("gT_in_psum")
        g_probs = sem("g_probs")
        g_pv = sem("g_pv")
        g_rows_ready = sem("g_rows_ready")
        g_stored = sem("g_stored")
        table_ready = sem("table_ready")
        xsum_ready = sem("xsum_ready")
        pool_step = sem("pool_step")
        xsumT_in_psum = sem("xsumT_in_psum")
        xsumT_ready = sem("xsumT_ready")
        vall_in_psum = sem("vall_in_psum")
        vall_ready = sem("vall_ready")
        ffn_w_ready = sem("ffn_w_ready")
        xs_ready = [sem("xs_ready0"), sem("xs_ready1")]
        xT_in_psum = sem("xT_in_psum")
        xT_ready = sem("xT_ready")
        q_in_psum = sem("q_in_psum")
        q_ready = sem("q_ready")
        kv_in_psum = sem("kv_in_psum")
        k_ready = sem("k_ready")
        v_ready = sem("v_ready")
        scores_in_psum = sem("scores_in_psum")
        max_ready = sem("max_ready")
        guard_ready = sem("guard_ready")
        shifted_ready = sem("shifted_ready")
        cut_ready = sem("cut_ready")
        dT_in_psum = sem("dT_in_psum")
        probs_ready = sem("probs_ready")
        pv_in_psum = sem("pv_in_psum")
        pvT_ready = sem("pvT_ready")
        sums_in_psum = sem("sums_in_psum")
        r_in_psum = sem("r_in_psum")
        rest_ready = sem("rest_ready")
        e_arg_ready = sem("e_arg_ready")
        e_ready = sem("e_ready")
        rest_step = sem("rest_step")
        num_ready = sem("num_ready")
        rden_ready = sem("rden_ready")
        attn_ready = sem("attn_ready")
        aT_in_psum = sem("aT_in_psum")
        aT_ready = sem("aT_ready")
        o_in_psum = sem("o_in_psum")
        biased_ready = sem("biased_ready")
        residual_ready = sem("residual_ready")
        bn_ready = sem("bn_ready")
        stats_ready = sem("stats_ready")
        moments_ready = sem("moments_ready")
        centred = sem("centred")
        kept = [sem("kept0"), sem("kept1")]
        ln_step = sem("ln_step")
        ln_ready = sem("ln_ready")
        xh_ready = sem("xh_ready")
        xhT_in_psum = sem("xhT_in_psum")
        xhT_ready = sem("xhT_ready")
        z_in_psum = sem("z_in_psum")
        route_step = sem("route_step")
        onehot_ready = sem("onehot_ready")
        ohT_in_psum = sem("ohT_in_psum")
        ohT_ready = sem("ohT_ready")
        h_in_psum = sem("h_in_psum")
        mask_in_psum = sem("mask_in_psum")
        h_ready = sem("h_ready")
        hm_ready = sem("hm_ready")
        y_in_psum = sem("y_in_psum")
        ysum_ready = sem("ysum_ready")
        ybn_ready = sem("ybn_ready")
        ystat_ready = sem("ystat_ready")
        y_newton = sem("y_newton")
        yrs_ready = sem("yrs_ready")
        y_centred = sem("y_centred")
        yout_ready = sem("yout_ready")
        stored = [sem("stored0"), sem("stored1")]

        WQ, WK, WV, WO = range(4)
        x_w = x_dram.rearrange("b (w p) d -> p (b w) d", p=P)
        block = ctx.enter_context(nc.Block())

        LOOP_A = (3, NW - 1)
        EARLY = NW - TG

        def attention_steps(eng, step):
            for t in range(-1, LOOP_A[0]):
                step(t, t % 2)
            with eng.Fori(LOOP_A[0], LOOP_A[1] - 1, 2) as t:
                for k in range(2):
                    step(t + k, (LOOP_A[0] + k) % 2, steady=True)
            for t in range(LOOP_A[1], NW + 2):
                step(t, t % 2)

        def live(w, steady):
            return steady or 0 <= w < NW

        LOOP_B = (2, NG - 2)

        def expert_steps(eng, step):
            for n in range(-1, LOOP_B[0]):
                step(n, n % 2)
            with eng.Fori(LOOP_B[0], LOOP_B[1] - 1, 2) as n:
                for k in range(2):
                    step(n + k, (LOOP_B[0] + k) % 2, steady=True)
            for n in range(LOOP_B[1], NG + 2):
                step(n, n % 2)

        def live_group(n, steady):
            return steady or 0 <= n < NG

        @block.sync
        def _(sp):
            sp.dma_start(xg[:], x_dram.rearrange("b (g s) d -> (b g) s d", s=STRIDE)[:, 0, :]).then_inc(ld_xg, 16)
            for i, w in enumerate((wq_dram, wk_dram, wv_dram, wo_dram)):
                sp.dma_start(w_raw[:, i, :, :], w.rearrange("(c p) n -> p c n", p=P)).then_inc(ld_w, 16)
            x_t = x_w
            rows_v = rows[:].rearrange("p (w d) -> p w d", d=HID)
            for i in range(8):
                k = NW // 8
                sp.dma_start(rows_v[:, i * k:(i + 1) * k, :], x_t[:, i * k:(i + 1) * k, :]).then_inc(ld_x[i], 16)
            for c in range(KC):
                sp.dma_start(w1[:, c, :, :], w1_dram[:, c * P:(c + 1) * P, :].rearrange("e p h -> p e h")).then_inc(ld_w1, 16)
            sp.dma_start(w2[:], w2_dram.rearrange("(c e) h d -> (e h) c d", e=EPC)).then_inc(ld_w2, 16)
            sp.wait_ge(g_rows_ready, 2)
            sp.dma_start(scratch, g_row[:]).then_inc(g_stored, 16)
            sp.wait_ge(g_stored, 16)
            sp.wait_ge(table_zero, 1)
            sp.dma_start(table[0:P:STRIDE, :].rearrange("a (w c) -> a w c", c=EXW),
                         scratch.rearrange("(w a) c -> a w c", a=GPW)).then_inc(table_ready, 16)

            def step(t, p, steady=False):
                if live(t + 1, steady):
                    need(sp, xT_in_psum, t)
                    sp.dma_start(xs[:, 1 - p, :], x_w[:, bass.ds(t + 1, 1), :]).then_inc(xs_ready[1 - p], 16)
                if live(t - 3, steady):
                    sp.wait_ge(centred, t - 2)
                    sp.dma_start(row(rows, t - 3, HID), residual[:, 1 - p, :]).then_inc(kept[1 - p], 16)

            attention_steps(sp, step)
            sp.wait_ge(centred, NW)
            sp.dma_start(row(rows, NW - 1, HID), residual[:, (NW - 1) % 2, :]).then_inc(kept[(NW - 1) % 2], 16)

            def step(n, p, steady=False):
                if live_group(n - 2, steady):
                    sp.wait_ge(yout_ready, n - 1)
                    out_t = out_dram.rearrange("b (w p) d -> p (b w) d", p=P)
                    sp.dma_start(out_t[:, bass.ds((n - 2) * TG, TG), :], yout[:, p, :, :]).then_inc(stored[p], 16)
            expert_steps(sp, step)
            for p in range(2):
                sp.wait_ge(stored[p], 16 * (NG // 2))

        @block.gpsimd
        def _(pool):
            pool.memset(ident[:], 0.0).then_inc(pool_const, 1)
            pool.memset(ident_b[:], 0.0).then_inc(pool_const, 1)
            pool.memset(pick[:], 0.0).then_inc(pool_const, 1)
            pool.wait_ge(pool_const, 3)
            for m in (ident, ident_b):
                pool.affine_select(out=m[:], in_=m[:], compare_op=ALU.not_equal, fill=1.0, base=0,
                                   pattern=[[-1, P]], channel_multiplier=1).then_inc(pool_const, 1)
            pool.iota(pid[:], pattern=[[0, 1]], base=0, channel_multiplier=1).then_inc(pool_const, 1)
            pool.iota(cid[:], pattern=[[1, P]], base=0, channel_multiplier=0).then_inc(pool_const, 1)
            pool.affine_select(out=pick[:].rearrange("r c (k h) -> r c k h", k=EPC), in_=pick[:].rearrange("r c (k h) -> r c k h", k=EPC),
                               compare_op=ALU.not_equal, fill=1.0, base=0,
                               pattern=[[-EPC, FC], [-1, EPC], [0, EH]], channel_multiplier=1).then_inc(pool_const, 1)
            pool.iota(rank_i[:], pattern=[[-1, EXPERTS]], base=EXPERTS, channel_multiplier=0).then_inc(pool_const, 1)
            pool.memset(va[:], 0.0).then_inc(pool_const, 1)
            pool.wait_ge(pool_const, 10)
            pool.memset(padded(va[:].rearrange("p b n -> p (b n)"))[:, :, DH:VA], 1.0).then_inc(pool_const, 1)
            pool.memset(vg[:], 1.0).then_inc(pool_const, 1)
            pool.memset(zeros16[:], 0.0).then_inc(pool_const, 1)
            pool.memset(table[:], 0.0).then_inc(table_zero, 1)
            for b in range(B):
                for i in range(4):
                    pool.wait_ge(ld_x[4 * b + i], 16)
                n = WPB // 2 * HID
                base = b * WPB * HID
                pool.tensor_tensor(xsum[:, b, 0:n], rows[:, base:base + n], rows[:, base + n:base + 2 * n],
                                   ALU.add).then_inc(pool_step, 1)
                k = 1
                while n > HID:
                    n //= 2
                    pool.wait_ge(pool_step, 4 * b + k)
                    done = pool.tensor_tensor(xsum[:, b, 0:n], xsum[:, b, 0:n], xsum[:, b, n:2 * n], ALU.add)
                    done.then_inc(pool_step, 1)
                    k += 1
            pool.wait_ge(table_ready, 16)

            def step(t, p, steady=False):
                nxt, cur, prev, pp = (live(t + k, steady) for k in (1, 0, -1, -2))

                def cut(u):
                    pool.wait_ge(shifted_ready, 4 * t + u + 1)
                    part = shifted[:, u, :].rearrange("p (h j) -> p h j", j=P)[:, :, 0:P:STRIDE]
                    pool.tensor_tensor(part, part, cut_cols[:], ALU.add).then_inc(cut_ready, 1)

                if cur:
                    cut(0)
                if prev:
                    pool.wait_ge(rest_ready, t)
                    pool.wait_ge(e_ready, t)
                    e = e_val[:, 1 - p, :]
                    r = wide(rest[:, 1 - p, :])
                    pool.tensor_tensor(r, r, e[:, 0:HEADS].unsqueeze(2).broadcast_to([P, HEADS, VA]),
                                       ALU.mult).then_inc(rest_step, 1)
                    pool.tensor_tensor(wide(gl[:]), wide(table[:, bass.ds((t - 1) * EXW, NV)]),
                                       e[:, HEADS:2 * HEADS].unsqueeze(2).broadcast_to([P, HEADS, VA]),
                                       ALU.mult).then_inc(rest_step, 1)
                    pool.wait_ge(rest_step, 3 * t - 1)
                    pool.tensor_tensor(rest[:, 1 - p, :], rest[:, 1 - p, :], gl[:], ALU.add).then_inc(rest_step, 1)
                if cur:
                    cut(1)
                if cur:
                    cut(2)
                if pp:
                    need(pool, residual_ready, t - 3)
                    pool.tensor_tensor(biased[:, p, :], row(rows, t - 2, HID), out_bias[:], ALU.add).then_inc(biased_ready, 1)
                if live(t - 3, steady):
                    pool.wait_ge(stats_ready, t - 2)
                    pool.tensor_tensor(residual[:, 1 - p, :], residual[:, 1 - p, :],
                                       mean_var[:, 1 - p, 0:1].broadcast_to([P, HID]), ALU.subtract).then_inc(centred, 1)
                if cur:
                    cut(3)
                    need(pool, e_ready, t - 1)
                    pool.wait_ge(guard_ready, 4 * t + 4)
                    pool.tensor_tensor(e_arg[:, p, 0:HEADS], zeros16[:], guard[:, p, :], ALU.subtract)
                    pool.tensor_tensor(e_arg[:, p, HEADS:2 * HEADS], table[:, bass.ds(t * EXW + NV, HEADS)],
                                       guard[:, p, :], ALU.subtract).then_inc(e_arg_ready, 1)
                if prev:
                    need(pool, aT_in_psum, t - 2)
                    pool.wait_ge(rden_ready, t)
                    pool.tensor_tensor(attn[:, 1 - p, :].rearrange("p (h e) -> p h e", e=DH),
                                       wide(num[:, 1 - p, :])[:, :, 0:DH],
                                       rden[:, 1 - p, :].unsqueeze(2).broadcast_to([P, HEADS, DH]),
                                       ALU.mult).then_inc(attn_ready, 1)

            attention_steps(pool, step)
            pool.wait_ge(stats_ready, NW)
            last = (NW - 1) % 2
            pool.tensor_tensor(residual[:, last, :], residual[:, last, :],
                               mean_var[:, last, 0:1].broadcast_to([P, HID]), ALU.subtract).then_inc(centred, 1)

            def normalise(m, p):
                part = ysum[:, p, :, :]
                need(pool, stored[p], 16 * (m // 2))
                pool.wait_ge(ystat_ready, m + 1)
                pool.tensor_tensor(yout[:, p, :, :], part, ystat[:, p, :, 0:1].broadcast_to([P, TG, HID]),
                                   ALU.subtract).then_inc(y_centred, 1)
                pool.wait_ge(y_centred, m + 1)
                pool.wait_ge(yrs_ready, m + 1)
                pool.tensor_tensor(yout[:, p, :, :], yout[:, p, :, :],
                                   yrs[:, p, :].unsqueeze(2).broadcast_to([P, TG, HID]), ALU.mult).then_inc(yout_ready, 1)

            def step(n, p, steady=False):
                if live_group(n - 2, steady):
                    normalise(n - 2, p)

            expert_steps(pool, step)

        @block.scalar
        def _(act):
            act.dma_start(bo_wide[:], bo_dram.rearrange("(a n) -> a n", a=1).broadcast_to([P, HID])).then_inc(ld_bo, 16)
            for i, src in enumerate((wg_dram, ln_scale_dram, ln_bias_dram)):
                act.dma_start(vec_rows[EXPERTS * i:EXPERTS * (i + 1), :], src).then_inc(ld_gate, 16)
            for i, src in enumerate((bq_dram, bk_dram, bv_dram)):
                act.dma_start(vec_rows[3 * EXPERTS + i:3 * EXPERTS + i + 1, :],
                              src.rearrange("(a n) -> a n", a=1)).then_inc(ld_gate, 16)
            act.dma_start(b1_rows[:], b1_dram.rearrange("(c e) h -> c (e h)", e=EPC)).then_inc(ld_gate, 16)
            for i in range(3):
                act.dma_start(b2_f[EXPERTS * i:EXPERTS * (i + 1), :], b2_dram).then_inc(ld_b, 16)

            def copy(dst, src):
                return act.activation(dst, src, ACT.Copy)

            act.wait_ge(xgT_in_psum, 1)
            copy(xgT[:].rearrange("p c n -> p (c n)"), ps[:, 5, 0:HID]).then_inc(xgT_ready, 1)
            act.wait_ge(vecT_in_psum, 1)
            copy(b1[:], ps[:, 4, KC * NVEC:KC * NVEC + FC])
            copy(vecT[:].rearrange("p c n -> p (c n)"), ps[:, 4, 0:KC * NVEC]).then_inc(vecT_ready, 1)
            for i in (WV, WO):
                act.wait_ge(wT_in_psum, i + 1)
                copy(wT[:, i, :, :].rearrange("p c n -> p (c n)"), ps[:, i, :]).then_inc(wT_ready, 1)
            act.wait_ge(kvg_in_psum, 1)
            act.wait_ge(pool_const, 13)
            for c in range(KC):
                last = act.activation(kg[:, c, :], ps[:, 7, c * P:(c + 1) * P], ACT.Identity, bias=bk_col[:, c:c + 1])
            last.then_inc(kvg_ready, 1)
            copy(wide(vg[:])[:, :, 0:DH], ps[:, 7, HID:2 * HID].rearrange("p (h e) -> p h e", e=DH)).then_inc(kvg_ready, 1)
            for u in range(UNITS):
                act.wait_ge(gT_in_psum, u + 1)
                act.activation(pg[:, u, :], ps[:, u, :], ACT.Exp).then_inc(g_probs, 1)
            act.wait_ge(g_pv, 1)
            copy(g_row[:, 0:NV], ps[:, 5, 0:NV]).then_inc(g_rows_ready, 1)
            for b in range(B):
                act.wait_ge(xsumT_in_psum, b + 1)
                copy(xsumT[:, b, :, :].rearrange("p c n -> p (c n)"), ps[:, 2 + b, 0:HID]).then_inc(xsumT_ready, 1)

            def step(t, p, steady=False):
                nxt, cur, prev, pp = (live(t + k, steady) for k in (1, 0, -1, -2))

                def exp(w, u):
                    g = 4 * w + u
                    need(act, pv_in_psum, g - 3)
                    act.wait_ge(dT_in_psum, g + 1)
                    act.activation(probs[:, u, :], ps_dT[u % 2], ACT.Exp).then_inc(probs_ready, 1)

                if prev:
                    exp(t - 1, 2)
                    need(act, rest_step, 3 * (t - 2))
                    act.wait_ge(e_arg_ready, t)
                    act.activation(e_val[:, 1 - p, :], e_arg[:, 1 - p, :], ACT.Exp).then_inc(e_ready, 1)
                if nxt:
                    need(act, kv_in_psum, t)
                    act.wait_ge(xT_in_psum, t + 2)
                    copy(xT[:, 1 - p, :, :].rearrange("p c n -> p (c n)"), ps_xq[:, 0:HID]).then_inc(xT_ready, 1)
                if prev:
                    exp(t - 1, 3)
                if pp:
                    need(act, o_in_psum, t - 3)
                    act.wait_ge(aT_in_psum, t - 1)
                    copy(aT[:, p, :, :].rearrange("p c n -> p (c n)"), ps_rao[:, 0:HID]).then_inc(aT_ready, 1)
                if nxt:
                    need(act, scores_in_psum, 4 * t)
                    act.wait_ge(kv_in_psum, t + 2)
                    for c in range(KC):
                        last = act.activation(kT[:, 1 - p, c, :], ps_kv[:, c * P:(c + 1) * P], ACT.Identity,
                                              bias=bk_col[:, c:c + 1])
                    last.then_inc(k_ready, 1)
                if cur:
                    exp(t, 0)
                if prev:
                    need(act, sums_in_psum, t - 1)
                    act.wait_ge(pv_in_psum, 4 * t)
                    copy(pvT[:], ps_pv).then_inc(pvT_ready, 1)
                if nxt:
                    need(act, pv_in_psum, 4 * t)
                    copy(padded(va[:, 1 - p, :])[:, :, 0:DH],
                         ps_kv[:, HID:2 * HID].rearrange("p (h e) -> p h e", e=DH)).then_inc(v_ready, 1)
                if cur:
                    exp(t, 1)

            attention_steps(act, step)

            def scale_rows(n, pair):
                for j in (2 * pair, 2 * pair + 1):
                    w = TG * n + j
                    act.activation(xh[:, j, :], row(rows, w, HID), ACT.Copy, scale=rs2[:, bass.ds(w, 1)]).then_inc(xh_ready, 1)

            def step(n, p, steady=False):
                nxt, cur, prev = (live_group(n + k, steady) for k in (1, 0, -1))

                def evacuate(pair):
                    need(act, h_in_psum, 4 * n)
                    act.wait_ge(xhT_in_psum, 2 * (n + 1) + pair + 1)
                    act.activation(xhT[:, 1 - p, :, pair * 2 * P:(pair + 1) * 2 * P].rearrange("p c (t n) -> p t c n", t=2),
                                   ps[:, 6, :].rearrange("p (t c n) -> p t c n", t=2, c=KC), ACT.Copy).then_inc(xhT_ready, 1)
                    if live_group(n + 2, steady):
                        scale_rows(n + 2, pair)

                for c in range(FC):
                    if cur:
                        need(act, hm_ready, 4 * n + c - 3)
                        act.wait_ge(h_in_psum, 4 * n + c + 1)
                        act.activation(hT[:, c, :], ps[:, c % 2, :], ACT.Gelu, bias=b1s[:, c:c + 1]).then_inc(h_ready, 1)
                    if nxt and c < 2:
                        evacuate(c)
                if nxt:
                    need(act, y_in_psum, 4 * n)
                    act.wait_ge(ohT_in_psum, n + 2)
                    act.activation(ohT[:, 1 - p, :], ps[0:3 * EXPERTS, 7, 64:64 + GT // 2].bitcast(bf16), ACT.Copy).then_inc(ohT_ready, 1)
                if not steady and n == 0:
                    for k in kept:
                        act.wait_ge(k, 16 * (NW // 2))
                    act.wait_ge(ln_ready, 2)

            act.wait_ge(ffn_w_ready, 1)
            for k in kept:
                act.wait_ge(k, 16 * (EARLY // 2))
            act.wait_ge(ln_ready, 1)
            for pair in range(2):
                scale_rows(0, pair)
            expert_steps(act, step)

        @block.vector
        def _(dve):
            count = [0]

            def link(ins):
                count[0] += 1
                ins.then_inc(dve_const, 1)
                dve.wait_ge(dve_const, count[0])

            dve.wait_ge(pool_const, 13)
            dve.tensor_scalar(pbits[:, 0:1], pid[:], DH, None, ALU.bitwise_and)
            dve.tensor_scalar(pbits[:, 1:2], pid[:], 2, None, ALU.logical_shift_right)
            dve.tensor_scalar(pbits[:, 2:3], pid[:], 6, None, ALU.logical_shift_right)
            link(dve.tensor_scalar(pbits[:, 3:4], pid[:], STRIDE - 1, None, ALU.bitwise_and))
            dve.tensor_scalar(cbits[:, 0, :], cid[:], 2, None, ALU.logical_shift_right)
            link(dve.tensor_scalar(cbits[:, 1, :], cid[:], 6, None, ALU.logical_shift_right))
            dve.tensor_copy(pvals[:], pbits[:])
            link(dve.tensor_copy(cvals[:], cbits[:]))
            dve.tensor_scalar(q_scale[:, 0, :], pvals[:, 0:1].broadcast_to([P, P]), 0.0, SCALE, ALU.is_equal, ALU.mult)
            link(dve.tensor_scalar(q_scale[:, 1, :], pvals[:, 0:1].broadcast_to([P, P]), float(DH), SCALE, ALU.is_equal, ALU.mult))
            for i in (WQ, WK):
                dve.wait_ge(wT_in_psum, i + 1)
                dve.tensor_copy(wT[:, i, :, :].rearrange("p c n -> p (c n)"), ps[:, i, :]).then_inc(wT_ready, 1)
            dve.tensor_scalar(g_factor[:], cvals[:, 0, :], pvals[:, 1:2], 1.0, ALU.is_equal, ALU.add)
            link(dve.tensor_scalar(g_cut[:], cvals[:, 1, :], pvals[:, 2:3], 1.0, ALU.is_equal, ALU.subtract))
            link(dve.tensor_scalar(g_cut[:], g_cut[:], -CUT, None, ALU.mult))
            dve.wait_ge(vecT_ready, 1)
            dve.wait_ge(qg_in_psum, 1)
            for c in range(KC):
                last = dve.scalar_tensor_tensor(qg[:, c, :, :], ps[:, 6, c * P:(c + 1) * P].unsqueeze(1).broadcast_to([P, 2, P]),
                                                bq_col[:, c:c + 1], q_scale[:], ALU.add, ALU.mult)
            last.then_inc(qg_ready, 1)
            link(dve.tensor_scalar(is_glob[:], pvals[:, 3:4], 0.0, None, ALU.is_equal))
            link(dve.memset(zero_w[:], 1.0))
            link(dve.scalar_tensor_tensor(zero_w[:, 0:P:STRIDE], zero_w[:, 0:P:STRIDE], is_glob[:],
                                          zero_w[:, 0:P:STRIDE], ALU.subtract, ALU.mult))
            link(dve.tensor_scalar(neg_zero_w[:], zero_w[:], -1.0, None, ALU.mult))
            link(dve.tensor_scalar(cut_cols[:].rearrange("p h g -> p (h g)"), is_glob[:].broadcast_to([P, HPU * GPW]), CUT, None, ALU.mult))
            dve.tensor_copy(bv_wide[:], bv_col.unsqueeze(2).broadcast_to([P, KC, P]))
            for b in range(B):
                last = dve.tensor_scalar(wide(v_all[:, b * NV:(b + 1) * NV])[:, :, DH], is_glob[:].broadcast_to([P, HEADS]),
                                         float(-GLOBALS), float(S), ALU.mult, ALU.add)
            link(last)
            link(dve.tensor_copy(rank[:], rank_i[:]))
            consts_done = count[0]

            for u in range(UNITS):
                dve.wait_ge(gs_in_psum, u + 1)
                dve.tensor_tensor(keys(dg[:, u, :]), keys(ps[:, u, :]),
                                  g_factor[:].unsqueeze(1).unsqueeze(1).broadcast_to([P, KC, 2, P]), ALU.mult).then_inc(gs_scaled, 1)
                dve.wait_ge(gs_scaled, u + 1)
                dve.tensor_tensor(keys(dg[:, u, :]), keys(dg[:, u, :]),
                                  g_cut[:].unsqueeze(1).unsqueeze(1).broadcast_to([P, KC, 2, P]), ALU.add).then_inc(gs_cut, 1)
                dve.wait_ge(gs_cut, u + 1)
                dve.tensor_reduce(by_head(mg_raw[:])[:, u], keys(dg[:, u, :]), op=ALU.max, axis=AX.X).then_inc(gs_max, 1)
                dve.wait_ge(gs_max, 2 * u + 1)
                dve.tensor_scalar(by_head(g_row[:, NV:EXW])[:, u], by_head(mg_raw[:])[:, u], 0.0, None, ALU.max).then_inc(gs_max, 1)
                dve.wait_ge(gs_max, 2 * u + 2)
                dve.tensor_tensor(keys(dg[:, u, :]), keys(dg[:, u, :]),
                                  by_head(g_row[:, NV:EXW])[:, u].unsqueeze(3).broadcast_to([P, KC, 2, P]),
                                  ALU.subtract).then_inc(gs_shifted, 1)
            dve.wait_ge(gs_shifted, UNITS)
            dve.wait_ge(bias_in_psum, 1)
            dve.wait_ge(ld_bo, 16)
            dve.tensor_tensor(out_bias[:], ps[:, 4, 0:HID], bo_wide[:], ALU.add).then_inc(g_rows_ready, 1)
            dve.wait_ge(ld_w1, 16 * KC)
            dve.wait_ge(vecT_ready, 1)
            for c in range(KC):
                last = dve.tensor_tensor(w1s[:, c, :].rearrange("p (e h) -> p e h", h=EH), w1[:, c, :, :],
                                         vecT[:, c, EXPERTS:2 * EXPERTS].unsqueeze(2).broadcast_to([P, EXPERTS, EH]), ALU.mult)
            dve.wait_ge(b1_in_psum, 1)
            dve.wait_ge(ld_b, 48)
            for k in range(EPC):
                part = slice(k * EH, (k + 1) * EH)
                last = dve.tensor_tensor(b1s[part, :], ps[part, 6, k:EPC * FC:EPC], b1[part, :], ALU.add)
            dve.tensor_scalar(b2_sel[:, 0:1], pvals[:, 1:2], 1.5, None, ALU.is_le)
            dve.tensor_scalar(b2_sel[:, 2:3], pvals[:, 1:2], 3.5, None, ALU.is_ge)
            link(dve.tensor_copy(b2_h[:, 0, :], b2_f[:]))
            link(dve.tensor_tensor(b2_t[:, 0, :], b2_f[:], b2_h[:, 0, :], ALU.subtract))
            link(dve.tensor_copy(b2_h[:, 1, :], b2_t[:, 0, :]))
            link(dve.tensor_tensor(b2_t[:, 1, :], b2_t[:, 0, :], b2_h[:, 1, :], ALU.subtract))
            link(dve.tensor_tensor(b2_sel[:, 1:2], b2_sel[:, 0:1], b2_sel[:, 2:3], ALU.add))
            link(dve.tensor_scalar(b2_sel[:, 1:2], b2_sel[:, 1:2], -1.0, 1.0, ALU.mult, ALU.add))
            rs = slice(0, 3 * EXPERTS)
            link(dve.tensor_scalar(b2_t[:, 2, :], b2_t[:, 1, :], b2_sel[rs, 2:3], None, ALU.mult))
            link(dve.scalar_tensor_tensor(b2_t[:, 0, :], b2_h[:, 1, :], b2_sel[rs, 1:2], b2_t[:, 2, :], ALU.mult, ALU.add))
            dve.scalar_tensor_tensor(b2_stack[:], b2_h[:, 0, :], b2_sel[rs, 0:1], b2_t[:, 0, :], ALU.mult, ALU.add).then_inc(ffn_w_ready, 1)
            for b in range(B):
                dve.wait_ge(vall_in_psum, b + 1)
                dve.tensor_copy(wide(v_all[:, b * NV:(b + 1) * NV])[:, :, 0:DH],
                                ps[:, 2 + b, HID:2 * HID].rearrange("p (h e) -> p h e", e=DH)).then_inc(vall_ready, 1)
            dve.wait_ge(vall_ready, B)
            dve.wait_ge(table_ready, 16)

            def step(t, p, steady=False):
                nxt, cur, prev, pp = (live(t + k, steady) for k in (1, 0, -1, -2))

                def reduce(u):
                    dve.wait_ge(scores_in_psum, 4 * t + u + 1)
                    dve.tensor_reduce(by_head(row_max[:, p, :])[:, u], keys(ps_score[u % 2]), op=ALU.max,
                                      axis=AX.X).then_inc(max_ready, 1)

                def bound(u):
                    if u == 0:
                        need(dve, e_arg_ready, t - 1)
                    dve.wait_ge(max_ready, 4 * t + u + 1)
                    dve.tensor_tensor(by_head(guard[:, p, :])[:, u], by_head(row_max[:, p, :])[:, u],
                                      by_head(table[:, bass.ds(t * EXW + NV, HEADS)])[:, u], ALU.max).then_inc(guard_ready, 1)

                def shift(u):
                    need(dve, dT_in_psum, 4 * t + u - 3)
                    dve.wait_ge(guard_ready, 4 * t + u + 1)
                    dve.tensor_tensor(keys(shifted[:, u, :]), keys(ps_score[u % 2]),
                                      by_head(guard[:, p, :])[:, u].unsqueeze(3).broadcast_to([P, KC, 2, P]),
                                      ALU.subtract).then_inc(shifted_ready, 1)

                def queries(c):
                    dve.wait_ge(q_in_psum, t + 2)
                    return dve.scalar_tensor_tensor(qm[:, 1 - p, c, :, :],
                                                    ps_xq[:, HID + c * P:HID + (c + 1) * P].unsqueeze(1).broadcast_to([P, 2, P]),
                                                    bq_col[:, c:c + 1], q_scale[:], ALU.add, ALU.mult)

                if not steady and t == NW:
                    factors(0, EARLY)
                if cur:
                    reduce(0)
                    need(dve, num_ready, t - 1)
                    dve.wait_ge(r_in_psum, t + 1)
                    dve.tensor_tensor(rest[:, p, :], ps_rao[:, 0:NV], v_all[:, bass.ds(t // WPB * NV, NV)],
                                      ALU.add).then_inc(rest_ready, 1)
                    bound(0)
                if cur:
                    shift(0)
                    reduce(1)
                    bound(1)
                    shift(1)
                    reduce(2)
                if nxt:
                    queries(0)
                if cur:
                    bound(2)
                if nxt:
                    queries(1).then_inc(q_ready, 1)
                if cur:
                    shift(2)
                    reduce(3)
                if pp:
                    need(dve, kept[p], 16 * ((t - 2) // 2))
                    dve.wait_ge(o_in_psum, t - 1)
                    dve.wait_ge(biased_ready, t - 1)
                    dve.tensor_tensor(residual[:, p, :], ps_rao[:, 0:HID], biased[:, p, :], ALU.add).then_inc(residual_ready, 1)
                if cur:
                    bound(3)
                if pp:
                    dve.wait_ge(residual_ready, t - 1)
                    dve.bn_stats(bn6[:, 0, :], residual[:, p, :]).then_inc(bn_ready, 1)
                if cur:
                    shift(3)
                if prev:
                    need(dve, attn_ready, t - 2)
                    dve.wait_ge(sums_in_psum, t)
                    dve.wait_ge(rest_step, 3 * t)
                    if pp:
                        dve.wait_ge(bn_ready, t - 1)
                    sums = ps_pv.rearrange("p (u c a e) -> p c u a e", u=UNITS, c=KC, a=2)
                    for c in range(KC):
                        half = slice(c * NV // KC, (c + 1) * NV // KC)
                        view = num[:, 1 - p, half].rearrange("p (u a e) -> p u a e", u=UNITS, a=2)
                        last = dve.tensor_tensor(view, sums[:, c, :, :, 0:VA],
                                                 rest[:, 1 - p, half].rearrange("p (u a e) -> p u a e", u=UNITS, a=2), ALU.add)
                    last.then_inc(num_ready, 1)
                elif pp:
                    dve.wait_ge(bn_ready, t - 1)
                if pp:
                    dve.bn_aggr(mean_var[:, p, :], bn6[:, 0, :]).then_inc(stats_ready, 1)
                if prev:
                    if pp:
                        dve.wait_ge(stats_ready, t - 1)
                    dve.wait_ge(num_ready, t)
                    dve.reciprocal(rden[:, 1 - p, :], wide(num[:, 1 - p, :])[:, :, DH]).then_inc(rden_ready, 1)
                elif pp:
                    dve.wait_ge(stats_ready, t - 1)
                if pp:
                    dve.tensor_copy(row(stats, t - 2, 2), mean_var[:, p, :]).then_inc(moments_ready, 1)

            def rsqrt(x, y, t, signal, start):
                k = [0]

                def link(ins):
                    k[0] += 1
                    ins.then_inc(signal, 1)
                    dve.wait_ge(signal, start + k[0])

                link(dve.tensor_scalar(t.bitcast(i32), x.bitcast(i32), 1, None, ALU.logical_shift_right))
                link(dve.tensor_scalar(y.bitcast(i32), t.bitcast(i32), -1.0, RSQRT_SEED, ALU.mult, ALU.add))
                for _ in range(NEWTON):
                    link(dve.tensor_tensor(t, y, y, ALU.mult))
                    link(dve.tensor_tensor(t, t, x, ALU.mult))
                    link(dve.tensor_scalar(t, t, -0.5, 1.5, ALU.mult, ALU.add))
                    link(dve.tensor_tensor(y, y, t, ALU.mult))
                return start + k[0]

            ln_done = [0]

            def factors(first, end):
                part = slice(first, end)
                var = stats[:].rearrange("p (w s) -> p w s", s=2)[:, part, 1]

                def ln_link(ins):
                    ln_done[0] += 1
                    ins.then_inc(ln_step, 1)
                    dve.wait_ge(ln_step, ln_done[0])

                dve.wait_ge(moments_ready, end)
                ln_link(dve.tensor_scalar(nx[:, part], var, EPS, None, ALU.add))
                ln_done[0] = rsqrt(nx[:, part], rs1[:, part], nt[:, part], ln_step, ln_done[0])
                ln_link(dve.tensor_tensor(var1[:, part], rs1[:, part], rs1[:, part], ALU.mult))
                ln_link(dve.tensor_tensor(var1[:, part], var1[:, part], var, ALU.mult))
                ln_link(dve.tensor_scalar(var1[:, part], var1[:, part], EPS, None, ALU.add))
                ln_done[0] = rsqrt(var1[:, part], rs2[:, part], nt[:, part], ln_step, ln_done[0])
                dve.tensor_tensor(rs2[:, part], rs1[:, part], rs2[:, part], ALU.mult).then_inc(ln_ready, 1)

            attention_steps(dve, step)
            factors(EARLY, NW)
            for k in kept:
                dve.wait_ge(k, 16 * (NW // 2))

            def step(n, p, steady=False):
                nxt, cur, prev, pp = (live_group(n + k, steady) for k in (1, 0, -1, -2))
                y = yrs[:, p, :]

                def newton(k):
                    at = NEWTON_STEPS * (n - 2)
                    if k == 0:
                        dve.wait_ge(ystat_ready, n - 1)
                        last = dve.tensor_scalar(yvar[:], ystat[:, p, :, 1], EPS, None, ALU.add)
                    else:
                        dve.wait_ge(y_newton, at + k)
                    if k == 1:
                        last = dve.tensor_scalar(ytmp[:].bitcast(i32), yvar[:].bitcast(i32), 1, None, ALU.logical_shift_right)
                    if k == 2:
                        if not steady:
                            need(dve, yout_ready, n - 3)
                        last = dve.tensor_scalar(y.bitcast(i32), ytmp[:].bitcast(i32), -1.0, RSQRT_SEED, ALU.mult, ALU.add)
                    if k >= 3:
                        i = (k - 3) % 4
                        if i == 0:
                            last = dve.tensor_tensor(ytmp[:], y, y, ALU.mult)
                        if i == 1:
                            last = dve.tensor_tensor(ytmp[:], ytmp[:], yvar[:], ALU.mult)
                        if i == 2:
                            last = dve.tensor_scalar(ytmp[:], ytmp[:], -0.5, 1.5, ALU.mult, ALU.add)
                        if i == 3:
                            last = dve.tensor_tensor(y, y, ytmp[:], ALU.mult)
                    last.then_inc(yrs_ready if k == NEWTON_STEPS else y_newton, 1)

                def newtons(first, end):
                    if pp:
                        for k in range(first, end):
                            newton(k)

                def finish(j):
                    w = TG * (n - 1) + j
                    if j == 0:
                        need(dve, y_centred, n - 2)
                    dve.wait_ge(y_in_psum, w + 1)
                    dve.scalar_tensor_tensor(ysum[:, 1 - p, j, :], row(rows, w, HID), rs1[:, bass.ds(w, 1)],
                                             ps[:, 4 + j % 2, 0:HID], ALU.mult, ALU.add).then_inc(ysum_ready, 1)
                    newtons(4 * j, min(4 * j + 2, NEWTON_STEPS + 1))
                    dve.wait_ge(ysum_ready, w + 1)
                    dve.bn_stats(bn6[:, j, :], ysum[:, 1 - p, j, :]).then_inc(ybn_ready, 1)

                z = ps[:, 7, 0:TG * EXPERTS].rearrange("p (t e) -> p t e", e=EXPERTS)

                def route(k):
                    dve.wait_ge(z_in_psum, n + 2) if k == 0 else dve.wait_ge(route_step, 4 * (n + 1) + k)
                    if k == 0:
                        dve.tensor_reduce(zmax[:, 0, :], z, op=ALU.max, axis=AX.X).then_inc(route_step, 1)
                    if k == 1:
                        dve.tensor_tensor(hit[:], z, zmax[:, 0, :].unsqueeze(2).broadcast_to([P, TG, EXPERTS]),
                                          ALU.is_equal).then_inc(route_step, 1)
                    if k == 2:
                        dve.tensor_tensor(hit[:], hit[:], rank[:].unsqueeze(1).broadcast_to([P, TG, EXPERTS]),
                                          ALU.mult).then_inc(route_step, 1)
                    if k == 3:
                        dve.tensor_reduce(zmax[:, 1, :], hit[:], op=ALU.max, axis=AX.X).then_inc(route_step, 1)
                    if k == 4:
                        dve.tensor_tensor(onehot[:], hit[:].unsqueeze(2).broadcast_to([P, TG, 3, EXPERTS]),
                                          zmax[:, 1, :].unsqueeze(2).unsqueeze(2).broadcast_to([P, TG, 3, EXPERTS]),
                                          ALU.is_equal).then_inc(onehot_ready, 1)

                for c in range(FC):
                    if cur:
                        dve.wait_ge(h_ready, 4 * n + c + 1)
                        dve.wait_ge(mask_in_psum, 4 * n + c + 1)
                        need(dve, y_in_psum, 4 * (n - 1))
                        dve.tensor_tensor(hm[:, p, c, :], ps[:, 2 + c % 2, :], hT[:, c, :], ALU.mult).then_inc(hm_ready, 1)
                    if nxt and c == 2:
                        for k in range(5):
                            route(k)
                    if prev:
                        finish(c)
                    elif pp:
                        newtons(4 * c, min(4 * c + 2, NEWTON_STEPS + 1))
                    if prev and c == FC - 1:
                        dve.wait_ge(ybn_ready, 4 * n)
                    newtons(4 * c + 2, min(4 * c + 4, NEWTON_STEPS + 1))
                if prev:
                    for j in range(TG):
                        last = dve.bn_aggr(ystat[:, 1 - p, j, :], bn6[:, j, :])
                    last.then_inc(ystat_ready, 1)

            expert_steps(dve, step)

        @block.tensor
        def _(pe):
            mm = nc.tensor.matmul

            def product(out, lhsT, rhs):
                for c in range(KC):
                    last = mm(out, lhsT(c), rhs(c), start=(c == 0), stop=(c == KC - 1))
                return last

            pe.wait_ge(pool_const, 5)
            pe.wait_ge(ld_xg, 16)
            for c in range(KC):
                last = nc.tensor.transpose(ps[:, 5, c * P:(c + 1) * P], xg[:, c * P:(c + 1) * P], ident[:])
            last.then_inc(xgT_in_psum, 1)
            pe.wait_ge(ld_gate, 112)
            for c in range(KC):
                last = nc.tensor.transpose(ps[:, 4, c * NVEC:(c + 1) * NVEC],
                                           vec_rows[:, c * P:(c + 1) * P], ident[0:NVEC, 0:NVEC])
            last = nc.tensor.transpose(ps[:, 4, KC * NVEC:KC * NVEC + FC], b1_rows[:], ident[0:FC, 0:FC])
            last.then_inc(vecT_in_psum, 1)
            pe.wait_ge(ld_w, 64)
            for i in range(4):
                for oc in range(KC):
                    for ic in range(KC):
                        last = nc.tensor.transpose(ps[:, i, ic * HID + oc * P:ic * HID + (oc + 1) * P],
                                                   w_raw[:, i, oc, ic * P:(ic + 1) * P], ident[:])
                last.then_inc(wT_in_psum, 1)
            pe.wait_ge(xgT_ready, 1)
            pe.wait_ge(wT_ready, 4)
            for o in range(KC):
                last = product(ps[:, 6, o * P:(o + 1) * P], lambda c: wT[:, WQ, c, o * P:(o + 1) * P], lambda c: xgT[:, c, :])
            last.then_inc(qg_in_psum, 1)
            for o in range(KC):
                product(ps[:, 7, o * P:(o + 1) * P], lambda c: wT[:, WK, c, o * P:(o + 1) * P], lambda c: xgT[:, c, :])
            product(ps[:, 7, HID:2 * HID], lambda c: xgT[:, c, :], lambda c: wT[:, WV, c, :]).then_inc(kvg_in_psum, 1)
            pe.wait_ge(qg_ready, 1)
            pe.wait_ge(kvg_ready, 1)
            for u in range(UNITS):
                for i, (c, a, _) in enumerate(heads_of(u)):
                    last = mm(ps[:, u, i * P:(i + 1) * P], qg[quad(u), c, a, :], kg[quad(u), c, :], start=True, stop=True)
                last.then_inc(gs_in_psum, 1)
            pe.wait_ge(vecT_ready, 1)
            pe.wait_ge(dve_const, 12)
            product(ps[:, 4, 0:HID], lambda c: bv_wide[:, c, :], lambda c: wT[:, WO, c, :]).then_inc(bias_in_psum, 1)
            pe.wait_ge(ld_w1, 16 * KC)
            for f in range(FC):
                last = product(ps[:, 6, f * EPC:(f + 1) * EPC],
                               lambda c: w1[:, c, f * EPC:(f + 1) * EPC, :].rearrange("p e h -> p (e h)"),
                               lambda c: vecT[:, c, 2 * EXPERTS + f * EPC:2 * EXPERTS + (f + 1) * EPC])
            last.then_inc(b1_in_psum, 1)
            for u in range(UNITS):
                pe.wait_ge(gs_shifted, u + 1)
                for i in range(HPU):
                    last = nc.tensor.transpose(ps[:, u, i * P:(i + 1) * P], dg[:, u, i * P:(i + 1) * P], ident[:])
                last.then_inc(gT_in_psum, 1)
            pe.wait_ge(kvg_ready, 2)
            for u in range(UNITS):
                pe.wait_ge(g_probs, u + 1)
                for i, (_, _, h) in enumerate(heads_of(u)):
                    last = mm(ps[:, 5, h * VA:(h + 1) * VA], pg[:, u, i * P:(i + 1) * P], vg[:, h * VA:(h + 1) * VA],
                              start=True, stop=True)
            last.then_inc(g_pv, 1)
            for b in range(B):
                pe.wait_ge(pool_step, 4 * (b + 1))
                for c in range(KC):
                    last = mm(ps[:, 2 + b, c * P:(c + 1) * P], xsum[:, b, c * P:(c + 1) * P], zero_w[:], start=True, stop=True)
                last.then_inc(xsumT_in_psum, 1)
            for b in range(B):
                pe.wait_ge(xsumT_ready, b + 1)
                product(ps[:, 2 + b, HID:2 * HID], lambda c: xsumT[:, b, c, :], lambda c: wT[:, WV, c, :]).then_inc(vall_in_psum, 1)
            pe.wait_ge(vall_ready, B)
            pe.wait_ge(g_rows_ready, 2)

            def step(t, p, steady=False):
                nxt, cur, prev, pp = (live(t + k, steady) for k in (1, 0, -1, -2))

                def scores(u):
                    g = 4 * t + u
                    if u == 0:
                        pe.wait_ge(q_ready, t + 1)
                        pe.wait_ge(k_ready, t + 1)
                    need(pe, shifted_ready, g - 1)
                    for i, (c, a, _) in enumerate(heads_of(u)):
                        last = mm(ps_score[u % 2][:, i * P:(i + 1) * P], qm[quad(u), p, c, a, :], kT[quad(u), p, c, :],
                                  start=True, stop=True)
                    last.then_inc(scores_in_psum, 1)

                def turn(w, u):
                    g = 4 * w + u
                    need(pe, probs_ready, g - 1)
                    pe.wait_ge(cut_ready, g + 1)
                    for i in range(HPU):
                        last = nc.tensor.transpose(ps_dT[u % 2][:, i * P:(i + 1) * P], shifted[:, u, i * P:(i + 1) * P], ident[:])
                    last.then_inc(dT_in_psum, 1)

                def weigh(w, u, pw):
                    pe.wait_ge(probs_ready, 4 * w + u + 1)
                    if u == 0:
                        need(pe, num_ready, w)
                    for i, (_, _, h) in enumerate(heads_of(u)):
                        last = mm(ps_pv[quad(i), u * P:(u + 1) * P], va[:, pw, h * VP:(h + 1) * VP],
                                  probs[:, u, i * P:(i + 1) * P], start=True, stop=True, tile_position=(0, 32 * i))
                    last.then_inc(pv_in_psum, 1)

                if cur:
                    scores(0)
                if prev:
                    turn(t - 1, 2)
                    weigh(t - 1, 0, 1 - p)
                if nxt:
                    need(pe, q_ready, t + 1)
                    pe.wait_ge(xs_ready[1 - p], 16 * ((t + 1) // 2 + 1))
                    for c in range(KC):
                        last = nc.tensor.transpose(ps_xq[:, c * P:(c + 1) * P], xs[:, 1 - p, c * P:(c + 1) * P], ident[:])
                    last.then_inc(xT_in_psum, 1)
                if cur:
                    scores(1)
                if prev:
                    turn(t - 1, 3)
                    weigh(t - 1, 1, 1 - p)
                if pp:
                    if cur:
                        pe.wait_ge(rest_ready, t + 1)
                    pe.wait_ge(attn_ready, t - 1)
                    for c in range(KC):
                        last = nc.tensor.transpose(ps_rao[:, c * P:(c + 1) * P], attn[:, p, c * P:(c + 1) * P], ident[:])
                    last.then_inc(aT_in_psum, 1)
                if nxt:
                    pe.wait_ge(xT_ready, t + 2)
                    for o in range(KC):
                        last = product(ps_xq[:, HID + o * P:HID + (o + 1) * P], lambda c: wT[:, WQ, c, o * P:(o + 1) * P],
                                       lambda c: xT[:, 1 - p, c, :])
                    last.then_inc(q_in_psum, 1)
                    need(pe, v_ready, t + 1)
                    for o in range(KC):
                        product(ps_kv[:, o * P:(o + 1) * P], lambda c: wT[:, WK, c, o * P:(o + 1) * P],
                                lambda c: xT[:, 1 - p, c, :])
                    product(ps_kv[:, HID:2 * HID], lambda c: xT[:, 1 - p, c, :], lambda c: wT[:, WV, c, :]).then_inc(kv_in_psum, 1)
                if cur:
                    scores(2)
                    turn(t, 0)
                if prev:
                    weigh(t - 1, 2, 1 - p)
                    weigh(t - 1, 3, 1 - p)
                if pp:
                    pe.wait_ge(aT_ready, t - 1)
                    product(ps_rao[:, 0:HID], lambda c: aT[:, p, c, :], lambda c: wT[:, WO, c, :]).then_inc(o_in_psum, 1)
                if cur:
                    scores(3)
                    turn(t, 1)
                if prev:
                    pe.wait_ge(pvT_ready, t)
                    for i in range(UNITS):
                        last = nc.tensor.transpose(ps_pv[:, i * P:(i + 1) * P], pvT[:, i * P:(i + 1) * P], ident[:])
                    last.then_inc(sums_in_psum, 1)
                if nxt:
                    need(pe, residual_ready, t - 1)
                    pe.wait_ge(v_ready, t + 2)
                    mm(ps_rao[:, 0:NV], neg_zero_w[:], padded(va[:, 1 - p, :])[:, :, 0:VA], start=True, stop=True).then_inc(r_in_psum, 1)

            attention_steps(pe, step)
            pe.wait_ge(ffn_w_ready, 1)
            pe.wait_ge(residual_ready, NW)
            pe.wait_ge(ld_w2, 16)

            def step(n, p, steady=False):
                nxt, cur, prev = (live_group(n + k, steady) for k in (1, 0, -1))
                for c in range(FC):
                    if cur:
                        if c == 0:
                            pe.wait_ge(xhT_ready, 2 * n + 2)
                        need(pe, h_ready, 4 * n + c - 1)
                        product(ps[:, c % 2, :], lambda k: w1s[:, k, c * P:(c + 1) * P], lambda k: xhT[:, p, k, :]).then_inc(h_in_psum, 1)
                        if c == 0:
                            pe.wait_ge(ohT_ready, n + 1)
                        need(pe, hm_ready, 4 * n + c - 1)
                        mm(ps[:, 2 + c % 2, :], pick[:, c, :], ohT[:, p, :], start=True, stop=True).then_inc(mask_in_psum, 1)
                    if nxt and c < 2:
                        g = 2 * (n + 1) + c
                        need(pe, xhT_ready, g)
                        pe.wait_ge(xh_ready, 2 * g + 2)
                        for j in range(2):
                            for k in range(KC):
                                last = nc.tensor.transpose(ps[:, 6, (j * KC + k) * P:(j * KC + k + 1) * P],
                                                           xh[:, 2 * c + j, k * P:(k + 1) * P], ident[:])
                        last.then_inc(xhT_in_psum, 1)
                    if nxt and c == 3:
                        pe.wait_ge(onehot_ready, n + 2)
                        for j in range(TG):
                            last = nc.tensor.transpose(ps[0:3 * EXPERTS, 7, 64 + j * P // 2:64 + (j + 1) * P // 2].bitcast(bf16),
                                                       onehot[:, j, :, :].rearrange("p r e -> p (r e)"), ident_b[:])
                        last.then_inc(ohT_in_psum, 1)
                    if nxt and c == 2:
                        pe.wait_ge(xhT_ready, 2 * n + 4)
                        need(pe, ohT_ready, n + 1)
                        for j in range(TG):
                            last = product(ps[:, 7, j * EXPERTS:(j + 1) * EXPERTS],
                                           lambda k: xhT[:, 1 - p, k, j * P:(j + 1) * P], lambda k: vecT[:, k, 0:EXPERTS])
                        last.then_inc(z_in_psum, 1)
                    if prev:
                        w = TG * (n - 1) + c
                        if c == 0:
                            pe.wait_ge(hm_ready, 4 * n)
                        need(pe, ysum_ready, w - 1)
                        y = ps[:, 4 + c % 2, 0:HID]
                        for f in range(FC):
                            mm(y, hm[:, 1 - p, f, c * P:(c + 1) * P], w2[:, f, :], start=(f == 0), stop=False)
                        mm(y, ohT[:, 1 - p, c * P:(c + 1) * P], b2_stack[:], start=False, stop=True).then_inc(y_in_psum, 1)

            expert_steps(pe, step)


_INS = ['L0_attn_x', 'L0_attn_wq', 'L0_attn_bq', 'L0_attn_wk', 'L0_attn_bk', 'L0_attn_wv', 'L0_attn_bv',
        'L0_attn_wo', 'L0_attn_bo', 'L0_ffn_Wg', 'L0_ffn_ln_scale', 'L0_ffn_ln_bias', 'L0_ffn_W1', 'L0_ffn_b1',
        'L0_ffn_W2', 'L0_ffn_b2']
_OUTS = [((2, 2048, 256), 'float32')]


def kernel(**inputs):
    import numpy as _np
    import concourse.bacc as _bacc
    from concourse import mybir as _mybir
    from concourse.bass_utils import run_bass_kernel_spmd as _run

    nc = _bacc.Bacc("TRN2", target_bir_lowering=False, num_devices=1)
    arrays, args = {}, []
    for name in _INS:
        a = _np.ascontiguousarray(inputs[name])
        arrays[f"in_{name}_dram"] = a
        args.append(nc.dram_tensor(f"in_{name}_dram", a.shape, _mybir.dt.from_np(a.dtype), kind="ExternalInput").ap())
    for i, (shape, dtype) in enumerate(_OUTS):
        dt = _mybir.dt.from_np(_np.dtype(dtype))
        args.append(nc.dram_tensor(f"out_{i}_dram", shape, dt, kind="ExternalOutput").ap())
    windowed_attention_then_top1_experts(nc, *args)
    r = _run(nc, [arrays], core_ids=[0])
    got = tuple(r.results[0][f"out_{i}_dram"] for i in range(len(_OUTS)))
    return got[0]
```

```python
import concourse.bass as bass
from concourse import mybir
from contextlib import ExitStack


def windowed_attention_then_top1_experts(
    nc: bass.Bass,
    x_dram: bass.AP,
    wq_dram: bass.AP,
    bq_dram: bass.AP,
    wk_dram: bass.AP,
    bk_dram: bass.AP,
    wv_dram: bass.AP,
    bv_dram: bass.AP,
    wo_dram: bass.AP,
    bo_dram: bass.AP,
    wg_dram: bass.AP,
    ln_scale_dram: bass.AP,
    ln_bias_dram: bass.AP,
    w1_dram: bass.AP,
    b1_dram: bass.AP,
    w2_dram: bass.AP,
    b2_dram: bass.AP,
    out_dram: bass.AP,
):
    fp32 = mybir.dt.float32
    bf16 = mybir.dt.bfloat16
    i32 = mybir.dt.int32
    fp32r = mybir.dt.float32r
    ALU = mybir.AluOpType
    ACT = mybir.ActivationFunctionType
    AX = mybir.AxisListType

    P = 128
    B, S, HID = x_dram.shape
    HEADS = 16
    DH = HID // HEADS
    WINDOW = 128
    GLOBALS = 64
    STRIDE = S // GLOBALS
    GPW = WINDOW // STRIDE
    NW = B * S // WINDOW
    WPB = S // WINDOW
    KC = HID // P
    QUADS = 4
    UNITS = 4
    HPU = HEADS // UNITS
    VP = 32
    VA = DH + 1
    NV = HEADS * VA
    EXW = NV + HEADS
    SCALE = float(DH) ** -0.5
    CUT = -1.0e30
    EXPERTS, _, EH = w1_dram.shape
    FC = EXPERTS * EH // P
    EPC = P // EH
    EPS = 1e-5
    TG = 4
    NG = NW // TG
    NVEC = 3 * EXPERTS + 3
    GT = TG * P
    RSQRT_SEED = float(0x5F3759DF)
    NEWTON = 3
    NEWTON_STEPS = 2 + 3 * NEWTON
    FACTOR_STEPS = 5 + 2 * NEWTON_STEPS

    ctx = ExitStack()
    with ctx:
        def sb(name, shape, dt=fp32):
            return ctx.enter_context(nc.sbuf_tensor(name, shape, dt))

        def sem(name):
            return ctx.enter_context(nc.semaphore(name))

        with ExitStack() as first:
            def early_sb(name, shape, dt=fp32):
                return first.enter_context(nc.sbuf_tensor(name, shape, dt))

            w_raw = early_sb("w_raw", [P, 4, KC, HID])
            shifted = early_sb("shifted", [P, UNITS, HPU * P])
            probs = early_sb("probs", [P, UNITS, HPU * P])
            xg = early_sb("xg", [P, HID])
            xgT = early_sb("xgT", [P, KC, P])
            cid = early_sb("cid", [P, P], i32)
            cbits = early_sb("cbits", [P, P], i32)
            cvals = early_sb("cvals", [P, P])
        w1_part = [sb(f"w1_part{i}", [P, KC, EXPERTS * EH], fp32r) for i in range(2)]
        xh_part = [sb(f"xh_part{i}", [P, 2, KC, GT], fp32r) for i in range(2)]
        a_part = [sb(f"a_part{i}", [P, KC, P], fp32r) for i in range(2)]
        x_part = [sb(f"x_part{i}", [P, KC, P], fp32r) for i in range(2)]
        wv_part = [sb(f"wv_part{i}", [P, KC, HID], fp32r) for i in range(2)]
        wo_part = [sb(f"wo_part{i}", [P, KC, HID], fp32r) for i in range(2)]
        rows = sb("rows", [P, NW * HID])
        wT = sb("wT", [P, 4, KC, HID])
        bv_wide = sb("bv_wide", [P, KC, P])
        out_bias = sb("out_bias", [P, HID])
        ident = sb("ident", [P, P])
        ident_b = sb("ident_b", [P, P], bf16)
        pid = sb("pid", [P, 1], i32)
        pbits = sb("pbits", [P, 4], i32)
        pvals = sb("pvals", [P, 4])
        is_glob = sb("is_glob", [P, 1])
        q_scale = sb("q_scale", [P, 2, P])
        zero_w = sb("zero_w", [P, P])
        neg_zero_w = sb("neg_zero_w", [P, P])
        cut_cols = sb("cut_cols", [P, HPU, GPW])
        zeros16 = sb("zeros16", [P, HEADS])
        g_factor = sb("g_factor", [P, P])
        mg_raw = sb("mg_raw", [P, HEADS])
        g_row = sb("g_row", [P, EXW])
        xsum = sb("xsum", [P, B, WPB // 2 * HID])
        xsumT = sb("xsumT", [P, B, KC, P])
        v_all = sb("v_all", [P, B * NV])

        with ExitStack() as attention_only:
            xs = attention_only.enter_context(nc.sbuf_tensor("xs", [P, 2, HID], fp32))
            xT = attention_only.enter_context(nc.sbuf_tensor("xT", [P, 2, KC, P], fp32))
            table = attention_only.enter_context(nc.sbuf_tensor("table", [P, NW * EXW], fp32))
            q_part = [attention_only.enter_context(nc.sbuf_tensor(f"q_part{i}", [P, 2, KC, 2, P], fp32r)) for i in range(2)]
            k_part = [attention_only.enter_context(nc.sbuf_tensor(f"k_part{i}", [P, 2, KC, QUADS, P], fp32r)) for i in range(2)]
        w2 = sb("w2", [P, FC, HID])
        hm_part = [sb(f"hm_part{i}", [P, 2, FC, GT], fp32r) for i in range(2)]
        ysum = sb("ysum", [P, 2, TG, HID])
        yout = sb("yout", [P, 2, TG, HID])
        w2_part = [sb(f"w2_part{i}", [P, FC, HID], fp32r) for i in range(2)]
        ohT = sb("ohT", [3 * EXPERTS, 2, GT], bf16)
        sb("rest_of_k_part", [P, 2 * HID])
        qf = sb("qf", [P, KC, 2, P])
        kf = sb("kf", [P, KC, P])
        va = sb("va", [P, 2, HEADS * VP])
        pvT = sb("pvT_t", [P, 512])
        row_max = sb("row_max_t", [P, 2, HEADS])
        guard = sb("guard_t", [P, 2, HEADS])
        dg, pg, vg = shifted, probs, va[:, 1, :]
        e_arg = sb("e_arg_t", [P, 2, 2 * HEADS])
        e_val = sb("e_val_t", [P, 2, 2 * HEADS])
        rest = sb("rest_t", [P, 2, NV])
        gl = sb("gl_t", [P, NV])
        num = sb("num_t", [P, 2, NV])
        rden = sb("rden_t", [P, 2, HEADS])
        attn = sb("attn_t", [P, 2, HID])
        aT = sb("aT_t", [P, 2, KC, P])
        biased = sb("biased_t", [P, 2, HID])
        residual = sb("residual_t", [P, 2, HID])
        bn6 = sb("bn6", [P, TG, 6])
        mean_var = sb("mean_var", [P, 2, 2])
        stats = sb("stats_t", [P, NW * 2])

        rs1 = sb("rs1", [P, NW])
        var1 = sb("var1", [P, NW])
        rs2 = sb("rs2", [P, NW])
        nt = sb("newton_t", [P, NW])
        nx = sb("newton_x", [P, NW])

        vec_rows = sb("vec_rows", [NVEC, HID])
        vecT = sb("vecT", [P, KC, NVEC])
        bq_col, bk_col, bv_col = (vecT[:, :, 3 * EXPERTS + i] for i in range(3))
        b1_rows = sb("b1_rows", [FC, P])
        w1 = sb("w1", [P, KC, EXPERTS, EH])
        b1 = sb("b1", [P, FC])
        b1s = sb("b1s", [P, FC])
        b2_f = attn[0:3 * EXPERTS, 0, :]
        b2_h = sb("b2_h", [3 * EXPERTS, 2, HID], bf16)
        b2_sel = sb("b2_sel", [P, 3])
        b2_t = [residual[0:3 * EXPERTS, 0, :], residual[0:3 * EXPERTS, 1, :], biased[0:3 * EXPERTS, 0, :]]
        b2_stack = sb("b2_stack", [3 * EXPERTS, HID], bf16)
        pick = sb("pick", [3 * EXPERTS, FC, P], bf16)
        rank = sb("rank", [P, EXPERTS])
        rank_i = sb("rank_i", [P, EXPERTS], i32)
        xh = sb("xh", [P, TG, HID])
        w1s = xh[:].rearrange("p t n -> p (t n)").rearrange("p (c n) -> p c n", c=KC)
        xhT = xsum[:, 0, :].rearrange("p (b c n) -> p b c n", b=2, c=KC)
        gate = sb("gate", [P, KC, VP])
        zT = sb("zT", [P, P])
        zmax = sb("zmax", [P, 2, TG])
        hit = sb("hit", [P, TG, EXPERTS])
        onehot = sb("onehot", [P, TG, 3, EXPERTS], bf16)
        hT = xsum[:, 1, :].rearrange("p (f n) -> p f n", f=FC)
        ystat = sb("ystat", [P, 2, TG, 2])
        yrs = sb("yrs", [P, 2, TG])
        yvar = sb("yvar", [P, TG])
        ytmp = sb("ytmp", [P, TG])

        scratch = nc.dram_tensor("global_sums", (P, EXW), fp32, kind="Internal").ap()

        ps = ctx.enter_context(nc.psum_tensor("ps", [P, 8, 512], fp32))
        ps_score = [ps[:, 0, :], ps[:, 1, :]]
        ps_dT = [ps[:, 2, :], ps[:, 3, :]]
        ps_xq = ps[:, 4, :]
        ps_kv = ps[:, 5, :]
        ps_rao = ps[:, 6, :]
        ps_pv = ps[:, 7, :]

        def batch_bank(b):
            return ps_dT[0] if b == 0 else ps_pv

        def group_banks(n):
            return (ps[:, 0, :], ps[:, 1, :], ps[:, 4, :]) if isinstance(n, int) and n == 0 else (ps[:, 6, :], ps[:, 6, :], ps[:, 7, :])

        def quad(u):
            return slice(32 * u, 32 * u + 32)

        def by_head(ap, u):
            return ap.rearrange("p (c q a) -> p c a q", c=KC, q=QUADS)[:, u // 2, u % 2]

        def heads_of(u):
            return [8 * (u // 2) + 2 * q + u % 2 for q in range(QUADS)]

        def keys(ap):
            return ap.rearrange("p (i j) -> p i j", j=P)

        def wide(ap):
            return ap.rearrange("p (h e) -> p h e", e=VA)

        def padded(ap):
            return ap.rearrange("p (h e) -> p h e", e=VP)

        def row(ap, w, width):
            return ap[:, bass.ds(w * width, width)]

        def need(eng, s, count):
            if not isinstance(count, int) or count > 0:
                eng.wait_ge(s, count)

        ld_xg, ld_bo, ld_gate, ld_w1, ld_w2, ld_b = (
            sem(n) for n in ("ld_xg", "ld_bo", "ld_gate", "ld_w1", "ld_w2", "ld_b"))
        ld_w = [sem(f"ld_proj{i}") for i in range(4)]
        ld_x = [sem(f"ld_x{i}") for i in range(8)]
        pool_const = sem("pool_const")
        dve_const = sem("dve_const")
        consts_ready = sem("consts_ready")
        table_zero = sem("table_zero")
        wT_in_psum = sem("wT_in_psum")
        wqk_ready = sem("wqk_ready")
        wvo_ready = sem("wvo_ready")
        wvo_high_ready = sem("wvo_high_ready")
        wvo_low_ready = sem("wvo_low_ready")
        vecT_in_psum = sem("vecT_in_psum")
        vecT_ready = sem("vecT_ready")
        xgT_in_psum = sem("xgT_in_psum")
        xgT_ready = sem("xgT_ready")
        qg_in_psum = sem("qg_in_psum")
        kg_in_psum = sem("kg_in_psum")
        vg_in_psum = sem("vg_in_psum")
        qgf_ready, qg_high_ready, qg_ready = (sem(n) for n in ("qgf_ready", "qg_high_ready", "qg_ready"))
        kgf_ready, kg_high_ready, kg_ready = (sem(n) for n in ("kgf_ready", "kg_high_ready", "kg_ready"))
        vg_ready = sem("vg_ready")
        k_zero = [sem("k_zero0"), sem("k_zero1")]
        bias_in_psum = sem("bias_in_psum")
        out_bias_ready = sem("out_bias_ready")
        b1_in_psum = sem("b1_in_psum")
        gs_in_psum = sem("gs_in_psum")
        gs_scaled = sem("gs_scaled")
        gs_max = sem("gs_max")
        gs_shifted = sem("gs_shifted")
        gT_in_psum = sem("gT_in_psum")
        g_probs = sem("g_probs")
        g_pv = sem("g_pv")
        g_pvT_ready = sem("g_pvT_ready")
        g_sums_in_psum = sem("g_sums_in_psum")
        g_sums_ready = sem("g_sums_ready")
        g_stored = sem("g_stored")
        guards_in_table = sem("guards_in_table")
        sums_in_table = sem("sums_in_table")
        pool_step = sem("pool_step")
        xsumT_in_psum = sem("xsumT_in_psum")
        xsumT_ready = sem("xsumT_ready")
        vall_in_psum = sem("vall_in_psum")
        vall_ready = sem("vall_ready")
        ffn_w_ready = sem("ffn_w_ready")
        xs_ready = [sem("xs_ready0"), sem("xs_ready1")]
        xT_in_psum = sem("xT_in_psum")
        xT_ready = sem("xT_ready")
        x_high_ready = sem("x_high_ready")
        x_low_ready = sem("x_low_ready")
        q_in_psum = sem("q_in_psum")
        qf_ready = sem("qf_ready")
        q_high_ready = sem("q_high_ready")
        q_ready = sem("q_ready")
        k_in_psum = sem("k_in_psum")
        v_in_psum = sem("v_in_psum")
        kf_ready = sem("kf_ready")
        k_high_ready = sem("k_high_ready")
        k_ready = sem("k_ready")
        v_ready = sem("v_ready")
        scores_in_psum = sem("scores_in_psum")
        max_ready = sem("max_ready")
        guard_ready = sem("guard_ready")
        shifted_ready = sem("shifted_ready")
        cut_ready = sem("cut_ready")
        dT_in_psum = sem("dT_in_psum")
        probs_ready = sem("probs_ready")
        pv_in_psum = sem("pv_in_psum")
        pvT_ready = sem("pvT_ready")
        sums_in_psum = sem("sums_in_psum")
        r_in_psum = sem("r_in_psum")
        rest_ready = sem("rest_ready")
        e_arg_ready = sem("e_arg_ready")
        e_ready = sem("e_ready")
        rest_step = sem("rest_step")
        num_ready = sem("num_ready")
        rden_ready = sem("rden_ready")
        attn_ready = sem("attn_ready")
        aT_in_psum = sem("aT_in_psum")
        aT_ready = sem("aT_ready")
        a_high_ready = sem("a_high_ready")
        a_low_ready = sem("a_low_ready")
        o_in_psum = sem("o_in_psum")
        biased_ready = sem("biased_ready")
        residual_ready = sem("residual_ready")
        bn_ready = sem("bn_ready")
        stats_ready = sem("stats_ready")
        moments_ready = sem("moments_ready")
        centred = sem("centred")
        kept = [sem("kept0"), sem("kept1")]
        ln_step = sem("ln_step")
        ln_ready = sem("ln_ready")
        xh_ready = sem("xh_ready")
        xhT_in_psum = sem("xhT_in_psum")
        xhT_ready = sem("xhT_ready")
        high_ready = sem("high_ready")
        low_ready = sem("low_ready")
        zT_in_psum = sem("zT_in_psum")
        zT_ready = sem("zT_ready")
        z_in_psum = sem("z_in_psum")
        route_step = sem("route_step")
        onehot_ready = sem("onehot_ready")
        ohT_in_psum = sem("ohT_in_psum")
        ohT_ready = sem("ohT_ready")
        h_in_psum = sem("h_in_psum")
        mask_in_psum = sem("mask_in_psum")
        h_ready = sem("h_ready")
        hm_ready = sem("hm_ready")
        hm_high_ready = sem("hm_high_ready")
        hm_low_ready = [sem("hm_low_ready0"), sem("hm_low_ready1")]
        w2_high_ready = sem("w2_high_ready")
        w2_low_ready = sem("w2_low_ready")
        y_in_psum = sem("y_in_psum")
        ysum_ready = sem("ysum_ready")
        ybn_ready = sem("ybn_ready")
        ystat_ready = sem("ystat_ready")
        y_newton = sem("y_newton")
        yrs_ready = sem("yrs_ready")
        y_centred = sem("y_centred")
        yout_ready = sem("yout_ready")
        last_out_ready = sem("last_out_ready")
        stored = [sem("stored0"), sem("stored1")]

        WQ, WK, WV, WO = range(4)
        x_w = x_dram.rearrange("b (w p) d -> p (b w) d", p=P)
        block = ctx.enter_context(nc.Block())

        LOOP_A = (3, NW - 5)
        EARLY = NW - 2 * TG

        def attention_steps(eng, step, first):
            for t in range(first, LOOP_A[0]):
                step(t, t % 2)
            with eng.Fori(LOOP_A[0], LOOP_A[1] - 1, 2) as t:
                for k in range(2):
                    step(t + k, (LOOP_A[0] + k) % 2, steady=True)
            for t in range(LOOP_A[1], NW + 2):
                step(t, t % 2)

        def live(w, steady):
            return steady or 0 <= w < NW

        LOOP_B = (2, NG - 2)

        def expert_steps(eng, step):
            for n in range(LOOP_B[0]):
                step(n, n % 2)
            with eng.Fori(LOOP_B[0], LOOP_B[1] - 1, 2) as n:
                for k in range(2):
                    step(n + k, (LOOP_B[0] + k) % 2, steady=True)
            for n in range(LOOP_B[1], NG + 2):
                step(n, n % 2)

        def live_group(n, steady):
            return steady or 0 <= n < NG

        @block.sync
        def _(sp):
            sp.dma_start(xg[:], x_dram.rearrange("b (g s) d -> (b g) s d", s=STRIDE)[:, 0, :]).then_inc(ld_xg, 16)
            for i, w in enumerate((wq_dram, wk_dram, wv_dram, wo_dram)):
                sp.dma_start(w_raw[:, i, :, :], w.rearrange("(c p) n -> p c n", p=P)).then_inc(ld_w[i], 16)

            def step(t, p, steady=False):
                if live(t + 2, steady):
                    need(sp, xT_in_psum, t + 1)
                    sp.dma_start(xs[:, p, :], x_w[:, bass.ds(t + 2, 1), :]).then_inc(xs_ready[p], 16)
                if not steady and t == NW - 1:
                    sp.wait_ge(v_in_psum, NW)
                    sp.wait_ge(x_low_ready, NW)
                    sp.dma_start(w2[:], w2_dram.rearrange("(c e) h d -> (e h) c d", e=EPC)).then_inc(ld_w2, 16)
                if live(t - 3, steady):
                    sp.wait_ge(centred, t - 2)
                    sp.dma_start(row(rows, t - 3, HID), residual[:, 1 - p, :]).then_inc(kept[1 - p], 16)

            for t in (-2, -1):
                step(t, t % 2)
            rows_v = rows[:].rearrange("p (w d) -> p w d", d=HID)
            for i in range(8):
                k = NW // 8
                sp.dma_start(rows_v[:, i * k:(i + 1) * k, :], x_w[:, i * k:(i + 1) * k, :]).then_inc(ld_x[i], 16)
                if i == 3:
                    sp.dma_start(out_bias[:], bo_dram.rearrange("(a n) -> a n", a=1).broadcast_to([P, HID])).then_inc(ld_bo, 16)
                    for k in range(3):
                        sp.dma_start(b2_f[EXPERTS * k:EXPERTS * (k + 1), :], b2_dram).then_inc(ld_b, 16)
                    for c in range(KC):
                        sp.dma_start(w1[:, c, :, :], w1_dram[:, c * P:(c + 1) * P, :].rearrange("e p h -> p e h")).then_inc(ld_w1, 16)
            to_table = table[0:P:STRIDE, :].rearrange("a (w c) -> a w c", c=EXW)
            by_window = scratch.rearrange("(w a) c -> a w c", a=GPW)
            sp.wait_ge(gs_max, 2 * UNITS)
            sp.dma_start(scratch[:, NV:EXW], g_row[:, NV:EXW]).then_inc(g_stored, 16)
            sp.wait_ge(g_stored, 16)
            sp.wait_ge(table_zero, 1)
            sp.dma_start(to_table[:, :, NV:EXW], by_window[:, :, NV:EXW]).then_inc(guards_in_table, 16)
            sp.wait_ge(g_sums_ready, 1)
            sp.dma_start(scratch[:, 0:NV], g_row[:, 0:NV]).then_inc(g_stored, 16)
            sp.wait_ge(g_stored, 32)
            sp.dma_start(to_table[:, :, 0:NV], by_window[:, :, 0:NV]).then_inc(sums_in_table, 16)
            attention_steps(sp, step, first=0)
            sp.wait_ge(centred, NW)
            sp.dma_start(row(rows, NW - 1, HID), residual[:, (NW - 1) % 2, :]).then_inc(kept[(NW - 1) % 2], 16)

            def step(n, p, steady=False):
                out_t = out_dram.rearrange("b (w p) d -> p (b w) d", p=P)
                if not steady and n == NG + 1:
                    for j in range(2):
                        half = slice(j * TG // 2, (j + 1) * TG // 2)
                        sp.wait_ge(last_out_ready, j + 1)
                        sp.dma_start(out_t[:, (n - 2) * TG:(n - 1) * TG, :][:, half, :], yout[:, p, half, :]).then_inc(stored[p], 16)
                elif live_group(n - 2, steady):
                    sp.wait_ge(yout_ready, n - 1)
                    sp.dma_start(out_t[:, bass.ds((n - 2) * TG, TG), :], yout[:, p, :, :]).then_inc(stored[p], 16)
            expert_steps(sp, step)
            sp.wait_ge(stored[0], 16 * (NG // 2))
            sp.wait_ge(stored[1], 16 * (NG // 2 + 1))

        @block.gpsimd
        def _(pool):
            pool.memset(zeros16[:], 0.0).then_inc(pool_const, 1)
            pool.memset(ident[:], 0.0).then_inc(pool_const, 1)
            pool.memset(ident_b[:], 0.0).then_inc(pool_const, 1)
            pool.memset(pick[:], 0.0).then_inc(pool_const, 1)
            pool.wait_ge(pool_const, 4)
            for m in (ident, ident_b):
                pool.affine_select(out=m[:], in_=m[:], compare_op=ALU.not_equal, fill=1.0, base=0,
                                   pattern=[[-1, P]], channel_multiplier=1).then_inc(pool_const, 1)
            pool.iota(pid[:], pattern=[[0, 1]], base=0, channel_multiplier=1).then_inc(pool_const, 1)
            pool.iota(cid[:], pattern=[[1, P]], base=0, channel_multiplier=0).then_inc(pool_const, 1)
            pool.affine_select(out=pick[:].rearrange("r c (k h) -> r c k h", k=EPC), in_=pick[:].rearrange("r c (k h) -> r c k h", k=EPC),
                               compare_op=ALU.not_equal, fill=1.0, base=0,
                               pattern=[[-EPC, FC], [-1, EPC], [0, EH]], channel_multiplier=1).then_inc(pool_const, 1)
            pool.iota(rank_i[:], pattern=[[-1, EXPERTS]], base=EXPERTS, channel_multiplier=0).then_inc(pool_const, 1)
            pool.memset(va[:], 0.0).then_inc(pool_const, 1)
            pool.wait_ge(pool_const, 11)
            pool.memset(padded(va[:].rearrange("p b n -> p (b n)"))[:, :, DH:VA], 1.0).then_inc(pool_const, 1)
            pool.memset(table[:], 0.0).then_inc(table_zero, 1)

            def query_low(slot):
                return pool.tensor_tensor(q_part[1][:, slot], qf[:], q_part[0][:, slot].bitcast(fp32), ALU.subtract)

            for part in k_part:
                pool.memset(part[:, 0].bitcast(fp32), 0.0).then_inc(k_zero[0], 1)
            def sum_windows(b):
                for i in range(4):
                    pool.wait_ge(ld_x[4 * b + i], 16)
                n = WPB // 2 * HID
                base = b * WPB * HID
                pool.tensor_tensor(xsum[:, b, 0:n], rows[:, base:base + n], rows[:, base + n:base + 2 * n],
                                   ALU.add).then_inc(pool_step, 1)
                k = 1
                while n > HID:
                    n //= 2
                    pool.wait_ge(pool_step, 4 * b + k)
                    done = pool.tensor_tensor(xsum[:, b, 0:n], xsum[:, b, 0:n], xsum[:, b, n:2 * n], ALU.add)
                    done.then_inc(pool_step, 1)
                    k += 1

            for i, part in enumerate((wv_part, wo_part)):
                pool.wait_ge(wvo_high_ready, i + 1)
                pool.tensor_tensor(part[1][:], wT[:, WV + i, :, :], part[0][:].bitcast(fp32), ALU.subtract).then_inc(wvo_low_ready, 1)
            sum_windows(0)

            def take_low(n, p, pair):
                half = slice(pair * 2 * P, (pair + 1) * 2 * P)
                need(pool, h_in_psum, 4 * (n - 1))
                pool.wait_ge(high_ready, 2 * n + pair + 1)
                pool.tensor_tensor(xh_part[1][:, p, :, half], xhT[:, p, :, half], xh_part[0][:, p, :, half].bitcast(fp32),
                                   ALU.subtract).then_inc(low_ready, 1)

            def step(t, p, steady=False):
                nxt, cur, prev, pp = (live(t + k, steady) for k in (1, 0, -1, -2))

                def cut(u):
                    pool.wait_ge(shifted_ready, 4 * t + u + 1)
                    part = shifted[:, u, :].rearrange("p (h j) -> p h j", j=P)[:, :, 0:P:STRIDE]
                    pool.tensor_tensor(part, part, cut_cols[:], ALU.add).then_inc(cut_ready, 1)

                if nxt and (steady or t >= 0):
                    pool.wait_ge(x_high_ready, t + 2)
                    pool.tensor_tensor(x_part[1][:], xT[:, 1 - p, :, :], x_part[0][:].bitcast(fp32),
                                       ALU.subtract).then_inc(x_low_ready, 1)
                if cur:
                    cut(0)
                if prev:
                    if not steady and t == 1:
                        pool.wait_ge(sums_in_table, 16)
                    pool.wait_ge(rest_ready, t)
                    pool.wait_ge(e_ready, t)
                    e = e_val[:, 1 - p, :]
                    r = wide(rest[:, 1 - p, :])
                    pool.tensor_tensor(r, r, e[:, 0:HEADS].unsqueeze(2).broadcast_to([P, HEADS, VA]),
                                       ALU.mult).then_inc(rest_step, 1)
                    pool.tensor_tensor(wide(gl[:]), wide(table[:, bass.ds((t - 1) * EXW, NV)]),
                                       e[:, HEADS:2 * HEADS].unsqueeze(2).broadcast_to([P, HEADS, VA]),
                                       ALU.mult).then_inc(rest_step, 1)
                    pool.wait_ge(rest_step, 3 * t - 1)
                    pool.tensor_tensor(rest[:, 1 - p, :], rest[:, 1 - p, :], gl[:], ALU.add).then_inc(rest_step, 1)
                if cur:
                    cut(1)
                if pp and (steady or t < NW):
                    pool.wait_ge(a_high_ready, t - 1)
                    pool.tensor_tensor(a_part[1][:], aT[:, p, :, :], a_part[0][:].bitcast(fp32),
                                       ALU.subtract).then_inc(a_low_ready, 1)
                if pp:
                    if not steady and t == 2:
                        pool.wait_ge(out_bias_ready, 1)
                    need(pool, residual_ready, t - 3)
                    pool.tensor_tensor(biased[:, p, :], row(rows, t - 2, HID), out_bias[:], ALU.add).then_inc(biased_ready, 1)
                if nxt:
                    need(pool, scores_in_psum, 4 * t)
                    pool.wait_ge(q_high_ready, t + 2)
                    query_low(1 - p).then_inc(q_ready, 1)
                if cur:
                    cut(2)
                if live(t - 3, steady):
                    pool.wait_ge(stats_ready, t - 2)
                    pool.tensor_tensor(residual[:, 1 - p, :], residual[:, 1 - p, :],
                                       mean_var[:, 1 - p, 0:1].broadcast_to([P, HID]), ALU.subtract).then_inc(centred, 1)
                if cur:
                    cut(3)
                    need(pool, e_ready, t - 1)
                    pool.wait_ge(guard_ready, 4 * t + 4)
                    pool.tensor_tensor(e_arg[:, p, 0:HEADS], zeros16[:], guard[:, p, :], ALU.subtract)
                    pool.tensor_tensor(e_arg[:, p, HEADS:2 * HEADS], table[:, bass.ds(t * EXW + NV, HEADS)],
                                       guard[:, p, :], ALU.subtract).then_inc(e_arg_ready, 1)
                if prev:
                    need(pool, aT_in_psum, t - 2)
                    pool.wait_ge(rden_ready, t)
                    pool.tensor_tensor(attn[:, 1 - p, :].rearrange("p (h e) -> p h e", e=DH),
                                       wide(num[:, 1 - p, :])[:, :, 0:DH],
                                       rden[:, 1 - p, :].unsqueeze(2).broadcast_to([P, HEADS, DH]),
                                       ALU.mult).then_inc(attn_ready, 1)

            step(-1, 1)
            sum_windows(1)
            attention_steps(pool, step, first=0)
            pool.wait_ge(stats_ready, NW)
            last = (NW - 1) % 2
            pool.tensor_tensor(residual[:, last, :], residual[:, last, :],
                               mean_var[:, last, 0:1].broadcast_to([P, HID]), ALU.subtract).then_inc(centred, 1)

            pool.wait_ge(w2_high_ready, 1)
            pool.tensor_tensor(w2_part[1][:], w2[:], w2_part[0][:].bitcast(fp32), ALU.subtract).then_inc(w2_low_ready, 1)

            def step(n, p, steady=False):
                pp = live_group(n - 2, steady) and (steady or n < NG + 1)
                if pp:
                    need(pool, stored[p], 16 * ((n - 2) // 2))
                    pool.wait_ge(ystat_ready, n - 1)
                    pool.tensor_tensor(yout[:, p, :, :], ysum[:, p, :, :], ystat[:, p, :, 0:1].broadcast_to([P, TG, HID]),
                                       ALU.subtract).then_inc(y_centred, 1)
                for c in range(2):
                    if live_group(n, steady):
                        pool.wait_ge(hm_high_ready, 4 * n + c + 1)
                        pool.tensor_tensor(hm_part[1][:, p, c, :], hT[:, c, :], hm_part[0][:, p, c, :].bitcast(fp32),
                                           ALU.subtract).then_inc(hm_low_ready[0], 1)
                    if live_group(n + 1, steady):
                        take_low(n + 1, 1 - p, c)
                if pp:
                    pool.wait_ge(y_centred, n - 1)
                    pool.wait_ge(yrs_ready, n - 1)
                    pool.tensor_tensor(yout[:, p, :, :], yout[:, p, :, :],
                                       yrs[:, p, :].unsqueeze(2).broadcast_to([P, TG, HID]), ALU.mult).then_inc(yout_ready, 1)

            expert_steps(pool, step)

        @block.scalar
        def _(act):
            for i, src in enumerate((wg_dram, ln_scale_dram, ln_bias_dram)):
                act.dma_start(vec_rows[EXPERTS * i:EXPERTS * (i + 1), :], src).then_inc(ld_gate, 16)
            for i, src in enumerate((bq_dram, bk_dram, bv_dram)):
                act.dma_start(vec_rows[3 * EXPERTS + i:3 * EXPERTS + i + 1, :],
                              src.rearrange("(a n) -> a n", a=1)).then_inc(ld_gate, 16)
            act.dma_start(b1_rows[:], b1_dram.rearrange("(c e) h -> c (e h)", e=EPC)).then_inc(ld_gate, 16)
            act.wait_ge(pool_const, 1)
            act.activation(e_val[:, 0, 0:HEADS], zeros16[:], ACT.Exp)

            def copy(dst, src):
                return act.activation(dst, src, ACT.Copy)

            def query_high(slot):
                return copy(q_part[0][:, slot], qf[:])

            def key_rows(bank):
                for c in range(KC):
                    last = act.activation(kf[:, c, :], bank[:, c * P:(c + 1) * P], ACT.Identity, bias=bk_col[:, c:c + 1])
                return last

            def key_high(slot):
                for q in range(QUADS):
                    last = copy(k_part[0][quad(q), slot, :, q, :], kf[quad(q), :, :])
                return last

            act.wait_ge(xgT_in_psum, 1)
            copy(xgT[:].rearrange("p c n -> p (c n)"), ps[:, 5, 0:HID]).then_inc(xgT_ready, 1)
            act.wait_ge(vecT_in_psum, 1)
            copy(b1[:], ps[:, 4, KC * NVEC:KC * NVEC + FC])
            copy(vecT[:].rearrange("p c n -> p (c n)"), ps[:, 4, 0:KC * NVEC]).then_inc(vecT_ready, 1)
            for i in (WV, WO):
                act.wait_ge(wT_in_psum, i + 1)
                copy(wT[:, i, :, :].rearrange("p c n -> p (c n)"), ps[:, i, :]).then_inc(wvo_ready, 1)
            for i, part in enumerate((wv_part, wo_part)):
                act.wait_ge(wvo_ready, i + 1)
                copy(part[0][:], wT[:, WV + i, :, :]).then_inc(wvo_high_ready, 1)
            act.wait_ge(kg_in_psum, 1)
            act.wait_ge(vecT_ready, 1)
            key_rows(ps[:, 7, :]).then_inc(kgf_ready, 1)
            act.wait_ge(kgf_ready, 1)
            act.wait_ge(k_zero[1], 1)
            key_high(1).then_inc(kg_high_ready, 1)
            act.wait_ge(qgf_ready, 1)
            query_high(1).then_inc(qg_high_ready, 1)
            act.wait_ge(pool_const, 12)
            act.wait_ge(vg_in_psum, 1)
            copy(padded(vg)[:, :, 0:DH], ps[:, 4, HID:2 * HID].rearrange("p (h e) -> p h e", e=DH)).then_inc(vg_ready, 1)

            def keep_xsumT(b):
                act.wait_ge(xsumT_in_psum, b + 1)
                copy(xsumT[:, b, :, :].rearrange("p c n -> p (c n)"), batch_bank(b)[:, 0:HID]).then_inc(xsumT_ready, 1)

            def scale_rows(n, pair):
                for j in (2 * pair, 2 * pair + 1):
                    w = TG * n + j
                    act.activation(xh[:, j, :], row(rows, w, HID), ACT.Copy, scale=rs2[:, bass.ds(w, 1)]).then_inc(xh_ready, 1)

            def evacuate(n, p, pair, more):
                need(act, zT_in_psum, n - 1)
                need(act, low_ready, 2 * (n - 1))
                act.wait_ge(xhT_in_psum, 2 * n + pair + 1)
                act.activation(xhT[:, p, :, pair * 2 * P:(pair + 1) * 2 * P].rearrange("p c (t n) -> p t c n", t=2),
                               group_banks(n)[pair].rearrange("p (t c n) -> p t c n", t=2, c=KC), ACT.Copy).then_inc(xhT_ready, 1)
                if more:
                    scale_rows(n + 1, pair)

            def keep_logits(n):
                need(act, z_in_psum, n)
                act.wait_ge(zT_in_psum, n + 1)
                copy(zT[:], group_banks(n)[2][:, 0:P]).then_inc(zT_ready, 1)

            def keep_onehot(n, p):
                need(act, y_in_psum, 4 * (n - 1))
                act.wait_ge(ohT_in_psum, n + 1)
                act.activation(ohT[:, p, :], group_banks(n)[2][0:3 * EXPERTS, 2 * P:2 * P + GT // 2].bitcast(bf16),
                               ACT.Copy).then_inc(ohT_ready, 1)

            def step(t, p, steady=False):
                nxt, cur, prev, pp = (live(t + k, steady) for k in (1, 0, -1, -2))

                def exp(w, u):
                    g = 4 * w + u
                    need(act, pv_in_psum, g - 3)
                    act.wait_ge(dT_in_psum, g + 1)
                    act.activation(probs[:, u, :], ps_dT[u % 2], ACT.Exp).then_inc(probs_ready, 1)

                if not steady and t == NW:
                    evacuate(0, 0, 0, True)
                if prev:
                    exp(t - 1, 2)
                    need(act, rest_step, 3 * (t - 2))
                    act.wait_ge(e_arg_ready, t)
                    act.activation(e_val[:, 1 - p, :], e_arg[:, 1 - p, :], ACT.Exp).then_inc(e_ready, 1)
                if nxt:
                    need(act, v_in_psum, t)
                    act.wait_ge(xT_in_psum, t + 2)
                    copy(xT[:, 1 - p, :, :].rearrange("p c n -> p (c n)"), ps_xq[:, 0:HID]).then_inc(xT_ready, 1)
                    copy(x_part[0][:].rearrange("p c n -> p (c n)"), ps_xq[:, 0:HID]).then_inc(x_high_ready, 1)
                if prev:
                    exp(t - 1, 3)
                if pp:
                    need(act, o_in_psum, t - 2)
                    act.wait_ge(aT_in_psum, t - 1)
                    copy(aT[:, p, :, :].rearrange("p c n -> p (c n)"), ps_rao[:, 0:HID]).then_inc(aT_ready, 1)
                    copy(a_part[0][:].rearrange("p c n -> p (c n)"), ps_rao[:, 0:HID]).then_inc(a_high_ready, 1)
                if not steady and t == NW:
                    evacuate(0, 0, 1, True)
                if nxt:
                    if not steady and t == -1:
                        act.wait_ge(kg_ready, 1)
                        act.wait_ge(k_zero[0], 2)
                    need(act, scores_in_psum, 4 * t)
                    need(act, k_ready, t + 1)
                    act.wait_ge(k_in_psum, t + 2)
                    key_rows(ps_kv).then_inc(kf_ready, 1)
                    act.wait_ge(kf_ready, t + 2)
                    key_high(1 - p).then_inc(k_high_ready, 1)
                    act.wait_ge(qf_ready, t + 2)
                    query_high(1 - p).then_inc(q_high_ready, 1)
                if cur:
                    exp(t, 0)
                if prev:
                    need(act, sums_in_psum, t - 1)
                    act.wait_ge(pv_in_psum, 4 * t)
                    copy(pvT[:], ps_pv).then_inc(pvT_ready, 1)
                if not steady and t == NW:
                    keep_logits(0)
                if not steady and t == NW - 1:
                    for k in kept:
                        act.wait_ge(k, 16 * (EARLY // 2))
                    act.wait_ge(ln_ready, 1)
                    for pair in range(2):
                        scale_rows(0, pair)
                if not steady and t == NW + 1:
                    act.activation(e_arg[:, 0, 0:HEADS], zeros16[:], ACT.Gelu)
                    keep_onehot(0, 0)
                    act.wait_ge(scores_in_psum, 4 * NW)
                    act.wait_ge(ld_w2, 16)
                    copy(w2_part[0][:], w2[:]).then_inc(w2_high_ready, 1)
                if nxt:
                    act.wait_ge(v_in_psum, t + 2)
                    need(act, pv_in_psum, 4 * t)
                    copy(padded(va[:, 1 - p, :])[:, :, 0:DH],
                         ps_kv[:, HID:2 * HID].rearrange("p (h e) -> p h e", e=DH)).then_inc(v_ready, 1)
                if cur:
                    exp(t, 1)
                if not steady and t == 0:
                    keep_xsumT(1)

            step(-1, 1)
            for u in range(UNITS):
                act.wait_ge(gT_in_psum, u + 1)
                act.activation(pg[:, u, :], ps[:, u, :], ACT.Exp).then_inc(g_probs, 1)
            act.wait_ge(g_pv, 1)
            copy(pvT[:], ps_pv).then_inc(g_pvT_ready, 1)
            keep_xsumT(0)
            act.wait_ge(g_sums_in_psum, 1)
            for c in range(KC):
                last = copy(g_row[:, c * NV // KC:(c + 1) * NV // KC].rearrange("p (u a e) -> p u a e", u=UNITS, a=2),
                            ps_pv.rearrange("p (c a q e) -> p c q a e", c=KC, a=2, q=QUADS)[:, c, :, :, 0:VA])
            last.then_inc(g_sums_ready, 1)

            attention_steps(act, step, first=0)

            def step(n, p, steady=False):
                nxt, cur, prev = (live_group(n + k, steady) for k in (1, 0, -1))

                def hidden_high(c):
                    need(act, y_in_psum, 4 * (n - 1))
                    act.wait_ge(hm_ready, 4 * n + c + 1)
                    copy(hm_part[0][:, p, c, :], hT[:, c, :]).then_inc(hm_high_ready, 1)

                for c in range(FC):
                    if cur:
                        need(act, hm_low_ready[c // 2], 2 * (n - 1) + c % 2 + 1)
                        act.wait_ge(h_in_psum, 4 * n + c + 1)
                        act.activation(hT[:, c, :], ps[:, c % 2, :], ACT.Gelu, bias=b1s[:, c:c + 1]).then_inc(h_ready, 1)
                    if nxt and c < 2:
                        evacuate(n + 1, 1 - p, c, live_group(n + 2, steady))
                    if nxt and c == 2:
                        keep_logits(n + 1)
                    if nxt and c == FC - 1:
                        keep_onehot(n + 1, 1 - p)
                    if cur:
                        hidden_high(c)
                if not steady and n == 1:
                    for k in kept:
                        act.wait_ge(k, 16 * (NW // 2))
                    act.wait_ge(ln_ready, 2)

            act.wait_ge(ffn_w_ready, 1)
            expert_steps(act, step)

        @block.vector
        def _(dve):
            count = [0]

            def link(ins):
                count[0] += 1
                ins.then_inc(dve_const, 1)
                dve.wait_ge(dve_const, count[0])

            dve.wait_ge(pool_const, 10)
            dve.tensor_scalar(pbits[:, 0:1], pid[:], DH, None, ALU.bitwise_and)
            dve.tensor_scalar(pbits[:, 1:2], pid[:], 2, None, ALU.logical_shift_right)
            dve.tensor_scalar(pbits[:, 2:3], pid[:], 6, None, ALU.logical_shift_right)
            link(dve.tensor_scalar(pbits[:, 3:4], pid[:], STRIDE - 1, None, ALU.bitwise_and))
            link(dve.tensor_scalar(cbits[:], cid[:], 2, None, ALU.logical_shift_right))
            dve.tensor_copy(pvals[:], pbits[:])
            link(dve.tensor_copy(cvals[:], cbits[:]))
            dve.tensor_scalar(q_scale[:, 0, :], pvals[:, 0:1].broadcast_to([P, P]), 0.0, SCALE, ALU.is_equal, ALU.mult)
            link(dve.tensor_scalar(q_scale[:, 1, :], pvals[:, 0:1].broadcast_to([P, P]), float(DH), SCALE, ALU.is_equal, ALU.mult))
            for i in (WQ, WK):
                dve.wait_ge(wT_in_psum, i + 1)
                dve.tensor_copy(wT[:, i, :, :].rearrange("p c n -> p (c n)"), ps[:, i, :]).then_inc(wqk_ready, 1)
            for part in k_part:
                last = dve.memset(part[:, 1].bitcast(fp32), 0.0)
            last.then_inc(k_zero[1], 1)
            for b in range(B):
                mine, other = (slice(k * GLOBALS, (k + 1) * GLOBALS) for k in (b, 1 - b))
                dve.memset(dg[mine, :, :].rearrange("p u (h j) -> p (u h) j", j=P)[:, :, other], CUT)
            dve.tensor_scalar(g_factor[:], cvals[:], pvals[:, 1:2], 1.0, ALU.is_equal, ALU.add)
            dve.tensor_scalar(is_glob[:], pvals[:, 3:4], 0.0, None, ALU.is_equal)
            link(dve.memset(zero_w[:], 1.0))
            link(dve.scalar_tensor_tensor(zero_w[:, 0:P:STRIDE], zero_w[:, 0:P:STRIDE], is_glob[:],
                                          zero_w[:, 0:P:STRIDE], ALU.subtract, ALU.mult))
            dve.tensor_scalar(neg_zero_w[:], zero_w[:], -1.0, None, ALU.mult)
            dve.tensor_scalar(cut_cols[:].rearrange("p h g -> p (h g)"), is_glob[:].broadcast_to([P, HPU * GPW]), CUT, None, ALU.mult)
            for b in range(B):
                dve.tensor_scalar(wide(v_all[:, b * NV:(b + 1) * NV])[:, :, DH], is_glob[:].broadcast_to([P, HEADS]),
                                  float(-GLOBALS), float(S), ALU.mult, ALU.add)
            dve.tensor_copy(rank[:], rank_i[:])
            dve.memset(gate[:], 0.0).then_inc(dve_const, 1)
            count[0] += 1
            dve.wait_ge(vecT_ready, 1)
            dve.wait_ge(dve_const, count[0])
            dve.tensor_copy(gate[:, :, 0:EXPERTS], vecT[:, :, 0:EXPERTS])
            dve.tensor_copy(bv_wide[:], bv_col.unsqueeze(2).broadcast_to([P, KC, P])).then_inc(consts_ready, 1)
            dve.wait_ge(consts_ready, 1)

            def queries(c, bank):
                return dve.scalar_tensor_tensor(qf[:, c, :, :], bank[:, c * P:(c + 1) * P].unsqueeze(1).broadcast_to([P, 2, P]),
                                                bq_col[:, c:c + 1], q_scale[:], ALU.add, ALU.mult)

            def key_low(slot, q):
                return dve.tensor_tensor(k_part[1][quad(q), slot, :, q, :], kf[quad(q), :, :],
                                         k_part[0][quad(q), slot, :, q, :].bitcast(fp32), ALU.subtract)

            dve.wait_ge(qg_in_psum, 1)
            for c in range(KC):
                last = queries(c, ps[:, 6, :])
            last.then_inc(qgf_ready, 1)
            dve.wait_ge(kg_high_ready, 1)
            for q in range(QUADS):
                last = key_low(1, q)
            last.then_inc(kg_ready, 1)
            dve.wait_ge(qg_high_ready, 1)
            dve.tensor_tensor(q_part[1][:, 1], qf[:], q_part[0][:, 1].bitcast(fp32), ALU.subtract).then_inc(qg_ready, 1)


            def in_batch(b, ap):
                return keys(ap)[b * GLOBALS:(b + 1) * GLOBALS, :, b * GLOBALS:(b + 1) * GLOBALS]

            def scale(u):
                dve.wait_ge(gs_in_psum, u + 1)
                for b in range(B):
                    factor = g_factor[b * GLOBALS:(b + 1) * GLOBALS, b * GLOBALS:(b + 1) * GLOBALS]
                    last = dve.tensor_tensor(in_batch(b, dg[:, u, :]), in_batch(b, ps[:, u, :]),
                                             factor.unsqueeze(1).broadcast_to([GLOBALS, HPU, GLOBALS]), ALU.mult)
                last.then_inc(gs_scaled, 1)

            def maximum(u):
                dve.wait_ge(gs_scaled, u + 1)
                for b in range(B):
                    last = dve.tensor_reduce(by_head(mg_raw[b * GLOBALS:(b + 1) * GLOBALS, :], u), in_batch(b, dg[:, u, :]),
                                             op=ALU.max, axis=AX.X)
                last.then_inc(gs_max, 1)

            def subtract(u):
                dve.wait_ge(gs_max, 2 * UNITS)
                for b in range(B):
                    last = dve.tensor_tensor(in_batch(b, dg[:, u, :]), in_batch(b, dg[:, u, :]),
                                             by_head(g_row[b * GLOBALS:(b + 1) * GLOBALS, NV:EXW], u).unsqueeze(2)
                                             .broadcast_to([GLOBALS, HPU, GLOBALS]), ALU.subtract)
                last.then_inc(gs_shifted, 1)

            def newton_of(k, x, y, t):
                if k == 0:
                    return dve.tensor_scalar(t.bitcast(i32), x.bitcast(i32), 1, None, ALU.logical_shift_right)
                if k == 1:
                    return dve.tensor_scalar(y.bitcast(i32), t.bitcast(i32), -1.0, RSQRT_SEED, ALU.mult, ALU.add)
                if k % 3 == 2:
                    return dve.scalar_tensor_tensor(t, y, -0.5, y, ALU.mult, ALU.mult)
                if k % 3 == 0:
                    return dve.tensor_tensor(t, t, x, ALU.mult)
                return dve.scalar_tensor_tensor(y, t, 1.5, y, ALU.add, ALU.mult)

            def factors(first, end, k0, k1):
                part = slice(first, end)
                var = stats[:].rearrange("p (w s) -> p w s", s=2)[:, part, 1]
                n, r = NEWTON_STEPS, rs1[:, part]
                for k in range(k0, k1):
                    if k == 0:
                        dve.wait_ge(moments_ready, end)
                        last = dve.tensor_scalar(nx[:, part], var, EPS, None, ALU.add)
                    else:
                        dve.wait_ge(ln_step, (0 if first == 0 else FACTOR_STEPS - 1) + k)
                    if 1 <= k <= n:
                        last = newton_of(k - 1, nx[:, part], r, nt[:, part])
                    if k == n + 1:
                        last = dve.tensor_tensor(var1[:, part], r, r, ALU.mult)
                    if k == n + 2:
                        last = dve.tensor_tensor(var1[:, part], var1[:, part], var, ALU.mult)
                    if k == n + 3:
                        last = dve.tensor_scalar(var1[:, part], var1[:, part], EPS, None, ALU.add)
                    if n + 4 <= k < FACTOR_STEPS - 1:
                        last = newton_of(k - n - 4, var1[:, part], rs2[:, part], nt[:, part])
                    if k == FACTOR_STEPS - 1:
                        last = dve.tensor_tensor(rs2[:, part], r, rs2[:, part], ALU.mult)
                    last.then_inc(ln_ready if k == FACTOR_STEPS - 1 else ln_step, 1)

            def keep_values(b):
                dve.wait_ge(vall_in_psum, b + 1)
                dve.tensor_copy(wide(v_all[:, b * NV:(b + 1) * NV])[:, :, 0:DH],
                                batch_bank(b)[:, HID:2 * HID].rearrange("p (h e) -> p h e", e=DH)).then_inc(vall_ready, 1)

            def take_high(n, p, pair):
                half = slice(pair * 2 * P, (pair + 1) * 2 * P)
                need(dve, h_in_psum, 4 * (n - 1))
                need(dve, low_ready, 2 * (n - 1))
                dve.wait_ge(xhT_ready, 2 * n + pair + 1)
                dve.tensor_copy(xh_part[0][:, p, :, half], xhT[:, p, :, half]).then_inc(high_ready, 1)

            ROUTE_STEPS = 5
            EARLY_SLOTS = 7

            def route(k, n):
                z = group_banks(n)[2][:, P:2 * P].rearrange("p (t e) -> p t e", e=VP)[:, :, 0:EXPERTS]
                dve.wait_ge(z_in_psum, n + 1) if k == 0 else dve.wait_ge(route_step, 4 * n + k)
                if k == 0:
                    dve.tensor_reduce(zmax[:, 0, :], z, op=ALU.max, axis=AX.X).then_inc(route_step, 1)
                if k == 1:
                    dve.tensor_tensor(hit[:], z, zmax[:, 0, :].unsqueeze(2).broadcast_to([P, TG, EXPERTS]),
                                      ALU.is_equal).then_inc(route_step, 1)
                if k == 2:
                    dve.tensor_tensor(hit[:], hit[:], rank[:].unsqueeze(1).broadcast_to([P, TG, EXPERTS]),
                                      ALU.mult).then_inc(route_step, 1)
                if k == 3:
                    dve.tensor_reduce(zmax[:, 1, :], hit[:], op=ALU.max, axis=AX.X).then_inc(route_step, 1)
                if k == 4:
                    dve.tensor_tensor(onehot[:], hit[:].unsqueeze(2).broadcast_to([P, TG, 3, EXPERTS]),
                                      zmax[:, 1, :].unsqueeze(2).unsqueeze(2).broadcast_to([P, TG, 3, EXPERTS]),
                                      ALU.is_equal).then_inc(onehot_ready, 1)

            scale(0)
            for u in range(UNITS):
                if u + 1 < UNITS:
                    scale(u + 1)
                maximum(u)
            dve.wait_ge(x_high_ready, 1)
            dve.tensor_tensor(x_part[1][:], xT[:, 0, :, :], x_part[0][:].bitcast(fp32), ALU.subtract).then_inc(x_low_ready, 1)
            dve.wait_ge(qg_ready, 1)
            dve.wait_ge(q_in_psum, 1)
            queries(0, ps_xq[:, HID:2 * HID])
            queries(1, ps_xq[:, HID:2 * HID]).then_inc(qf_ready, 1)
            dve.wait_ge(gs_max, UNITS)
            dve.tensor_scalar(g_row[:, NV:EXW], mg_raw[:], 0.0, None, ALU.max).then_inc(gs_max, UNITS)
            for u in range(UNITS):
                subtract(u)

            def step(t, p, steady=False):
                nxt, cur, prev, pp = (live(t + k, steady) for k in (1, 0, -1, -2))

                def reduce(u):
                    dve.wait_ge(scores_in_psum, 4 * t + u + 1)
                    dve.tensor_reduce(by_head(row_max[:, p, :], u), keys(ps_score[u % 2]), op=ALU.max,
                                      axis=AX.X).then_inc(max_ready, 1)

                def bound(u):
                    if u == 0:
                        need(dve, e_arg_ready, t - 1)
                    dve.wait_ge(max_ready, 4 * t + u + 1)
                    dve.tensor_tensor(by_head(guard[:, p, :], u), by_head(row_max[:, p, :], u),
                                      by_head(table[:, bass.ds(t * EXW + NV, HEADS)], u), ALU.max).then_inc(guard_ready, 1)

                def shift(u):
                    need(dve, dT_in_psum, 4 * t + u - 3)
                    dve.wait_ge(guard_ready, 4 * t + u + 1)
                    dve.tensor_tensor(keys(shifted[:, u, :]), keys(ps_score[u % 2]),
                                      by_head(guard[:, p, :], u).unsqueeze(2).broadcast_to([P, HPU, P]),
                                      ALU.subtract).then_inc(shifted_ready, 1)

                def numerator():
                    need(dve, attn_ready, t - 2)
                    dve.wait_ge(sums_in_psum, t)
                    dve.wait_ge(rest_step, 3 * t)
                    sums = ps_pv.rearrange("p (c a q e) -> p c q a e", c=KC, a=2, q=QUADS)
                    for c in range(KC):
                        half = slice(c * NV // KC, (c + 1) * NV // KC)
                        view = num[:, 1 - p, half].rearrange("p (u a e) -> p u a e", u=UNITS, a=2)
                        last = dve.tensor_tensor(view, sums[:, c, :, :, 0:VA],
                                                 rest[:, 1 - p, half].rearrange("p (u a e) -> p u a e", u=UNITS, a=2), ALU.add)
                    last.then_inc(num_ready, 1)

                def reciprocal():
                    dve.wait_ge(num_ready, t)
                    dve.reciprocal(rden[:, 1 - p, :], wide(num[:, 1 - p, :])[:, :, DH]).then_inc(rden_ready, 1)

                turned = not steady and t == NW

                def early(slot):
                    k = EARLY_SLOTS * (t - LOOP_A[1]) + slot if not steady else -1
                    if cur and 0 <= k < FACTOR_STEPS:
                        factors(0, EARLY, k, k + 1)

                if cur:
                    early(0)
                    reduce(0)
                    need(dve, num_ready, t - 1)
                    dve.wait_ge(r_in_psum, t + 1)
                    dve.tensor_tensor(rest[:, p, :], ps_rao[:, 0:NV], v_all[:, bass.ds(t // WPB * NV, NV)],
                                      ALU.add).then_inc(rest_ready, 1)
                    bound(0)
                    early(1)
                    shift(0)
                    early(2)
                    reduce(1)
                    early(3)
                    bound(1)
                    shift(1)
                old = live(t - 3, steady)
                if old:
                    dve.wait_ge(residual_ready, t - 2)
                    dve.bn_stats(bn6[:, 0, :], residual[:, 1 - p, :]).then_inc(bn_ready, 1)
                if nxt:
                    need(dve, q_ready, t + 1)
                    dve.wait_ge(q_in_psum, t + 2)
                    queries(0, ps_xq[:, HID:2 * HID])
                if old:
                    dve.wait_ge(bn_ready, t - 2)
                if nxt:
                    queries(1, ps_xq[:, HID:2 * HID]).then_inc(qf_ready, 1)
                if old:
                    dve.bn_aggr(mean_var[:, 1 - p, :], bn6[:, 0, :]).then_inc(stats_ready, 1)
                    dve.wait_ge(stats_ready, t - 2)
                if cur:
                    reduce(2)
                if old:
                    dve.tensor_copy(row(stats, t - 3, 2), mean_var[:, 1 - p, :]).then_inc(moments_ready, 1)
                if cur:
                    early(4)
                if nxt:
                    dve.wait_ge(k_high_ready, t + 2)
                    for q in (0, 1):
                        key_low(1 - p, q)
                if cur:
                    bound(2)
                    early(5)
                if nxt:
                    key_low(1 - p, 2)
                if cur:
                    shift(2)
                if turned:
                    for pair in range(2):
                        take_high(0, 0, pair)
                if pp and not steady and t >= NW:
                    dve.wait_ge(a_high_ready, t - 1)
                    dve.tensor_tensor(a_part[1][:], aT[:, p, :, :], a_part[0][:].bitcast(fp32), ALU.subtract).then_inc(a_low_ready, 1)
                if not steady and t == NW + 1:
                    dve.wait_ge(pv_in_psum, 4 * NW)
                    dve.wait_ge(high_ready, 2)
                    for pair in range(2):
                        half = slice(pair * 2 * P, (pair + 1) * 2 * P)
                        dve.tensor_tensor(xh_part[1][:, 0, :, half], xhT[:, 0, :, half], xh_part[0][:, 0, :, half].bitcast(fp32),
                                          ALU.subtract).then_inc(low_ready, 1)
                    dve.wait_ge(b1_in_psum, 1)
                    for k in range(EPC):
                        part = slice(k * EH, (k + 1) * EH)
                        last = dve.tensor_tensor(b1s[part, :], ps[part, 0, k:EPC * FC:EPC], b1[part, :], ALU.add)
                    last.then_inc(ffn_w_ready, 1)
                if pp:
                    need(dve, kept[p], 16 * ((t - 2) // 2))
                    dve.wait_ge(o_in_psum, t - 1)
                    dve.wait_ge(biased_ready, t - 1)
                    dve.tensor_tensor(residual[:, p, :], ps_rao[:, 0:HID], biased[:, p, :], ALU.add).then_inc(residual_ready, 1)
                if nxt:
                    key_low(1 - p, 3).then_inc(k_ready, 1)
                if turned:
                    numerator()
                    reciprocal()
                if cur:
                    early(6)
                    reduce(3)
                if prev and not turned:
                    numerator()
                if cur:
                    bound(3)
                if prev and not turned:
                    reciprocal()
                if cur:
                    shift(3)
                if not steady and t == 0:
                    keep_values(1)
                if not steady and t == NW:
                    for k in range(ROUTE_STEPS):
                        route(k, 0)

            dve.wait_ge(k_zero[0], 2)
            dve.wait_ge(k_high_ready, 1)
            for q in range(QUADS):
                last = key_low(0, q)
            last.then_inc(k_ready, 1)
            dve.wait_ge(ld_w1, 16 * KC)
            for c in range(KC):
                last = dve.tensor_tensor(w1s[:, c, :].rearrange("p (e h) -> p e h", h=EH), w1[:, c, :, :],
                                         vecT[:, c, EXPERTS:2 * EXPERTS].unsqueeze(2).broadcast_to([P, EXPERTS, EH]), ALU.mult)
            link(last)
            high, low = w1_part
            link(dve.tensor_copy(high[:], w1s))
            dve.tensor_tensor(low[:], w1s, high[:].bitcast(fp32), ALU.subtract)
            dve.wait_ge(ld_b, 48)
            dve.tensor_scalar(b2_sel[:, 0:1], pvals[:, 1:2], 1.5, None, ALU.is_le)
            dve.tensor_scalar(b2_sel[:, 2:3], pvals[:, 1:2], 3.5, None, ALU.is_ge)
            link(dve.tensor_copy(b2_h[:, 0, :], b2_f))
            link(dve.tensor_tensor(b2_t[0], b2_f, b2_h[:, 0, :], ALU.subtract))
            link(dve.tensor_copy(b2_h[:, 1, :], b2_t[0]))
            link(dve.tensor_tensor(b2_t[1], b2_t[0], b2_h[:, 1, :], ALU.subtract))
            link(dve.tensor_tensor(b2_sel[:, 1:2], b2_sel[:, 0:1], b2_sel[:, 2:3], ALU.add))
            link(dve.tensor_scalar(b2_sel[:, 1:2], b2_sel[:, 1:2], -1.0, 1.0, ALU.mult, ALU.add))
            rs = slice(0, 3 * EXPERTS)
            link(dve.tensor_scalar(b2_t[2], b2_t[1], b2_sel[rs, 2:3], None, ALU.mult))
            link(dve.scalar_tensor_tensor(b2_t[0], b2_h[:, 1, :], b2_sel[rs, 1:2], b2_t[2], ALU.mult, ALU.add))
            dve.scalar_tensor_tensor(b2_stack[:], b2_h[:, 0, :], b2_sel[rs, 0:1], b2_t[0], ALU.mult, ALU.add)
            keep_values(0)
            dve.wait_ge(bias_in_psum, 1)
            dve.wait_ge(ld_bo, 16)
            dve.tensor_tensor(out_bias[:], ps_pv[:, 0:HID], out_bias[:], ALU.add).then_inc(out_bias_ready, 1)
            dve.wait_ge(vall_ready, 1)
            dve.wait_ge(guards_in_table, 16)

            attention_steps(dve, step, first=0)
            last = (NW - 1) % 2
            dve.wait_ge(residual_ready, NW)
            dve.bn_stats(bn6[:, 0, :], residual[:, last, :]).then_inc(bn_ready, 1)
            dve.wait_ge(bn_ready, NW)
            dve.bn_aggr(mean_var[:, last, :], bn6[:, 0, :]).then_inc(stats_ready, 1)
            dve.wait_ge(stats_ready, NW)
            dve.tensor_copy(row(stats, NW - 1, 2), mean_var[:, last, :]).then_inc(moments_ready, 1)
            for k in kept:
                dve.wait_ge(k, 16 * (EARLY // 2))

            def step(n, p, steady=False):
                nxt, cur, prev, pp = (live_group(n + k, steady) for k in (1, 0, -1, -2))
                y = yrs[:, p, :]

                def newton(k):
                    at = NEWTON_STEPS * (n - 2)
                    if k == 0:
                        dve.wait_ge(ystat_ready, n - 1)
                        last = dve.tensor_scalar(yvar[:], ystat[:, p, :, 1], EPS, None, ALU.add)
                    else:
                        dve.wait_ge(y_newton, at + k)
                    if k == 2 and not steady:
                        need(dve, yout_ready, n - 3)
                    if k >= 1:
                        last = newton_of(k - 1, yvar[:], y, ytmp[:])
                    last.then_inc(yrs_ready if k == NEWTON_STEPS else y_newton, 1)

                def newtons(first, end):
                    if pp:
                        for k in range(first, end):
                            newton(k)

                def finish(j):
                    w = TG * (n - 1) + j
                    if j == 0:
                        need(dve, y_centred, n - 2)
                    dve.wait_ge(y_in_psum, w + 1)
                    dve.scalar_tensor_tensor(ysum[:, 1 - p, j, :], row(rows, w, HID), rs1[:, bass.ds(w, 1)],
                                             ps[:, 4 + j % 2, 0:HID], ALU.mult, ALU.add).then_inc(ysum_ready, 1)
                    newtons(3 * j, 3 * j + 2)
                    dve.wait_ge(ysum_ready, w + 1)
                    dve.bn_stats(bn6[:, j, :], ysum[:, 1 - p, j, :]).then_inc(ybn_ready, 1)

                def hidden_low(m, pm, c):
                    dve.wait_ge(hm_high_ready, 4 * m + c + 1)
                    dve.tensor_tensor(hm_part[1][:, pm, c, :], hT[:, c, :], hm_part[0][:, pm, c, :].bitcast(fp32),
                                      ALU.subtract).then_inc(hm_low_ready[1], 1)

                for c in range(FC):
                    if prev and c == 0:
                        hidden_low(n - 1, 1 - p, FC - 1)
                    if cur and c == FC - 1:
                        hidden_low(n, p, FC - 2)
                    if cur:
                        dve.wait_ge(h_ready, 4 * n + c + 1)
                        dve.wait_ge(mask_in_psum, 4 * n + c + 1)
                        dve.tensor_tensor(hT[:, c, :], ps[:, 2 + c % 2, :], hT[:, c, :], ALU.mult).then_inc(hm_ready, 1)
                    if nxt and c < 2:
                        take_high(n + 1, 1 - p, c)
                    if nxt and c == 2:
                        for k in range(ROUTE_STEPS):
                            route(k, n + 1)
                    if prev:
                        finish(c)
                    elif pp:
                        newtons(3 * c, 3 * c + 2)
                    if prev and c == FC - 1:
                        dve.wait_ge(ybn_ready, 4 * n)
                    newtons(3 * c + 2, 3 * c + 3)
                    if not steady and n == 0:
                        factors(EARLY, NW, c * 7, min(c * 7 + 7, FACTOR_STEPS))
                if not steady and n == 1:
                    for k in kept:
                        dve.wait_ge(k, 16 * (NW // 2))
                if not steady and n == NG + 1:
                    need(dve, stored[p], 16 * ((n - 2) // 2))
                    dve.wait_ge(yrs_ready, n - 1)
                    for j in range(TG):
                        last = dve.tensor_scalar(yout[:, p, j, :], ysum[:, p, j, :], ystat[:, p, j, 0:1], yrs[:, p, j:j + 1],
                                                 ALU.subtract, ALU.mult)
                        if j % 2:
                            last.then_inc(last_out_ready, 1)
                if prev:
                    for j in range(TG):
                        last = dve.bn_aggr(ystat[:, 1 - p, j, :], bn6[:, j, :])
                    last.then_inc(ystat_ready, 1)

            expert_steps(dve, step)

        @block.tensor
        def _(pe):
            mm = nc.tensor.matmul

            def product(out, lhsT, rhs):
                for c in range(KC):
                    last = mm(out, lhsT(c), rhs(c), start=(c == 0), stop=(c == KC - 1))
                return last

            pe.wait_ge(pool_const, 6)
            pe.wait_ge(ld_xg, 16)
            for c in range(KC):
                last = nc.tensor.transpose(ps[:, 5, c * P:(c + 1) * P], xg[:, c * P:(c + 1) * P], ident[:])
            last.then_inc(xgT_in_psum, 1)
            for i in range(4):
                pe.wait_ge(ld_w[i], 16)
                for oc in range(KC):
                    for ic in range(KC):
                        last = nc.tensor.transpose(ps[:, i, ic * HID + oc * P:ic * HID + (oc + 1) * P],
                                                   w_raw[:, i, oc, ic * P:(ic + 1) * P], ident[:])
                last.then_inc(wT_in_psum, 1)
            pe.wait_ge(ld_gate, 112)
            for c in range(KC):
                last = nc.tensor.transpose(ps[:, 4, c * NVEC:(c + 1) * NVEC],
                                           vec_rows[:, c * P:(c + 1) * P], ident[0:NVEC, 0:NVEC])
            last = nc.tensor.transpose(ps[:, 4, KC * NVEC:KC * NVEC + FC], b1_rows[:], ident[0:FC, 0:FC])
            last.then_inc(vecT_in_psum, 1)
            pe.wait_ge(xgT_ready, 1)
            pe.wait_ge(wqk_ready, 2)
            for o in range(KC):
                last = product(ps[:, 7, o * P:(o + 1) * P], lambda c: wT[:, WK, c, o * P:(o + 1) * P], lambda c: xgT[:, c, :])
            last.then_inc(kg_in_psum, 1)
            for o in range(KC):
                last = product(ps[:, 6, o * P:(o + 1) * P], lambda c: wT[:, WQ, c, o * P:(o + 1) * P], lambda c: xgT[:, c, :])
            last.then_inc(qg_in_psum, 1)
            pe.wait_ge(wvo_ready, 2)
            product(ps[:, 4, HID:2 * HID], lambda c: xgT[:, c, :], lambda c: wT[:, WV, c, :]).then_inc(vg_in_psum, 1)

            SPLIT = ((0, 0), (1, 0), (0, 1))

            def split_product(out, rows_part, w_part):
                terms = [(a, b, c) for a, b in SPLIT for c in range(KC)]
                for i, (a, b, c) in enumerate(terms):
                    last = mm(out, rows_part[a][:, c, :], w_part[b][:, c, :], start=(i == 0), stop=(i == len(terms) - 1))
                return last

            def score(bank, slot, u):
                for i, (a, b) in enumerate(SPLIT):
                    last = mm(bank, q_part[a][:, slot, u // 2, u % 2, :], k_part[b][:, slot, u // 2, :, :].rearrange("p q j -> p (q j)"),
                              start=(i == 0), stop=(i == 2))
                return last

            def sum_rows(b):
                pe.wait_ge(pool_step, 4 * (b + 1))
                for c in range(KC):
                    last = mm(batch_bank(b)[:, c * P:(c + 1) * P], xsum[:, b, c * P:(c + 1) * P], zero_w[:], start=True, stop=True)
                last.then_inc(xsumT_in_psum, 1)

            def sum_values(b):
                pe.wait_ge(xsumT_ready, b + 1)
                product(batch_bank(b)[:, HID:2 * HID], lambda c: xsumT[:, b, c, :], lambda c: wT[:, WV, c, :]).then_inc(vall_in_psum, 1)

            def window_sums(t, p):
                need(pe, residual_ready, t - 1)
                pe.wait_ge(v_ready, t + 2)
                mm(ps_rao[:, 0:NV], neg_zero_w[:], padded(va[:, 1 - p, :])[:, :, 0:VA], start=True, stop=True).then_inc(r_in_psum, 1)

            def turn_rows(n, pair):
                if isinstance(n, int) and n == 1 and pair == 0:
                    pe.wait_ge(residual_ready, NW)
                need(pe, xhT_ready, 2 * n + pair)
                pe.wait_ge(xh_ready, 4 * n + 2 * pair + 2)
                for j in range(2):
                    for k in range(KC):
                        last = nc.tensor.transpose(group_banks(n)[pair][:, (j * KC + k) * P:(j * KC + k + 1) * P],
                                                   xh[:, 2 * pair + j, k * P:(k + 1) * P], ident[:])
                last.then_inc(xhT_in_psum, 1)

            def logits(n, p):
                pe.wait_ge(xhT_ready, 2 * n + 2)
                need(pe, ohT_ready, n)
                for k in range(KC):
                    for j in range(TG):
                        last = mm(group_banks(n)[2][quad(j), 0:P], gate[:, k, :], xhT[:, p, k, j * P:(j + 1) * P],
                                  start=(k == 0), stop=(k == KC - 1), tile_position=(0, 32 * j))
                last.then_inc(zT_in_psum, 1)

            def turn_logits(n):
                pe.wait_ge(zT_ready, n + 1)
                nc.tensor.transpose(group_banks(n)[2][:, P:2 * P], zT[:], ident[:]).then_inc(z_in_psum, 1)

            def turn_onehot(n):
                pe.wait_ge(onehot_ready, n + 1)
                for j in range(TG):
                    last = nc.tensor.transpose(group_banks(n)[2][0:3 * EXPERTS, 2 * P + j * P // 2:2 * P + (j + 1) * P // 2].bitcast(bf16),
                                               onehot[:, j, :, :].rearrange("p r e -> p (r e)"), ident_b[:])
                last.then_inc(ohT_in_psum, 1)

            def step(t, p, steady=False):
                nxt, cur, prev, pp = (live(t + k, steady) for k in (1, 0, -1, -2))

                def scores(u):
                    g = 4 * t + u
                    if u == 0:
                        pe.wait_ge(q_ready, t + 1)
                        pe.wait_ge(k_ready, t + 1)
                    need(pe, shifted_ready, g - 1)
                    score(ps_score[u % 2], p, u).then_inc(scores_in_psum, 1)

                def turn(w, u):
                    g = 4 * w + u
                    need(pe, probs_ready, g - 1)
                    pe.wait_ge(cut_ready, g + 1)
                    for i in range(HPU):
                        last = nc.tensor.transpose(ps_dT[u % 2][:, i * P:(i + 1) * P], shifted[:, u, i * P:(i + 1) * P], ident[:])
                    last.then_inc(dT_in_psum, 1)

                def weigh(w, u, pw):
                    pe.wait_ge(probs_ready, 4 * w + u + 1)
                    if u == 0:
                        need(pe, num_ready, w)
                    for i, h in enumerate(heads_of(u)):
                        last = mm(ps_pv[quad(i), u * P:(u + 1) * P], va[:, pw, h * VP:(h + 1) * VP],
                                  probs[:, u, i * P:(i + 1) * P], start=True, stop=True, tile_position=(0, 32 * i))
                    last.then_inc(pv_in_psum, 1)

                if cur:
                    scores(0)
                if prev:
                    turn(t - 1, 2)
                    if not steady and t == NW:
                        turn_rows(0, 0)
                    if not steady and t == 1:
                        sum_values(1)
                        pe.wait_ge(vall_ready, B)
                    weigh(t - 1, 0, 1 - p)
                if nxt:
                    need(pe, qf_ready, t + 1)
                    pe.wait_ge(xs_ready[1 - p], 16 * ((t + 1) // 2 + 1))
                    for c in range(KC):
                        last = nc.tensor.transpose(ps_xq[:, c * P:(c + 1) * P], xs[:, 1 - p, c * P:(c + 1) * P], ident[:])
                    last.then_inc(xT_in_psum, 1)
                if cur:
                    scores(1)
                if prev:
                    turn(t - 1, 3)
                    if not steady and t == NW:
                        turn_rows(0, 1)
                    weigh(t - 1, 1, 1 - p)
                if not steady and t == NW + 1:
                    pe.wait_ge(ld_w1, 16 * KC)
                    for f in range(FC):
                        last = product(ps[:, 0, f * EPC:(f + 1) * EPC],
                                       lambda c: w1[:, c, f * EPC:(f + 1) * EPC, :].rearrange("p e h -> p (e h)"),
                                       lambda c: vecT[:, c, 2 * EXPERTS + f * EPC:2 * EXPERTS + (f + 1) * EPC])
                    last.then_inc(b1_in_psum, 1)
                if pp:
                    if cur:
                        pe.wait_ge(rest_ready, t + 1)
                    pe.wait_ge(attn_ready, t - 1)
                    for c in range(KC):
                        last = nc.tensor.transpose(ps_rao[:, c * P:(c + 1) * P], attn[:, p, c * P:(c + 1) * P], ident[:])
                    last.then_inc(aT_in_psum, 1)
                if nxt:
                    pe.wait_ge(xT_ready, t + 2)
                    need(pe, v_ready, t + 1)
                    for o in range(KC):
                        last = product(ps_kv[:, o * P:(o + 1) * P], lambda c: wT[:, WK, c, o * P:(o + 1) * P],
                                       lambda c: xT[:, 1 - p, c, :])
                    last.then_inc(k_in_psum, 1)
                    pe.wait_ge(x_high_ready, t + 2)
                    for o in range(KC):
                        last = product(ps_xq[:, HID + o * P:HID + (o + 1) * P], lambda c: wT[:, WQ, c, o * P:(o + 1) * P],
                                       lambda c: xT[:, 1 - p, c, :])
                    last.then_inc(q_in_psum, 1)
                if cur:
                    scores(2)
                if nxt:
                    pe.wait_ge(kf_ready, t + 2)
                    pe.wait_ge(x_low_ready, t + 2)
                    split_product(ps_kv[:, HID:2 * HID], x_part, wv_part).then_inc(v_in_psum, 1)
                if cur:
                    if not steady and t == 0:
                        pe.wait_ge(vall_ready, 1)
                    turn(t, 0)
                if prev:
                    weigh(t - 1, 2, 1 - p)
                    weigh(t - 1, 3, 1 - p)
                if not steady and t == NW:
                    logits(0, 0)
                if pp:
                    pe.wait_ge(a_low_ready, t - 1)
                    split_product(ps_rao[:, 0:HID], a_part, wo_part).then_inc(o_in_psum, 1)
                if not steady and t == NW + 1:
                    turn_onehot(0)
                if cur:
                    scores(3)
                    turn(t, 1)
                if prev:
                    pe.wait_ge(pvT_ready, t)
                    for i in range(UNITS):
                        last = nc.tensor.transpose(ps_pv[:, i * P:(i + 1) * P], pvT[:, i * P:(i + 1) * P], ident[:])
                    last.then_inc(sums_in_psum, 1)
                if not steady and t == NW:
                    turn_logits(0)
                if nxt and (steady or t >= 0):
                    window_sums(t, p)
                if not steady and t == 0:
                    pe.wait_ge(out_bias_ready, 1)
                    sum_rows(1)

            pe.wait_ge(qg_ready, 1)
            pe.wait_ge(kg_ready, 1)
            for u in range(UNITS):
                score(ps[:, u, :], 1, u).then_inc(gs_in_psum, 1)
            pe.wait_ge(vg_ready, 1)
            pe.wait_ge(wvo_low_ready, 2)
            step(-1, 1)
            for u in range(UNITS):
                pe.wait_ge(gs_shifted, u + 1)
                for i in range(HPU):
                    last = nc.tensor.transpose(ps[:, u, i * P:(i + 1) * P], dg[:, u, i * P:(i + 1) * P], ident[:])
                last.then_inc(gT_in_psum, 1)
            for u in range(UNITS):
                pe.wait_ge(g_probs, u + 1)
                for i, h in enumerate(heads_of(u)):
                    last = mm(ps_pv[quad(i), u * P:(u + 1) * P], vg[:, h * VP:(h + 1) * VP], pg[:, u, i * P:(i + 1) * P],
                              start=True, stop=True, tile_position=(0, 32 * i))
            last.then_inc(g_pv, 1)
            window_sums(-1, 1)
            sum_rows(0)
            pe.wait_ge(g_pvT_ready, 1)
            for i in range(UNITS):
                last = nc.tensor.transpose(ps_pv[:, i * P:(i + 1) * P], pvT[:, i * P:(i + 1) * P], ident[:])
            last.then_inc(g_sums_in_psum, 1)
            sum_values(0)
            pe.wait_ge(consts_ready, 1)
            pe.wait_ge(g_sums_ready, 1)
            product(ps_pv[:, 0:HID], lambda c: bv_wide[:, c, :], lambda c: wT[:, WO, c, :]).then_inc(bias_in_psum, 1)
            attention_steps(pe, step, first=0)

            def step(n, p, steady=False):
                nxt, cur, prev = (live_group(n + k, steady) for k in (1, 0, -1))
                for c in range(FC):
                    if cur:
                        if c == 0:
                            if not steady and n == 0:
                                pe.wait_ge(ffn_w_ready, 1)
                            pe.wait_ge(high_ready, 2 * n + 2)
                            pe.wait_ge(low_ready, 2 * n + 2)
                        need(pe, h_ready, 4 * n + c - 1)
                        terms = [(k, a, b) for k in range(KC) for a, b in SPLIT]
                        for i, (k, a, b) in enumerate(terms):
                            last = mm(ps[:, c % 2, :], w1_part[a][:, k, c * P:(c + 1) * P],
                                      xh_part[b][:, p, k, :], start=(i == 0), stop=(i == len(terms) - 1))
                        last.then_inc(h_in_psum, 1)
                        if c == 0:
                            pe.wait_ge(ohT_ready, n + 1)
                        need(pe, hm_ready, 4 * n + c - 1)
                        mm(ps[:, 2 + c % 2, :], pick[:, c, :], ohT[:, p, :], start=True, stop=True).then_inc(mask_in_psum, 1)
                    if nxt and c < 2:
                        turn_rows(n + 1, c)
                    if nxt and c == 3:
                        turn_onehot(n + 1)
                    if nxt and c == 2:
                        logits(n + 1, 1 - p)
                        if not prev:
                            turn_logits(n + 1)
                    if prev:
                        w = TG * (n - 1) + c
                        if not steady and n == 1 and c == 0:
                            pe.wait_ge(w2_low_ready, 1)
                        need(pe, ysum_ready, w - 1)
                        y = ps[:, 4 + c % 2, 0:HID]
                        for f in range(FC):
                            if c == 0:
                                pe.wait_ge(hm_low_ready[f // 2], 2 * (n - 1) + f % 2 + 1)
                            for i, (a, b) in enumerate(SPLIT):
                                mm(y, hm_part[a][:, 1 - p, f, c * P:(c + 1) * P], w2_part[b][:, f, :],
                                   start=(f == 0 and i == 0), stop=False)
                        mm(y, ohT[:, 1 - p, c * P:(c + 1) * P], b2_stack[:], start=False, stop=True).then_inc(y_in_psum, 1)
                        if nxt and c == 2:
                            turn_logits(n + 1)

            expert_steps(pe, step)


_INS = ['L0_attn_x', 'L0_attn_wq', 'L0_attn_bq', 'L0_attn_wk', 'L0_attn_bk', 'L0_attn_wv', 'L0_attn_bv',
        'L0_attn_wo', 'L0_attn_bo', 'L0_ffn_Wg', 'L0_ffn_ln_scale', 'L0_ffn_ln_bias', 'L0_ffn_W1', 'L0_ffn_b1',
        'L0_ffn_W2', 'L0_ffn_b2']
_OUTS = [((2, 2048, 256), 'float32')]


def kernel(**inputs):
    import numpy as _np
    import concourse.bacc as _bacc
    from concourse import mybir as _mybir
    from concourse.bass_utils import run_bass_kernel_spmd as _run

    nc = _bacc.Bacc("TRN2", target_bir_lowering=False, num_devices=1)
    arrays, args = {}, []
    for name in _INS:
        a = _np.ascontiguousarray(inputs[name])
        arrays[f"in_{name}_dram"] = a
        args.append(nc.dram_tensor(f"in_{name}_dram", a.shape, _mybir.dt.from_np(a.dtype), kind="ExternalInput").ap())
    for i, (shape, dtype) in enumerate(_OUTS):
        dt = _mybir.dt.from_np(_np.dtype(dtype))
        args.append(nc.dram_tensor(f"out_{i}_dram", shape, dt, kind="ExternalOutput").ap())
    windowed_attention_then_top1_experts(nc, *args)
    r = _run(nc, [arrays], core_ids=[0])
    got = tuple(r.results[0][f"out_{i}_dram"] for i in range(len(_OUTS)))
    return got[0]
```
